# Optimizing a Trainium2 kernel written in Bass

```python
import numpy as np
import jax
import jax.numpy as jnp

def _softmax(x, axis=-1):
    return jax.nn.softmax(x, axis=axis)

def _gelu(x):
    return jax.nn.gelu(x, approximate=True)

def _silu(x):
    return jax.nn.silu(x)

def _sigmoid(x):
    return jax.nn.sigmoid(x)

def _layernorm(x, axis=-1, eps=1e-05):
    m = jnp.mean(x, axis=axis, keepdims=True)
    v = jnp.var(x, axis=axis, keepdims=True)
    return (x - m) / jnp.sqrt(v + eps)

def _scatter_add(tgt, idx, src, axis=0):
    return tgt.at[idx].add(src)

def _segment_sum(src, seg, n):
    return jax.ops.segment_sum(src, seg, n)
kernel_name = 'mk_seq_postln_d2_jaxref_r8_1ffb12'

def setup_inputs(seed: int=0):
    np.random.seed(seed)
    _w = jnp.asarray

    def _L0_attn_setup():
        import jax, jax.numpy as jnp
        import numpy as np
        NHEAD = 16
        EPS = 1e-05

        def layer_norm(x, w, b):
            mu = jnp.mean(x, axis=-1, keepdims=True)
            var = jnp.var(x, axis=-1, keepdims=True)
            return (x - mu) * jax.lax.rsqrt(var + EPS) * w + b
        key = jax.random.key(seed)
        ks = jax.random.split(key, 14)
        B, S, E, F = (16, 128, 128, 512)
        s = 0.02
        return {'x': jax.random.normal(ks[0], (B, S, E), jnp.float32), 'in_proj_w': jax.random.normal(ks[1], (3 * E, E), jnp.float32) * s, 'in_proj_b': jax.random.normal(ks[2], (3 * E,), jnp.float32) * s, 'out_w': jax.random.normal(ks[3], (E, E), jnp.float32) * s, 'out_b': jax.random.normal(ks[4], (E,), jnp.float32) * s, 'lin1_w': jax.random.normal(ks[5], (F, E), jnp.float32) * s, 'lin1_b': jax.random.normal(ks[6], (F,), jnp.float32) * s, 'lin2_w': jax.random.normal(ks[7], (E, F), jnp.float32) * s, 'lin2_b': jax.random.normal(ks[8], (E,), jnp.float32) * s, 'norm1_w': jnp.ones((E,), jnp.float32), 'norm1_b': jnp.zeros((E,), jnp.float32), 'norm2_w': jnp.ones((E,), jnp.float32), 'norm2_b': jnp.zeros((E,), jnp.float32)}
    _L0_attn_in = _L0_attn_setup()

    def _L0_ffn_setup():
        import jax, jax.numpy as jnp
        import numpy as np
        B, S, D, H, L, E, K = (4, 128, 128, 16, 2, 8, 2)
        DFF = 4 * D

        def _ln(x, w, b):
            m = x.mean(-1, keepdims=True)
            v = x.var(-1, keepdims=True)
            return (x - m) / jnp.sqrt(v + 1e-05) * w + b

        def _attn(x, wq, wk, wv, wo, bq, bk, bv, bo):
            Bb, T, C = x.shape
            hd = C // H
            q = (x @ wq + bq).reshape(Bb, T, H, hd).transpose(0, 2, 1, 3)
            k = (x @ wk + bk).reshape(Bb, T, H, hd).transpose(0, 2, 1, 3)
            v = (x @ wv + bv).reshape(Bb, T, H, hd).transpose(0, 2, 1, 3)
            att = jnp.einsum('bhqd,bhkd->bhqk', q, k) * hd ** (-0.5)
            causal = jnp.tril(jnp.ones((T, T), bool))
            att = jnp.where(causal, att, -jnp.inf)
            att = jax.nn.softmax(att, axis=-1)
            y = jnp.einsum('bhqk,bhkd->bhqd', att, v).transpose(0, 2, 1, 3).reshape(Bb, T, C)
            return y @ wo + bo

        def _ffn(h, w1, b1, w2, b2):
            return jax.nn.gelu(h @ w1 + b1, approximate=False) @ w2 + b2

        def _combine_weights(logits):
            vals, idx = jax.lax.top_k(logits, K)
            w = jax.nn.softmax(vals, axis=-1)
            onehot = (idx[..., None] == jnp.arange(E)).astype(w.dtype)
            return jnp.sum(w[..., None] * onehot, axis=-2)

        def _token_moe(h, gw, gb, w1, b1, w2, b2):
            cw = _combine_weights(h @ gw + gb)
            out = jnp.zeros_like(h)
            for e in range(E):
                out = out + _ffn(h, w1[e], b1[e], w2[e], b2[e]) * cw[..., e:e + 1]
            return out

        def _seq_moe(h, gw, gb, w1, b1, w2, b2):
            cw = _combine_weights(h.mean(axis=1) @ gw + gb)
            out = jnp.zeros_like(h)
            for e in range(E):
                out = out + _ffn(h, w1[e], b1[e], w2[e], b2[e]) * cw[:, e, None, None]
            return out
        key = jax.random.key(seed)
        ks = jax.random.split(key, 9)
        n = lambda k, shp: jax.random.normal(k, shp, dtype=jnp.float32) * 0.02
        return {'x': jax.random.normal(ks[0], (B, S, D), dtype=jnp.float32), 'ln1_w': jnp.ones((L, D), jnp.float32), 'ln1_b': jnp.zeros((L, D), jnp.float32), 'ln2_w': jnp.ones((L, D), jnp.float32), 'ln2_b': jnp.zeros((L, D), jnp.float32), 'wq': n(ks[1], (L, D, D)), 'wk': n(ks[2], (L, D, D)), 'wv': n(ks[3], (L, D, D)), 'wo': n(ks[4], (L, D, D)), 'bq': jnp.zeros((L, D), jnp.float32), 'bk': jnp.zeros((L, D), jnp.float32), 'bv': jnp.zeros((L, D), jnp.float32), 'bo': jnp.zeros((L, D), jnp.float32), 'gate_w': n(ks[5], (L, D, E)), 'gate_b': jnp.zeros((L, E), jnp.float32), 'e_w1': n(ks[6], (L, E, D, DFF)), 'e_b1': jnp.zeros((L, E, DFF), jnp.float32), 'e_w2': n(ks[7], (L, E, DFF, D)), 'e_b2': jnp.zeros((L, E, D), jnp.float32)}
    _L0_ffn_in = _L0_ffn_setup()

    def _L1_attn_setup():
        import jax, jax.numpy as jnp
        import numpy as np
        NUM_HEADS = 16
        N_EMBD = 128

        def alibi_bias(num_heads: int, seq_len: int) -> jnp.ndarray:
            pos = jnp.arange(seq_len, dtype=jnp.float32)
            dgrid = pos[None, :] - pos[:, None]
            slopes = 2.0 ** (-8.0 / num_heads * (jnp.arange(num_heads, dtype=jnp.float32) + 1.0))
            bias = slopes[:, None, None] * dgrid[None, :, :]
            return jnp.where(dgrid[None, :, :] > 0, -jnp.inf, bias)
        key = jax.random.key(seed)
        k1, k2, k3 = jax.random.split(key, 3)
        B, L, E = (2, 256, N_EMBD)
        x = jax.random.normal(k1, (B, L, E), dtype=jnp.float32)
        w_in = jax.random.normal(k2, (3 * E, E), dtype=jnp.float32) * 0.02
        w_out = jax.random.normal(k3, (E, E), dtype=jnp.float32) * 0.02
        return {'x': x, 'w_in': w_in, 'w_out': w_out}
    _L1_attn_in = _L1_attn_setup()

    def _L1_ffn_setup():
        import jax, jax.numpy as jnp
        import numpy as np
        D_MODEL = 128
        D_FF = 512
        N_EXPERTS = 8
        D_EXPERT = D_FF // N_EXPERTS
        TOP_K = 2
        LB_WEIGHT = 0.01
        B, S = (4, 256)

        def _top_k_softmax(logits, k):
            vals, _ = jax.lax.top_k(logits, k)
            thresh = vals[..., -1:]
            masked = jnp.where(logits >= thresh, logits, -jnp.inf)
            return jax.nn.softmax(masked, axis=-1)
        key = jax.random.key(seed)
        ks = jax.random.split(key, 8)
        x = jax.random.normal(ks[0], (B, S, D_MODEL), dtype=jnp.float32)
        w1 = jax.random.normal(ks[1], (N_EXPERTS, D_MODEL, D_EXPERT), dtype=jnp.float32) * (1.0 / np.sqrt(D_MODEL))
        b1 = jnp.zeros((N_EXPERTS, D_EXPERT), dtype=jnp.float32)
        w2 = jax.random.normal(ks[2], (N_EXPERTS, D_EXPERT, D_MODEL), dtype=jnp.float32) * (1.0 / np.sqrt(D_EXPERT))
        b2 = jnp.zeros((N_EXPERTS, D_MODEL), dtype=jnp.float32)
        centroids = jax.random.normal(ks[3], (N_EXPERTS, D_MODEL), dtype=jnp.float32) * 0.02
        w_route = jax.random.normal(ks[4], (N_EXPERTS, D_MODEL), dtype=jnp.float32) * (1.0 / np.sqrt(D_MODEL))
        return {'x': x, 'w1': w1, 'b1': b1, 'w2': w2, 'b2': b2, 'centroids': centroids, 'w_route': w_route}
    _L1_ffn_in = _L1_ffn_setup()
    _d = {'L0_attn_x': _L0_attn_in['x'], 'L0_attn_in_proj_w': _L0_attn_in['in_proj_w'], 'L0_attn_in_proj_b': _L0_attn_in['in_proj_b'], 'L0_attn_out_w': _L0_attn_in['out_w'], 'L0_attn_out_b': _L0_attn_in['out_b'], 'L0_attn_lin1_w': _L0_attn_in['lin1_w'], 'L0_attn_lin1_b': _L0_attn_in['lin1_b'], 'L0_attn_lin2_w': _L0_attn_in['lin2_w'], 'L0_attn_lin2_b': _L0_attn_in['lin2_b'], 'L0_attn_norm1_w': _L0_attn_in['norm1_w'], 'L0_attn_norm1_b': _L0_attn_in['norm1_b'], 'L0_attn_norm2_w': _L0_attn_in['norm2_w'], 'L0_attn_norm2_b': _L0_attn_in['norm2_b'], 'L0_ffn_ln1_w': _L0_ffn_in['ln1_w'], 'L0_ffn_ln1_b': _L0_ffn_in['ln1_b'], 'L0_ffn_ln2_w': _L0_ffn_in['ln2_w'], 'L0_ffn_ln2_b': _L0_ffn_in['ln2_b'], 'L0_ffn_wq': _L0_ffn_in['wq'], 'L0_ffn_wk': _L0_ffn_in['wk'], 'L0_ffn_wv': _L0_ffn_in['wv'], 'L0_ffn_wo': _L0_ffn_in['wo'], 'L0_ffn_bq': _L0_ffn_in['bq'], 'L0_ffn_bk': _L0_ffn_in['bk'], 'L0_ffn_bv': _L0_ffn_in['bv'], 'L0_ffn_bo': _L0_ffn_in['bo'], 'L0_ffn_gate_w': _L0_ffn_in['gate_w'], 'L0_ffn_gate_b': _L0_ffn_in['gate_b'], 'L0_ffn_e_w1': _L0_ffn_in['e_w1'], 'L0_ffn_e_b1': _L0_ffn_in['e_b1'], 'L0_ffn_e_w2': _L0_ffn_in['e_w2'], 'L0_ffn_e_b2': _L0_ffn_in['e_b2'], 'L1_attn_w_in': _L1_attn_in['w_in'], 'L1_attn_w_out': _L1_attn_in['w_out'], 'L1_ffn_w1': _L1_ffn_in['w1'], 'L1_ffn_b1': _L1_ffn_in['b1'], 'L1_ffn_w2': _L1_ffn_in['w2'], 'L1_ffn_b2': _L1_ffn_in['b2'], 'L1_ffn_centroids': _L1_ffn_in['centroids'], 'L1_ffn_w_route': _L1_ffn_in['w_route']}
    _x0 = _d['L0_attn_x']
    _d['L0_attn_x'] = jax.random.normal(jax.random.fold_in(jax.random.key(seed), 1), (2, 1024, 128), dtype=_x0.dtype)
    del _x0
    return _d

def reference(L0_attn_x, L0_attn_in_proj_w, L0_attn_in_proj_b, L0_attn_out_w, L0_attn_out_b, L0_attn_lin1_w, L0_attn_lin1_b, L0_attn_lin2_w, L0_attn_lin2_b, L0_attn_norm1_w, L0_attn_norm1_b, L0_attn_norm2_w, L0_attn_norm2_b, L0_ffn_ln1_w, L0_ffn_ln1_b, L0_ffn_ln2_w, L0_ffn_ln2_b, L0_ffn_wq, L0_ffn_wk, L0_ffn_wv, L0_ffn_wo, L0_ffn_bq, L0_ffn_bk, L0_ffn_bv, L0_ffn_bo, L0_ffn_gate_w, L0_ffn_gate_b, L0_ffn_e_w1, L0_ffn_e_b1, L0_ffn_e_w2, L0_ffn_e_b2, L1_attn_w_in, L1_attn_w_out, L1_ffn_w1, L1_ffn_b1, L1_ffn_w2, L1_ffn_b2, L1_ffn_centroids, L1_ffn_w_route):

    def _L0_attn_ref(x, in_proj_w, in_proj_b, out_w, out_b, lin1_w, lin1_b, lin2_w, lin2_b, norm1_w, norm1_b, norm2_w, norm2_b):
        import jax, jax.numpy as jnp
        import numpy as np
        NHEAD = 16
        EPS = 1e-05

        def layer_norm(x, w, b):
            mu = jnp.mean(x, axis=-1, keepdims=True)
            var = jnp.var(x, axis=-1, keepdims=True)
            return (x - mu) * jax.lax.rsqrt(var + EPS) * w + b
        B, S, E = x.shape
        H = NHEAD
        D = E // H
        xn = layer_norm(x, norm1_w, norm1_b)
        qkv = xn @ in_proj_w.T + in_proj_b
        q, k, v = jnp.split(qkv, 3, axis=-1)
        q = q.reshape(B, S, H, D)
        k = k.reshape(B, S, H, D)
        v = v.reshape(B, S, H, D)
        scale = 1.0 / jnp.sqrt(jnp.asarray(D, x.dtype))
        scores = jnp.einsum('bqhd,bkhd->bhqk', q, k) * scale
        attn = jax.nn.softmax(scores, axis=-1)
        ctx = jnp.einsum('bhqk,bkhd->bqhd', attn, v).reshape(B, S, E)
        attn_out = ctx @ out_w.T + out_b
        x = x + attn_out
        xn2 = layer_norm(x, norm2_w, norm2_b)
        h = jax.nn.gelu(xn2 @ lin1_w.T + lin1_b, approximate=False)
        x = x + (h @ lin2_w.T + lin2_b)
        return x

    def _L0_ffn_ref(x, ln1_w, ln1_b, ln2_w, ln2_b, wq, wk, wv, wo, bq, bk, bv, bo, gate_w, gate_b, e_w1, e_b1, e_w2, e_b2):
        import jax, jax.numpy as jnp
        import numpy as np
        B, S, D, H, L, E, K = (4, 128, 128, 16, 2, 8, 2)
        DFF = 4 * D

        def _ln(x, w, b):
            m = x.mean(-1, keepdims=True)
            v = x.var(-1, keepdims=True)
            return (x - m) / jnp.sqrt(v + 1e-05) * w + b

        def _attn(x, wq, wk, wv, wo, bq, bk, bv, bo):
            Bb, T, C = x.shape
            hd = C // H
            q = (x @ wq + bq).reshape(Bb, T, H, hd).transpose(0, 2, 1, 3)
            k = (x @ wk + bk).reshape(Bb, T, H, hd).transpose(0, 2, 1, 3)
            v = (x @ wv + bv).reshape(Bb, T, H, hd).transpose(0, 2, 1, 3)
            att = jnp.einsum('bhqd,bhkd->bhqk', q, k) * hd ** (-0.5)
            causal = jnp.tril(jnp.ones((T, T), bool))
            att = jnp.where(causal, att, -jnp.inf)
            att = jax.nn.softmax(att, axis=-1)
            y = jnp.einsum('bhqk,bhkd->bhqd', att, v).transpose(0, 2, 1, 3).reshape(Bb, T, C)
            return y @ wo + bo

        def _ffn(h, w1, b1, w2, b2):
            return jax.nn.gelu(h @ w1 + b1, approximate=False) @ w2 + b2

        def _combine_weights(logits):
            vals, idx = jax.lax.top_k(logits, K)
            w = jax.nn.softmax(vals, axis=-1)
            onehot = (idx[..., None] == jnp.arange(E)).astype(w.dtype)
            return jnp.sum(w[..., None] * onehot, axis=-2)

        def _token_moe(h, gw, gb, w1, b1, w2, b2):
            cw = _combine_weights(h @ gw + gb)
            out = jnp.zeros_like(h)
            for e in range(E):
                out = out + _ffn(h, w1[e], b1[e], w2[e], b2[e]) * cw[..., e:e + 1]
            return out

        def _seq_moe(h, gw, gb, w1, b1, w2, b2):
            cw = _combine_weights(h.mean(axis=1) @ gw + gb)
            out = jnp.zeros_like(h)
            for e in range(E):
                out = out + _ffn(h, w1[e], b1[e], w2[e], b2[e]) * cw[:, e, None, None]
            return out
        for l in range(L):
            x = x + _attn(_ln(x, ln1_w[l], ln1_b[l]), wq[l], wk[l], wv[l], wo[l], bq[l], bk[l], bv[l], bo[l])
            h = _ln(x, ln2_w[l], ln2_b[l])
            moe = _token_moe if l % 2 == 0 else _seq_moe
            x = x + moe(h, gate_w[l], gate_b[l], e_w1[l], e_b1[l], e_w2[l], e_b2[l])
        return x

    def _L1_attn_ref(x, w_in, w_out):
        import jax, jax.numpy as jnp
        import numpy as np
        NUM_HEADS = 16
        N_EMBD = 128

        def alibi_bias(num_heads: int, seq_len: int) -> jnp.ndarray:
            pos = jnp.arange(seq_len, dtype=jnp.float32)
            dgrid = pos[None, :] - pos[:, None]
            slopes = 2.0 ** (-8.0 / num_heads * (jnp.arange(num_heads, dtype=jnp.float32) + 1.0))
            bias = slopes[:, None, None] * dgrid[None, :, :]
            return jnp.where(dgrid[None, :, :] > 0, -jnp.inf, bias)
        B, L, E = x.shape
        H = NUM_HEADS
        D = E // H
        qkv = jnp.einsum('ble,fe->blf', x, w_in)
        q, k, v = jnp.split(qkv, 3, axis=-1)

        def to_heads(t):
            return t.reshape(B, L, H, D).transpose(0, 2, 1, 3)
        q, k, v = (to_heads(q), to_heads(k), to_heads(v))
        scale = 1.0 / jnp.sqrt(jnp.asarray(D, dtype=x.dtype))
        scores = jnp.einsum('bhqd,bhkd->bhqk', q, k) * scale
        scores = scores + alibi_bias(H, L)[None]
        attn = jax.nn.softmax(scores, axis=-1)
        ctx = jnp.einsum('bhqk,bhkd->bhqd', attn, v)
        ctx = ctx.transpose(0, 2, 1, 3).reshape(B, L, E)
        return jnp.einsum('ble,fe->blf', ctx, w_out)

    def _L1_ffn_ref(x, w1, b1, w2, b2, centroids, w_route):
        import jax, jax.numpy as jnp
        import numpy as np
        D_MODEL = 128
        D_FF = 512
        N_EXPERTS = 8
        D_EXPERT = D_FF // N_EXPERTS
        TOP_K = 2
        LB_WEIGHT = 0.01
        B, S = (4, 256)

        def _top_k_softmax(logits, k):
            vals, _ = jax.lax.top_k(logits, k)
            thresh = vals[..., -1:]
            masked = jnp.where(logits >= thresh, logits, -jnp.inf)
            return jax.nn.softmax(masked, axis=-1)
        eps = 1e-12
        x_norm = x / jnp.maximum(jnp.linalg.norm(x, axis=-1, keepdims=True), eps)
        c_norm = centroids / jnp.maximum(jnp.linalg.norm(centroids, axis=-1, keepdims=True), eps)
        cos_scores = jnp.einsum('bsd,ed->bse', x_norm, c_norm)
        route_scores = jnp.einsum('bsd,ed->bse', x, w_route)
        logits = cos_scores + route_scores
        gates = _top_k_softmax(logits, TOP_K)
        h = jax.nn.gelu(jnp.einsum('bsd,edh->bseh', x, w1) + b1, approximate=False)
        expert_out = jnp.einsum('bseh,ehd->bsed', h, w2) + b2
        out = jnp.einsum('bse,bsed->bsd', gates, expert_out)
        return out
    x = L0_attn_x
    x = _layernorm(x + _L0_attn_ref(x, L0_attn_in_proj_w, L0_attn_in_proj_b, L0_attn_out_w, L0_attn_out_b, L0_attn_lin1_w, L0_attn_lin1_b, L0_attn_lin2_w, L0_attn_lin2_b, L0_attn_norm1_w, L0_attn_norm1_b, L0_attn_norm2_w, L0_attn_norm2_b), axis=-1)
    x = _layernorm(x + _L0_ffn_ref(x, L0_ffn_ln1_w, L0_ffn_ln1_b, L0_ffn_ln2_w, L0_ffn_ln2_b, L0_ffn_wq, L0_ffn_wk, L0_ffn_wv, L0_ffn_wo, L0_ffn_bq, L0_ffn_bk, L0_ffn_bv, L0_ffn_bo, L0_ffn_gate_w, L0_ffn_gate_b, L0_ffn_e_w1, L0_ffn_e_b1, L0_ffn_e_w2, L0_ffn_e_b2), axis=-1)
    x = _layernorm(x + _L1_attn_ref(x, L1_attn_w_in, L1_attn_w_out), axis=-1)
    x = _layernorm(x + _L1_ffn_ref(x, L1_ffn_w1, L1_ffn_b1, L1_ffn_w2, L1_ffn_b2, L1_ffn_centroids, L1_ffn_w_route), axis=-1)
    return x

_drawn_inputs = setup_inputs


def setup_inputs(seed=0):
    import zlib

    import numpy as np

    out = dict(_drawn_inputs(seed))
    spreads = {'L0_attn_norm1_w': (1.0, 0.6),
     'L0_attn_norm1_b': (0.0, 0.464),
     'L0_attn_norm2_w': (1.0, 0.6),
     'L0_attn_norm2_b': (0.0, 0.455),
     'L0_ffn_ln1_w': (1.0, 0.6),
     'L0_ffn_ln1_b': (0.0, 0.356),
     'L0_ffn_ln2_w': (1.0, 0.2),
     'L0_ffn_ln2_b': (0.0, 0.298),
     'L0_ffn_bq': (0.0, 0.8),
     'L0_ffn_bk': (0.0, 2.0),
     'L0_ffn_bv': (0.0, 0.1),
     'L0_ffn_bo': (0.0, 0.1),
     'L0_ffn_gate_b': (0.0, 0.1),
     'L0_ffn_e_b1': (0.0, 0.1),
     'L0_ffn_e_b2': (0.0, 0.1),
     'L1_ffn_b1': (0.0, 0.1),
     'L1_ffn_b2': (0.0, 0.1)}
    factors = {'L0_attn_in_proj_w': 4.34,
     'L0_attn_in_proj_b': 3.182,
     'L0_attn_out_w': 3.009,
     'L0_attn_lin1_b': 3.97,
     'L0_ffn_wq': 8.0,
     'L0_ffn_wk': 6.676,
     'L0_ffn_wv': 2.868}
    for name, (base, spread) in spreads.items():
        noise = np.random.default_rng([zlib.crc32(name.encode()), seed]).standard_normal(out[name].shape)
        drawn = base * np.exp(spread * noise) if base else spread * noise
        out[name] = jnp.asarray(drawn.astype(out[name].dtype))
    for name, factor in factors.items():
        out[name] = (out[name] * factor).astype(out[name].dtype)
    return out
```

```python
from contextlib import ExitStack

import concourse.bass as bass
from concourse import mybir

F32 = mybir.dt.float32
BF16 = mybir.dt.bfloat16
U32 = mybir.dt.uint32
ALU = mybir.AluOpType
ACT = mybir.ActivationFunctionType
AX_X = mybir.AxisListType.X

P = 128
NB, S, D = 2, 1024, 128
H, HD = 16, 8
TOK = NB * S
T = TOK // P
BANK = 512
TB = BANK // P
NCH = TOK // BANK
QT = S // P
G = 4
NG = NB * H // G
GW = G * HD
HG = H // G
E = 8
F = 512
FC = F // P
WCOLS = F + FC + FC * D
EPS = 1e-5
BIG = 3.0e38

Q_PART = [0, 0, 0, 1, 1, 1, 2, 2]
K_PART = [0, 1, 2, 0, 1, 2, 0, 1]
TERMS = len(Q_PART)
ROW_BIAS = TERMS * HD
ROW_MAX = P - 3
STACK_LD = NB * H * S


class Memory:
    pass


def allocate(nc, ctx):
    m = Memory()

    def sb(name, shape, dt=F32):
        return ctx.enter_context(nc.sbuf_tensor(name, shape, dt))

    m.psum = ctx.enter_context(nc.psum_tensor("psum", [P, 8, BANK], F32))
    m.x = sb("x_outer", [P, T, D])
    m.y = sb("y_inner", [P, T, D])
    m.nrm = sb("normalized", [P, T, D])
    m.stats = sb("stats", [P, T, 6])
    m.meanvar = sb("meanvar", [P, T, 2])
    m.std = sb("std", [P, T])
    m.rstd = sb("rstd", [P, T])
    m.xT = sb("xT", [P, TOK])
    m.ident = sb("ident", [P, P])
    m.identb = sb("identb", [P, P], BF16)
    m.mask = sb("mask", [P, 2, P])
    m.maskb = sb("maskb", [P, 2, P], BF16)
    m.iota8 = sb("iota8", [P, E])
    m.lncol = sb("lncol", [P, 6, 2])
    m.aw = sb("attn_w", [P, 4, D])
    m.abcol = sb("attn_bias_cols", [P, 4, 2])
    m.abrow = sb("attn_bias_rows", [P, 4, 2, D])
    m.qbias = sb("scaled_q_bias", [P, 4])
    m.part = sb("qk_parts", [P, 2, 3, TOK], BF16)
    m.full = sb("qk_full", [P, 2, 2, BANK])
    m.rest = sb("qk_rest", [P, 2, 2, BANK])
    m.v = sb("v_all", [P, NG, QT, GW])
    m.vst = sb("v_stage", [P, QT, G, 32])
    m.qs = sb("q_slots", [P, 3, G, S], BF16)
    m.ks = sb("k_slots", [P, 3, G, S], BF16)
    m.prob = sb("prob", [P, 4, 2, BANK])
    m.outT = sb("outT", [P, 2, BANK])
    m.rsum = sb("row_sum_inverse", [P, 2, TB, G])
    m.ctx = sb("ctx_all", [P, T, D])
    m.mx = sb("chunk_max", [P, G, QT, 2])
    m.negm = sb("neg_max", [P, G * QT])
    m.negr = sb("neg_max_rest", [P, G * QT])
    m.negp = sb("neg_max_parts", [P, 3, G * QT], BF16)
    m.maxT = sb("neg_max_turned", [3 * G * QT, P], BF16)
    m.wring = sb("expert_w", [P, 2, WCOLS])
    m.h = m.prob[:].rearrange("p s c n -> p (s c) n").rearrange("p (u k) n -> p u k n", u=2)
    m.gate_w = sb("gate_w", [P, 2, E])
    m.gate_b = sb("gate_b", [P, 2, E])
    m.b2 = sb("b2", [E, 3, D])
    m.b2ffn = sb("b2_ffn", [P, D])
    m.lg = sb("logits", [P, T, E])
    m.top = sb("top8", [P, T, 8])
    m.idx = sb("top8_index", [P, T, 8], U32)
    m.idxf = sb("top8_index_f", [P, T, 8])
    m.pick = sb("pick", [P, T, E])
    m.gate = sb("gates", [P, T, E])
    m.sel = sb("selected_weights", [P, T, 2])
    m.tmp = sb("gate_tmp", [P, T, 4])
    m.gT = sb("gatesT", [E, T, P])
    m.msum = sb("token_mean", [P, NB])
    m.mrep = sb("token_mean_rep", [P, NB, P])
    m.tail_w = sb("tail_w", [P, WCOLS])
    m.cent = sb("centroids", [E, D])
    m.cscr = sb("centroid_scratch", [E, D])
    m.cn = sb("centroid_norm", [E, 4])
    m.route = sb("route_w", [P, 2 * E])
    m.expand = sb("expand", [E, F])
    return m


STAGE_SEMAPHORES = 16


def stage_semaphores(nc, ctx, tag):
    if nc.free_len() < STAGE_SEMAPHORES:
        nc.clear_and_free_semaphores(RETIRED)
        RETIRED.clear()
        nc.all_engine_barrier()
    made = []

    def sem(name):
        made.append(nc.alloc_semaphore(f"{tag}_{name}"))
        return made[-1]

    ctx.callback(lambda: RETIRED.extend(made))
    return sem


RETIRED = []


def broadcast_rows(row, n=P):
    return row.partition_broadcast(n)


def load_stage(nc, m, ins):
    with ExitStack() as ctx:
        sem = stage_semaphores(nc, ctx, "shared")
        loaded, made, built = sem("loaded"), sem("made"), sem("built")
        block = ctx.enter_context(nc.Block())

        @block.sync
        def _(sp):
            sp.dma_start(m.x[:], ins["x"].rearrange("(t p) f -> p t f", p=P)).then_inc(loaded, 16)
            sp.dma_start(m.ident[:], ins["ident"]).then_inc(loaded, 16)
            sp.dma_start(m.mask[:], ins["mask"]).then_inc(loaded, 16)
            sp.dma_start(m.lncol[:], ins["lncol"]).then_inc(loaded, 16)
            sp.dma_start(m.abcol[:], ins["abcol"]).then_inc(loaded, 16)
            sp.dma_start(m.abrow[:], broadcast_rows(ins["abrow"])).then_inc(loaded, 16)
            sp.dma_start(m.gate_w[:], ins["gate_w"]).then_inc(loaded, 16)
            sp.dma_start(m.gate_b[:], broadcast_rows(ins["gate_b"])).then_inc(loaded, 16)
            sp.dma_start(m.iota8[:], broadcast_rows(ins["iota8"])).then_inc(loaded, 16)
            sp.dma_start(m.b2[:], ins["b2"]).then_inc(loaded, 16)
            sp.dma_start(m.b2ffn[:], broadcast_rows(ins["b2ffn"])).then_inc(loaded, 16)
            sp.dma_start(m.tail_w[:], ins["tail_w"]).then_inc(loaded, 16)
            sp.dma_start(m.cent[:], ins["centroids"]).then_inc(loaded, 16)
            sp.dma_start(m.route[:, E:2 * E], ins["route_w"]).then_inc(loaded, 16)
            sp.dma_start(m.expand[:], ins["expand"]).then_inc(loaded, 16)
            sp.wait_ge(loaded, 15 * 16)

        @block.gpsimd
        def _(pool):
            for n, (buffer, value) in enumerate(((m.qs[64:96], 1.0), (m.qs[96:128], 0.0))):
                if n:
                    pool.wait_ge(made, n)
                pool.memset(buffer, value).then_inc(made, 1)

        @block.vector
        def _(dve):
            dve.memset(m.ks[64:96], 0.0).then_inc(built, 1)
            dve.memset(m.ks[96:128], 1.0).then_inc(built, 1)
            dve.memset(m.vst[:], 0.0).then_inc(built, 1)
            dve.wait_ge(built, 3)
            dve.memset(m.vst[:, :, :, HD:HD + 1], 1.0).then_inc(built, 1)
            dve.wait_ge(loaded, 15 * 16)
            dve.tensor_copy(m.identb[:], m.ident[:]).then_inc(built, 1)
            dve.tensor_copy(m.maskb[:], m.mask[:]).then_inc(built, 1)
            dve.tensor_scalar(m.qbias[:], m.abcol[:, :, 0], float(HD) ** -0.5, None, ALU.mult).then_inc(built, 1)
            dve.tensor_copy(m.y[:], m.x[:]).then_inc(built, 1)
            dve.wait_ge(built, 8)
            dve.wait_ge(made, 2)


def norm_stage(nc, m, tag, src, turned=False, ln=0, add=None, plain_out=None):
    dst = plain_out if plain_out is not None else m.nrm
    work = m.y if add is not None else src
    with ExitStack() as ctx:
        sem = stage_semaphores(nc, ctx, f"{tag}")
        summed, measured, aggregated, var_ready = sem("summed"), sem("measured"), sem("aggregated"), sem("var_ready")
        std_ready, rstd_ready = sem("std_ready"), sem("rstd_ready")
        normalized, turned_sem, evacuated = sem("normalized"), sem("turned"), sem("evacuated")
        block = ctx.enter_context(nc.Block())

        @block.vector
        def _(dve):
            if add is not None:
                for c in range(NCH):
                    dve.tensor_tensor(work[:, TB * c:TB * (c + 1), :], src[:, TB * c:TB * (c + 1), :],
                                      add[:, TB * c:TB * (c + 1), :], ALU.add).then_inc(summed, 1)
            for t in range(T):
                if add is not None:
                    dve.wait_ge(summed, t // TB + 1)
                dve.bn_stats(m.stats[:, t, :], work[:, t, :]).then_inc(measured, 1)
            for t in range(T):
                dve.wait_ge(measured, t + 1)
                dve.bn_aggr(m.meanvar[:, t, :], m.stats[:, t, :]).then_inc(aggregated, 1)
            dve.wait_ge(aggregated, T)
            dve.tensor_scalar(m.std[:], m.meanvar[:, :, 1], EPS, None, ALU.add).then_inc(var_ready, 1)
            dve.wait_ge(std_ready, 1)
            dve.reciprocal(m.rstd[:], m.std[:]).then_inc(rstd_ready, 1)
            dve.wait_ge(rstd_ready, 1)
            for t in range(T):
                dve.tensor_scalar(dst[:, t, :], work[:, t, :], m.meanvar[:, t, 0:1], m.rstd[:, t:t + 1],
                                  ALU.subtract, ALU.mult).then_inc(normalized, 1)

        @block.scalar
        def _(act):
            act.wait_ge(var_ready, 1)
            act.activation(m.std[:], m.std[:], ACT.Sqrt).then_inc(std_ready, 1)
            if turned:
                for c in range(NCH):
                    act.wait_ge(turned_sem, c + 1)
                    out = m.xT[:, BANK * c:BANK * (c + 1)]
                    if ln is None:
                        act.activation(out, m.psum[:, c, :], ACT.Copy).then_inc(evacuated, 1)
                    else:
                        act.activation(out, m.psum[:, c, :], ACT.Identity, bias=m.lncol[:, ln, 1:2],
                                       scale=m.lncol[:, ln, 0:1]).then_inc(evacuated, 1)

        if turned:
            @block.tensor
            def _(pe):
                for t in range(T):
                    pe.wait_ge(normalized, t + 1)
                    ins = pe.transpose(m.psum[:, t // TB, P * (t % TB):P * (t % TB + 1)], dst[:, t, :], m.ident[:])
                    if t % TB == TB - 1:
                        ins.then_inc(turned_sem, 1)


def project_stage(nc, m, a, attn_w, q_stack, k_stack):
    with ExitStack() as ctx:
        sem = stage_semaphores(nc, ctx, f"proj{a}")
        w_loaded, qk_mm, v_mm = sem("w_loaded"), sem("qk_mm"), sem("v_mm")
        full_ready, hi_ready, rest_ready, mid_ready = sem("full_ready"), sem("hi_ready"), sem("rest_ready"), sem("mid_ready")
        lo_ready, v_ready, stored = sem("lo_ready"), sem("v_ready"), sem("stored")
        block = ctx.enter_context(nc.Block())
        parts = lambda s, part, c: m.part[:, s, part, BANK * c:BANK * (c + 1)]

        @block.sync
        def _(sp):
            sp.dma_start(m.aw[:], attn_w[a]).then_inc(w_loaded, 16)
            for b in range(NB):
                last = 2 * (NCH // NB) * (b + 1)
                for part, ready in ((0, hi_ready), (1, mid_ready), (2, lo_ready)):
                    sp.wait_ge(ready, last)
                    for s, (stack, of_term) in enumerate(((q_stack, Q_PART), (k_stack, K_PART))):
                        for t in range(TERMS):
                            if of_term[t] == part:
                                dst = stack[t * HD:(t + 1) * HD, b * H:(b + 1) * H, :]
                                sp.dma_start(dst, m.part[:, s, part, b * S:(b + 1) * S]).then_inc(stored, 16)
            sp.wait_ge(stored, 16 * 2 * TERMS * NB)

        @block.tensor
        def _(pe):
            pe.wait_ge(w_loaded, 16)
            for c in range(NCH):
                for s in range(2):
                    if c >= 2:
                        pe.wait_ge(hi_ready, 2 * (c - 2) + s + 1)
                    pe.matmul(m.psum[:, 2 * (c % 2) + s, :], m.aw[:, s, :], m.xT[:, BANK * c:BANK * (c + 1)],
                              start=True, stop=True).then_inc(qk_mm, 1)
                if c >= 2:
                    pe.wait_ge(v_ready, c - 1)
                for t in range(TB):
                    tok = BANK * c + P * t
                    ins = pe.matmul(m.psum[:, 4 + c % 2, P * t:P * (t + 1)], m.xT[:, tok:tok + P], m.aw[:, 2, :],
                                    start=True, stop=True)
                ins.then_inc(v_mm, 1)

        @block.scalar
        def _(act):
            for n in range(2 * NCH):
                c, s = n // 2, n % 2
                act.wait_ge(qk_mm, n + 1)
                if n >= 4:
                    act.wait_ge(rest_ready, n - 3)
                bias = m.qbias[:, a:a + 1] if s == 0 else m.abcol[:, a, 1:2]
                scale = float(HD) ** -0.5 if s == 0 else 1.0
                act.activation(m.full[:, s, c % 2, :], m.psum[:, 2 * (c % 2) + s, :], ACT.Identity, bias=bias,
                               scale=scale).then_inc(full_ready, 1)
                act.activation(parts(s, 0, c), m.psum[:, 2 * (c % 2) + s, :], ACT.Identity, bias=bias,
                               scale=scale).then_inc(hi_ready, 1)

        @block.vector
        def _(dve):
            for n in range(2 * NCH):
                c, s = n // 2, n % 2
                dve.wait_ge(full_ready, n + 1)
                dve.wait_ge(hi_ready, n + 1)
                if n >= 4:
                    dve.wait_ge(lo_ready, n - 3)
                dve.tensor_tensor(m.rest[:, s, c % 2, :], m.full[:, s, c % 2, :], parts(s, 0, c),
                                  ALU.subtract).then_inc(rest_ready, 1)
                dve.wait_ge(rest_ready, n + 1)
                dve.tensor_copy(parts(s, 1, c), m.rest[:, s, c % 2, :]).then_inc(mid_ready, 1)
                if s == 1:
                    dve.wait_ge(v_mm, c + 1)
                    b, kt = c // (NCH // NB), TB * (c % (NCH // NB))
                    out = m.v[:, b * HG:(b + 1) * HG, kt:kt + TB, :].rearrange("p g t w -> p t g w")
                    val = m.psum[:, 4 + c % 2, :].rearrange("p (t g w) -> p t g w", t=TB, g=HG)
                    for t in range(TB):
                        ins = dve.tensor_tensor(out[:, t], val[:, t],
                                                m.abrow[:, a, 0, :].rearrange("p (g w) -> p g w", g=HG), ALU.add)
                    ins.then_inc(v_ready, 1)

        @block.gpsimd
        def _(pool):
            for n in range(2 * NCH):
                c, s = n // 2, n % 2
                pool.wait_ge(mid_ready, n + 1)
                pool.tensor_tensor(parts(s, 2, c), m.rest[:, s, c % 2, :], parts(s, 1, c),
                                   ALU.subtract).then_inc(lo_ready, 1)


def attention_stage(nc, m, a, causal, bias_rows, q_stack, k_stack):
    RING = 3
    halves = [[kt for kt in range(QT) if not causal or kt < TB * (hf + 1)] for hf in range(2)]
    units = [(hf, kt) for hf in range(2) for kt in halves[hf]]
    U = len(units)
    rows = []
    for c in range(2):
        for qt in range(QT):
            keys = S if not causal else P * (qt + 1)
            for j in range(G):
                if keys > BANK * c:
                    rows.append((j, qt, BANK * c, min(keys - BANK * c, BANK)))
    first_q = lambda u: max(units[u][0] * BANK, units[u][1] * P) if causal else units[u][0] * BANK
    TURNS = 1 if causal else 2
    last_of_half = [len(halves[0]) - 1, U - 1]

    def plan(next_group, this_group, turn_prev):
        steps = []
        a_left = list(range(len(rows))) if next_group else []
        if not this_group:
            return ([("turn", 1, i) for i in range(TURNS)] if turn_prev else []) + [("row", i) for i in a_left] \
                + ([("turn_max",)] if next_group else [])
        rate = -(-len(rows) // (U - 2))
        for u in range(U):
            steps.append(("col", u))
            if u == 1 and turn_prev:
                steps += [("turn", 1, i) for i in range(TURNS)]
            if u == last_of_half[0] + 3:
                steps += [("turn", 0, i) for i in range(TURNS)]
            take, a_left = a_left[:rate], a_left[rate:]
            steps += [("row", i) for i in take]
            if next_group and not a_left and not take and ("turn_max",) not in steps:
                steps.append(("turn_max",))
            if u >= 1:
                steps.append(("pv", u - 1))
        steps.append(("pv", U - 1))
        assert not a_left
        return steps

    first = plan(True, False, False)
    body0 = plan(True, True, False)
    body = plan(True, True, True)
    last = plan(False, True, True)
    tail = plan(False, False, True)
    in_ring = lambda s: s[0] in ("row", "turn", "turn_max")
    ring_len = lambda steps: sum(in_ring(s) for s in steps)
    assert ring_len(body) % RING == 0

    def program(eng, run):
        base = 0
        run(first, -1, base, base)
        base += ring_len(first)
        run(body0, 0, base, base)
        base += ring_len(body0)
        n = ring_len(body)
        with eng.Fori(1, NG - 1) as it:
            run(body, it, it * n + (base - n), base)
        base += n * (NG - 2)
        run(last, NG - 1, base, base)
        base += ring_len(last)
        run(tail, NG, base, base)

    with ExitStack() as ctx:
        sem = stage_semaphores(nc, ctx, f"attn{a}")
        stacks_loaded, max_loaded = sem("stacks_loaded"), sem("max_loaded")
        ring_full, ring_free = sem("ring_full"), sem("ring_free")
        col_full, prob_full = sem("col_full"), sem("prob_full")
        pv_done, out_copied, inverted = sem("pv_done"), sem("out_copied"), sem("inverted")
        mx_set, v_staged, neg_step, neg_split = sem("mx_set"), sem("v_staged"), sem("neg_step"), sem("neg_split")
        block = ctx.enter_context(nc.Block())
        ROWS_DMA = 3 if bias_rows is not None else 2

        CRED_RING, CRED_COL, CRED_PV, CRED_OUT, CRED_TURN = RING, 2, 2, 1, 2 * TURNS
        OUT = 7
        TPT = TB // TURNS
        col_bank = lambda u, p: RING + 2 * ((2 * u + p) % 2)
        max_at = lambda steps: ring_len(steps[:steps.index(("turn_max",))]) + 1

        def stack_cols(stack, rows, slot, j, col, n):
            flat = stack[:].rearrange("p s j t -> p (s j t)")
            return flat[0:rows, bass.ds(slot + (j * S + col), n)]

        @block.sync
        def _(sp):
            def load(g):
                off = bass.ds(g * G, G)
                slot = bass.ds((g % 3) * G, G)
                qs, ks = (x[:].rearrange("p s j t -> p (s j) t") for x in (m.qs, m.ks))
                sp.dma_start(qs[0:ROW_BIAS, slot, :], q_stack[:, off, :]).then_inc(stacks_loaded, 16)
                sp.dma_start(ks[0:ROW_BIAS, slot, :], k_stack[:, off, :]).then_inc(stacks_loaded, 16)
                if bias_rows is not None:
                    sp.dma_start(ks[ROW_BIAS:ROW_BIAS + 3, slot, :], bias_rows[:, off, :]).then_inc(stacks_loaded, 16)

            def load_max(g, turned):
                sp.wait_ge(ring_free, turned)
                qs = m.qs[:].rearrange("p s j t -> p s (j t)")
                for part in range(3):
                    sp.dma_start(qs[ROW_MAX + part:ROW_MAX + part + 1, bass.ds(g % 3, 1), :],
                                 m.maxT[G * QT * part:G * QT * (part + 1), :]).then_inc(max_loaded, 16)

            n = ring_len(body)
            for g in range(3):
                load(g)
                sp.wait_ge(stacks_loaded, 16 * ROWS_DMA * (g + 1))
            load_max(0, CRED_RING + max_at(first))
            load_max(1, CRED_RING + ring_len(first) + max_at(body0))
            base = CRED_RING + ring_len(first) + ring_len(body0) + max_at(body)
            with sp.Fori(1, NG - 2) as it:
                sp.wait_ge(pv_done, it * U + CRED_PV)
                load(it + 2)
                sp.wait_ge(stacks_loaded, it * (16 * ROWS_DMA) + 3 * 16 * ROWS_DMA)
                load_max(it + 1, it * n + (base - n))
            load_max(NG - 1, base + n * (NG - 3))
            sp.wait_ge(max_loaded, 16 * 3 * NG)

        @block.tensor
        def _(pe):
            def run(steps, it, count, ring):
                n = 0
                this_slot, next_slot = ((it % 3) * (G * S), ((it + 1) % 3) * (G * S))
                if not isinstance(it, int):
                    this_slot, next_slot = pe.snap(this_slot), pe.snap(next_slot)
                for step in steps:
                    kind = step[0]
                    if kind in ("row", "turn", "turn_max"):
                        pe.wait_ge(ring_free, count + (n + 1))
                        bank = (ring + n) % RING
                        n += 1
                    if kind == "row":
                        j, qt, k0, keys = rows[step[1]]
                        g = it + 1
                        if step[1] == 0:
                            pe.wait_ge(stacks_loaded, g * (16 * ROWS_DMA) + 16 * ROWS_DMA)
                        diagonal = causal and k0 + keys == P * (qt + 1)
                        ins = pe.matmul(m.psum[:, bank, 0:keys], stack_cols(m.qs, ROW_MAX, next_slot, j, P * qt, P),
                                        stack_cols(m.ks, ROW_MAX, next_slot, j, k0, keys), start=True, stop=not diagonal)
                        if diagonal:
                            ins = pe.matmul(m.psum[:, bank, keys - P:keys], m.identb[:], m.maskb[:, 0, :],
                                            start=False, stop=True)
                        ins.then_inc(ring_full, 1)
                    elif kind == "turn_max":
                        pe.wait_ge(neg_split, (it + 1) + 1)
                        pe.matmul(m.psum[0:3 * G * QT, bank, 0:P], m.negp[:].rearrange("p a b -> p (a b)"), m.identb[:],
                                  start=True, stop=True).then_inc(ring_full, 1)
                    elif kind == "turn":
                        hf, i = step[1:]
                        g = it - 1 if hf == 1 else it
                        if i == 0:
                            pe.wait_ge(out_copied, g * 2 + (hf + 1 + CRED_OUT))
                        for k in range(TPT):
                            ins = pe.transpose(m.psum[:, bank, P * k:P * (k + 1)],
                                               m.outT[:, hf, P * (i * TPT + k):P * (i * TPT + k + 1)], m.ident[:])
                        ins.then_inc(ring_full, 1)
                    elif kind == "col":
                        u = step[1]
                        hf, kt = units[u]
                        q0 = first_q(u)
                        if u == 0:
                            pe.wait_ge(max_loaded, it * 48 + 48)
                        for p in range(2):
                            pe.wait_ge(prob_full, it * (2 * U) + (2 * u + p + 1))
                            for jj in range(2):
                                j = 2 * p + jj
                                out = m.psum[:, col_bank(u, p) + jj, q0 - BANK * hf:BANK]
                                diagonal = causal and kt >= TB * hf
                                ins = pe.matmul(out, stack_cols(m.ks, P, this_slot, j, P * kt, P),
                                                stack_cols(m.qs, P, this_slot, j, q0, BANK * (hf + 1) - q0),
                                                start=True, stop=not diagonal)
                                if diagonal:
                                    ins = pe.matmul(out[:, 0:P], m.identb[:], m.maskb[:, 1, :], start=False, stop=True)
                            ins.then_inc(col_full, 1)
                    else:
                        u = step[1]
                        hf, kt = units[u]
                        off = first_q(u) - BANK * hf
                        if u == 0:
                            pe.wait_ge(v_staged, it + 1)
                        if kt == 0:
                            pe.wait_ge(out_copied, it * 2 + (hf + 1))
                        pe.wait_ge(prob_full, it * (2 * U) + (2 * u + 2 + CRED_COL))
                        for j in range(G):
                            ins = pe.matmul(m.psum[32 * j:32 * (j + 1), OUT, off:BANK], m.vst[:, kt, j, :],
                                            m.prob[:, (2 * u + j // 2) % 4, j % 2, off:BANK],
                                            start=kt == 0, stop=kt == halves[hf][-1])
                        ins.then_inc(pv_done, 1)

            program(pe, run)

        @block.scalar
        def _(act):
            act.sem_inc(prob_full, CRED_COL)
            act.sem_inc(out_copied, CRED_OUT)

            def run(steps, it, count, ring):
                for step in steps:
                    if step[0] == "col":
                        u = step[1]
                        off = first_q(u) - BANK * units[u][0]
                        for p in range(2):
                            if p == 0:
                                act.wait_ge(pv_done, it * U + (u + 1))
                            act.wait_ge(col_full, it * (2 * U) + (2 * u + p + 1))
                            b = col_bank(u, p)
                            act.activation(m.prob[:, (2 * u + p) % 4, :, off:BANK], m.psum[:, b:b + 2, off:BANK],
                                           ACT.Exp).then_inc(prob_full, 1)
                    elif step[0] == "pv" and step[1] in last_of_half:
                        hf = last_of_half.index(step[1])
                        act.wait_ge(pv_done, it * U + (step[1] + 1 + CRED_PV))
                        act.wait_ge(inverted, it * (2 * TURNS) + TURNS * (hf + 1))
                        act.copy(m.outT[:, hf, :], m.psum[:, OUT, :]).then_inc(out_copied, 1)

            program(act, run)

        @block.vector
        def _(dve):
            dve.sem_inc(ring_free, CRED_RING)
            dve.sem_inc(pv_done, CRED_PV)
            dve.sem_inc(inverted, CRED_TURN)
            dve.memset(m.mx[:], -BIG).then_inc(mx_set, 1)
            dve.wait_ge(mx_set, 1)

            def run(steps, it, count, ring):
                n = 0
                if steps and steps[0][0] == "col":
                    dve.wait_ge(pv_done, it * U + CRED_PV)
                    v = m.v[:].rearrange("p g t w -> p g (t w)")[:, bass.ds(it, 1), :]
                    dve.tensor_copy(m.vst[:, :, :, 0:HD], v.rearrange("p g (t j w) -> p (g t) j w", t=QT, j=G))\
                        .then_inc(v_staged, 1)
                for step in steps:
                    kind = step[0]
                    if kind in ("row", "turn", "turn_max"):
                        bank = (ring + n) % RING
                        n += 1
                    if kind == "row":
                        j, qt, k0, keys = rows[step[1]]
                        dve.wait_ge(ring_full, count + n)
                        dve.reduce_max(m.mx[:, j, qt, k0 // BANK:k0 // BANK + 1], m.psum[:, bank, 0:keys], AX_X)\
                            .then_inc(ring_free, 1)
                    elif kind == "turn_max":
                        k = (it + 1) * 4
                        dve.wait_ge(ring_free, count + (n - 1 + CRED_RING))
                        dve.wait_ge(neg_split, it + 1)
                        dve.wait_ge(ring_full, count + (n - 1))
                        dve.tensor_reduce(m.negm[:], m.mx[:].rearrange("p j t c -> p (j t) c"), AX_X, ALU.max,
                                          negate=True).then_inc(neg_step, 1)
                        dve.wait_ge(neg_step, k + 1)
                        dve.tensor_copy(m.negp[:, 0, :], m.negm[:]).then_inc(neg_step, 1)
                        dve.wait_ge(neg_step, k + 2)
                        dve.tensor_tensor(m.negr[:], m.negm[:], m.negp[:, 0, :], ALU.subtract).then_inc(neg_step, 1)
                        dve.wait_ge(neg_step, k + 3)
                        dve.tensor_copy(m.negp[:, 1, :], m.negr[:]).then_inc(neg_step, 1)
                        dve.wait_ge(neg_step, k + 4)
                        dve.tensor_tensor(m.negp[:, 2, :], m.negr[:], m.negp[:, 1, :], ALU.subtract).then_inc(neg_split, 1)
                        dve.wait_ge(ring_full, count + n)
                        dve.wait_ge(max_loaded, (it + 1) * 48)
                        dve.tensor_copy(m.maxT[:], m.psum[0:3 * G * QT, bank, 0:P]).then_inc(ring_free, 1)
                    elif kind == "turn":
                        hf, i = step[1:]
                        g = it - 1 if hf == 1 else it
                        k = g * (2 * TURNS) + (hf * TURNS + i)
                        sums = m.psum[:, bank, 0:P * TPT].rearrange("p (t j w) -> p t j w", t=TPT, j=G)
                        dve.wait_ge(ring_full, count + n)
                        inv = m.rsum[:, hf, i * TPT:(i + 1) * TPT, :]
                        dve.reciprocal(inv, sums[:, :, :, HD]).then_inc(inverted, 1)
                        dve.wait_ge(inverted, k + (1 + CRED_TURN))
                        qt = hf * TB + i * TPT
                        out = m.ctx[:].rearrange("p t (g j w) -> p t g j w", g=HG, j=G)
                        out = out[:, bass.ds(g // HG * QT + qt, TPT), bass.ds(g % HG, 1), :, :]
                        out = out.rearrange("p t g j w -> p t (g j) w")
                        dve.tensor_tensor(out, sums[:, :, :, 0:HD], inv.unsqueeze(3).to_broadcast([P, TPT, G, HD]),
                                          ALU.mult).then_inc(ring_free, 1)

            program(dve, run)


def out_project_stage(nc, m, a):
    with ExitStack() as ctx:
        sem = stage_semaphores(nc, ctx, f"out{a}")
        turned, copied, projected, biased, added = sem("turned"), sem("copied"), sem("projected"), sem("biased"), sem("added")
        block = ctx.enter_context(nc.Block())
        ctxT = m.nrm[:].rearrange("p t f -> p (t f)")

        @block.tensor
        def _(pe):
            def project(c):
                pe.wait_ge(copied, c + 1)
                for k in range(TB):
                    col = BANK * c + P * k
                    ins = pe.matmul(m.psum[:, 4 + c, P * k:P * (k + 1)], ctxT[:, col:col + P], m.aw[:, 3, :],
                                    start=True, stop=True)
                ins.then_inc(projected, 1)

            for c in range(NCH):
                for k in range(TB):
                    ins = pe.transpose(m.psum[:, c, P * k:P * (k + 1)], m.ctx[:, TB * c + k, :], m.ident[:])
                ins.then_inc(turned, 1)
                if c:
                    project(c - 1)
            project(NCH - 1)

        @block.scalar
        def _(act):
            for c in range(NCH):
                act.wait_ge(turned, c + 1)
                act.copy(ctxT[:, BANK * c:BANK * (c + 1)], m.psum[:, c, :]).then_inc(copied, 1)

        @block.vector
        def _(dve):
            bias = m.abrow[:, a, 1, :].unsqueeze(1).to_broadcast([P, TB, D])
            for c in range(NCH):
                y = m.y[:, TB * c:TB * (c + 1), :]
                dve.tensor_tensor(y, y, bias, ALU.add).then_inc(biased, 1)
            for c in range(NCH):
                y = m.y[:, TB * c:TB * (c + 1), :]
                dve.wait_ge(projected, c + 1)
                dve.wait_ge(biased, c + 1)
                dve.tensor_tensor(y, m.psum[:, 4 + c, :].rearrange("p (t f) -> p t f", t=TB), y, ALU.add).then_inc(added, 1)


def ffn_bias_stage(nc, m):
    with ExitStack() as ctx:
        biased = stage_semaphores(nc, ctx, "ffn")("biased")
        block = ctx.enter_context(nc.Block())

        @block.vector
        def _(dve):
            dve.memset(m.gate[:], 1.0).then_inc(biased, 1)
            for c in range(NCH):
                y = m.y[:, TB * c:TB * (c + 1), :]
                dve.tensor_tensor(y, y, m.b2ffn[:].unsqueeze(1).to_broadcast([P, TB, D]), ALU.add).then_inc(biased, 1)


def top_two(dve, act, m, n, step, e2_ready):
    if act is not None:
        act.wait_ge(step, 2 * n + 1)
        act.activation(m.tmp[:, 0:n, 1], m.tmp[:, 0:n, 0], ACT.Exp).then_inc(e2_ready, 1)
        return
    for t in range(n):
        dve.max(m.top[:, t, :], m.lg[:, t, :]).then_inc(step, 1)
    for t in range(n):
        dve.wait_ge(step, t + 1)
        dve.max_index(m.idx[:, t, :], m.top[:, t, :], m.lg[:, t, :]).then_inc(step, 1)
    dve.wait_ge(step, 2 * n)
    dve.tensor_tensor(m.tmp[:, 0:n, 0], m.top[:, 0:n, 1], m.top[:, 0:n, 0], ALU.subtract).then_inc(step, 1)
    dve.tensor_copy(m.idxf[:, 0:n, :], m.idx[:, 0:n, :]).then_inc(step, 1)
    dve.wait_ge(e2_ready, 1)
    dve.tensor_scalar(m.tmp[:, 0:n, 2], m.tmp[:, 0:n, 1], 1.0, None, ALU.add).then_inc(step, 1)
    dve.wait_ge(step, 2 * n + 3)
    dve.reciprocal(m.sel[:, 0:n, 0], m.tmp[:, 0:n, 2]).then_inc(step, 1)
    dve.wait_ge(step, 2 * n + 4)
    dve.tensor_tensor(m.sel[:, 0:n, 1], m.sel[:, 0:n, 0], m.tmp[:, 0:n, 1], ALU.mult).then_inc(step, 1)
    dve.wait_ge(step, 2 * n + 5)
    iota = m.iota8[:].unsqueeze(1).to_broadcast([P, n, E])
    for k, out in ((0, m.gate), (1, m.pick)):
        out = out[:, 0:n, :]
        dve.tensor_tensor(out, iota, m.idxf[:, 0:n, k:k + 1].to_broadcast([P, n, E]), ALU.is_equal).then_inc(step, 1)
        dve.wait_ge(step, 2 * n + 6 + 2 * k)
        dve.tensor_tensor(out, out, m.sel[:, 0:n, k:k + 1].to_broadcast([P, n, E]), ALU.mult).then_inc(step, 1)
        dve.wait_ge(step, 2 * n + 7 + 2 * k)
    dve.tensor_tensor(m.gate[:, 0:n, :], m.gate[:, 0:n, :], m.pick[:, 0:n, :], ALU.add).then_inc(step, 1)
    dve.wait_ge(step, 2 * n + 10)


def gates_stage(nc, m, layer, by_sequence):
    with ExitStack() as ctx:
        sem = stage_semaphores(nc, ctx, f"gates{layer}")
        meaned, logits_mm, lg_ready, step, e2_ready = sem("meaned"), sem("logits_mm"), sem("lg_ready"), sem("step"), sem("e2_ready")
        gates_ready, turned, copied, biased_mm, biased = sem("gates_ready"), sem("turned"), sem("copied"), sem("biased_mm"), sem("biased")
        block = ctx.enter_context(nc.Block())
        n = NB if by_sequence else T
        lg_psum = m.psum[:, 0, 0:n * E].rearrange("p (t e) -> p t e", e=E)

        @block.tensor
        def _(pe):
            if by_sequence:
                pe.wait_ge(meaned, 2)
            for t in range(n):
                lhs = m.mrep[:, t, :] if by_sequence else m.xT[:, P * t:P * (t + 1)]
                ins = pe.matmul(m.psum[:, 0, E * t:E * (t + 1)], lhs, m.gate_w[:, layer, :], start=True, stop=True)
            ins.then_inc(logits_mm, 1)
            pe.wait_ge(gates_ready, NB)
            for t in range(T):
                ins = pe.transpose(m.psum[0:E, 1 + t // TB, P * (t % TB):P * (t % TB + 1)], m.gate[:, t, :], m.ident[:])
                if t % TB == TB - 1:
                    ins.then_inc(turned, 1)
            for c in range(NCH):
                pe.wait_ge(copied, c + 1)
                for k in range(TB):
                    bank = 5 + c % 3
                    if c == 3 and k == 0:
                        pe.wait_ge(biased, 1)
                    ins = pe.matmul(m.psum[:, bank, P * k:P * (k + 1)], m.gT[:, TB * c + k, :], m.b2[:, layer, :],
                                    start=True, stop=True)
                ins.then_inc(biased_mm, 1)

        @block.scalar
        def _(act):
            top_two(None, act, m, n, step, e2_ready)
            for c in range(NCH):
                act.wait_ge(turned, c + 1)
                act.copy(m.gT[:, TB * c:TB * (c + 1), :], m.psum[0:E, 1 + c, :].rearrange("e (t p) -> e t p", t=TB))\
                    .then_inc(copied, 1)

        @block.vector
        def _(dve):
            if by_sequence:
                dve.reduce_sum(m.msum[:], m.xT[:].rearrange("p (b s) -> p b s", b=NB), AX_X).then_inc(meaned, 1)
                dve.wait_ge(meaned, 1)
                dve.tensor_scalar(m.mrep[:], m.msum[:].unsqueeze(2).to_broadcast([P, NB, P]), 1.0 / S, None, ALU.mult)\
                    .then_inc(meaned, 1)
            dve.wait_ge(logits_mm, 1)
            dve.tensor_tensor(m.lg[:, 0:n, :], lg_psum, m.gate_b[:, layer, :].unsqueeze(1).to_broadcast([P, n, E]),
                              ALU.add).then_inc(lg_ready, 1)
            dve.wait_ge(lg_ready, 1)
            top_two(dve, None, m, n, step, e2_ready)
            if by_sequence:
                dve.tensor_copy(m.pick[:, 0:NB, :], m.gate[:, 0:NB, :]).then_inc(lg_ready, 1)
                dve.wait_ge(lg_ready, 2)
                for b in range(NB):
                    dve.tensor_copy(m.gate[:, b * QT:(b + 1) * QT, :], m.pick[:, b:b + 1, :].to_broadcast([P, QT, E]))\
                        .then_inc(gates_ready, 1)
            else:
                dve.sem_inc(gates_ready, NB)
            for c in range(NCH):
                dve.wait_ge(biased_mm, c + 1)
                y = m.y[:, TB * c:TB * (c + 1), :]
                dve.tensor_tensor(y, m.psum[:, 5 + c % 3, :].rearrange("p (t f) -> p t f", t=TB), y, ALU.add)\
                    .then_inc(biased, 1)


def experts_stage(nc, m, tag, experts, first, mode):
    with ExitStack() as ctx:
        sem = stage_semaphores(nc, ctx, f"{tag}")
        w_loaded = [sem("w_loaded0"), sem("w_loaded1")]
        up_mm, gelu_done, down_mm, added = sem("up_mm"), sem("gelu_done"), sem("down_mm"), sem("added")
        block = ctx.enter_context(nc.Block())
        chosen = mode == "chosen"
        passes = 2 if experts > 1 else 1
        loops = experts // passes
        C = NCH // NB if chosen else NCH
        UB = passes * C
        tok_step = S if chosen else 0
        CRED_UP, CRED_H, CRED_ACC = FC, 2, 2
        w1 = lambda p, k: m.wring[:, p, P * k:P * (k + 1)]
        b1 = lambda p, k: m.wring[:, p, F + k:F + k + 1]
        w2 = lambda p, k: m.wring[:, p, F + FC + D * k:F + FC + D * (k + 1)]

        def looped(eng, body):
            if loops == 1:
                body(0)
            else:
                with eng.Fori(0, loops) as i:
                    body(i)

        @block.sync
        def _(sp):
            experts_w = m.experts_w
            if loops == 1:
                sp.dma_start(m.wring[:, 0, :], experts_w[first]).then_inc(w_loaded[0], 16)
            else:
                for p in range(passes):
                    which = (sp.value_load(m.idx[0:1, 0:1, p:p + 1], min_val=0, max_val=E - 1) + first) if chosen else p + first
                    sp.dma_start(m.wring[:, p:p + 1, :], experts_w[bass.ds(which, 1)].rearrange("e p w -> p e w"))\
                        .then_inc(w_loaded[p], 16)
                with sp.Fori(1, loops) as i:
                    for p in range(passes):
                        if chosen:
                            which = sp.value_load(m.idx[0:1, bass.ds(i, 1), p:p + 1], min_val=0, max_val=E - 1) + first
                        else:
                            which = i * passes + (p + first)
                        sp.wait_ge(down_mm, i * UB + (CRED_H - (passes - 1 - p) * C))
                        sp.dma_start(m.wring[:, p:p + 1, :], experts_w[bass.ds(which, 1)].rearrange("e p w -> p e w"))\
                            .then_inc(w_loaded[p], 16)

        @block.tensor
        def _(pe):
            def body(i):
                for p in range(passes):
                    pe.wait_ge(w_loaded[p], i * 16 + 16)
                    for c in range(C):
                        u = p * C + c
                        for k in range(FC):
                            pe.wait_ge(gelu_done, i * (UB * FC) + (u * FC + k + 1))
                            pe.matmul(m.psum[:, k, :], w1(p, k), m.xT[:, bass.ds(i * tok_step + BANK * c, BANK)],
                                      start=True, stop=True).then_inc(up_mm, 1)
                        pe.wait_ge(added, i * UB + (u + 1))
                        for k in range(FC):
                            pe.wait_ge(gelu_done, i * (UB * FC) + (u * FC + k + 1 + CRED_UP))
                            for t in range(TB):
                                ins = pe.matmul(m.psum[:, 4 + u % 2, P * t:P * (t + 1)], m.h[:, u % 2, k, P * t:P * (t + 1)],
                                                w2(p, k), start=(k == 0 and t == 0), stop=k == FC - 1,
                                                skip_group_check=True)
                        ins.then_inc(down_mm, 1)
            looped(pe, body)

        @block.scalar
        def _(act):
            act.sem_inc(gelu_done, CRED_UP)

            def body(i):
                for p in range(passes):
                    act.wait_ge(w_loaded[p], i * 16 + 16)
                    for c in range(C):
                        u = p * C + c
                        act.wait_ge(down_mm, i * UB + (u + 1))
                        for k in range(FC):
                            act.wait_ge(up_mm, i * (UB * FC) + (u * FC + k + 1))
                            act.activation(m.h[:, u % 2, k, :], m.psum[:, k, :], ACT.Gelu, bias=b1(p, k))\
                                .then_inc(gelu_done, 1)
            looped(act, body)

        @block.vector
        def _(dve):
            dve.sem_inc(down_mm, CRED_H)
            dve.sem_inc(added, CRED_ACC)

            def body(i):
                for p in range(passes):
                    for c in range(C):
                        u = p * C + c
                        dve.wait_ge(down_mm, i * UB + (u + 1 + CRED_H))
                        dve.wait_ge(added, i * UB + (u + CRED_ACC))
                        for t in range(TB):
                            tile = TB * c + t
                            y = m.y[:].rearrange("p t f -> p (t f)")[:, bass.ds(i * (tok_step // P * D) + tile * D, D)]
                            if chosen:
                                gate = m.sel[:].rearrange("p t k -> p (t k)")[:, bass.ds(i * 2 + p, 1)]
                            else:
                                gate = m.gate[:].rearrange("p t e -> p (t e)")[:, bass.ds(i * passes + (tile * E + p), 1)]
                            ins = dve.scalar_tensor_tensor(out=y, in0=m.psum[:, 4 + u % 2, P * t:P * (t + 1)], scalar=gate,
                                                           in1=y, op0=ALU.mult, op1=ALU.add)
                        ins.then_inc(added, 1)
            looped(dve, body)


def tail_stage(nc, m, out):
    with ExitStack() as ctx:
        sem = stage_semaphores(nc, ctx, f"tail")
        cstep, csqrt, ct_mm, route_ready, score_mm = sem("cstep"), sem("csqrt"), sem("ct_mm"), sem("route_ready"), sem("score_mm")
        squared, xsqrt, lg_step, exp_ready = sem("squared"), sem("xsqrt"), sem("lg_step"), sem("exp_ready")
        turned, gt_ready, up_mm, gelu_done = sem("turned"), sem("gt_ready"), sem("up_mm"), sem("gelu_done")
        wide_mm, gated, down_mm, added = sem("wide_mm"), sem("gated"), sem("down_mm"), sem("added")
        block = ctx.enter_context(nc.Block())
        w1 = lambda k: m.tail_w[:, P * k:P * (k + 1)]
        b1 = lambda k: m.tail_w[:, F + k:F + k + 1]
        w2 = lambda k: m.tail_w[:, F + FC + D * k:F + FC + D * (k + 1)]
        N_SQ = 16

        @block.tensor
        def _(pe):
            pe.wait_ge(cstep, 5)
            pe.transpose(m.psum[:, 0, 0:E], m.cscr[:], m.ident[0:E, 0:E]).then_inc(ct_mm, 1)
            pe.wait_ge(route_ready, 1)
            for t in range(T):
                ins = pe.matmul(m.psum[:, 1, 2 * E * t:2 * E * (t + 1)], m.xT[:, P * t:P * (t + 1)], m.route[:],
                                start=True, stop=True)
            ins.then_inc(score_mm, 1)
            pe.wait_ge(lg_step, T + 7)
            for t in range(T):
                ins = pe.transpose(m.psum[0:E, 2 + t // TB, P * (t % TB):P * (t % TB + 1)], m.gate[:, t, :], m.ident[:])
                if t % TB == TB - 1:
                    ins.then_inc(turned, 1)
            for c in range(NCH):
                pe.wait_ge(gt_ready, NCH)
                for k in range(FC):
                    n = c * FC + k
                    if n >= 2:
                        pe.wait_ge(gelu_done, n - 1)
                    pe.matmul(m.psum[:, n % 2, :], w1(k), m.xT[:, BANK * c:BANK * (c + 1)], start=True, stop=True)\
                        .then_inc(up_mm, 1)
                    if n >= 2:
                        pe.wait_ge(gated, n - 1)
                    pe.matmul(m.psum[:, 2 + n % 2, :], m.expand[:, P * k:P * (k + 1)],
                              m.gT[:, TB * c:TB * (c + 1), :].rearrange("e t p -> e (t p)"), start=True, stop=True)\
                        .then_inc(wide_mm, 1)
                if c >= 2:
                    pe.wait_ge(added, c - 1)
                for k in range(FC):
                    pe.wait_ge(gated, c * FC + k + 1)
                    for t in range(TB):
                        pe.matmul(m.psum[:, 6 + c % 2, P * t:P * (t + 1)], m.h[:, c % 2, k, P * t:P * (t + 1)], w2(k),
                                  start=(k == 0 and t == 0), stop=False, skip_group_check=True)
                for t in range(TB):
                    ins = pe.matmul(m.psum[:, 6 + c % 2, P * t:P * (t + 1)], m.gT[:, TB * c + t, :], m.b2[:, 2, :],
                                    start=False, stop=True, skip_group_check=True)
                ins.then_inc(down_mm, 1)

        @block.scalar
        def _(act):
            act.wait_ge(cstep, 1)
            act.activation(m.cn[:, 1:2], m.cn[:, 0:1], ACT.Sqrt).then_inc(csqrt, 1)
            act.wait_ge(squared, 1 + T)
            act.activation(m.std[:], m.tmp[:, :, 0], ACT.Sqrt).then_inc(xsqrt, 1)
            act.wait_ge(lg_step, T + 3)
            act.activation(m.pick[:], m.lg[:], ACT.Exp).then_inc(exp_ready, 1)
            for c in range(NCH):
                act.wait_ge(turned, c + 1)
                act.copy(m.gT[:, TB * c:TB * (c + 1), :], m.psum[0:E, 2 + c, :].rearrange("e (t p) -> e t p", t=TB))\
                    .then_inc(gt_ready, 1)
            for c in range(NCH):
                if c >= 2:
                    act.wait_ge(down_mm, c - 1)
                for k in range(FC):
                    n = c * FC + k
                    act.wait_ge(up_mm, n + 1)
                    act.activation(m.h[:, c % 2, k, :], m.psum[:, n % 2, :], ACT.Gelu, bias=b1(k)).then_inc(gelu_done, 1)

        @block.vector
        def _(dve):
            dve.memset(m.cn[:], 0.0).then_inc(squared, 1)
            dve.wait_ge(squared, 1)
            dve.tensor_tensor_reduce(out=m.cscr[:], in0=m.cent[:], in1=m.cent[:], scale=1.0, scalar=0.0, op0=ALU.mult,
                                     op1=ALU.add, accum_out=m.cn[:, 0:1]).then_inc(cstep, 1)
            dve.wait_ge(csqrt, 1)
            dve.tensor_scalar(m.cn[:, 2:3], m.cn[:, 1:2], 1e-12, None, ALU.max).then_inc(cstep, 1)
            dve.wait_ge(cstep, 2)
            dve.reciprocal(m.cn[:, 3:4], m.cn[:, 2:3]).then_inc(cstep, 1)
            dve.wait_ge(cstep, 3)
            dve.tensor_scalar(m.cscr[:], m.cent[:], m.cn[:, 3:4], None, ALU.mult).then_inc(cstep, 2)
            dve.wait_ge(ct_mm, 1)
            dve.tensor_copy(m.route[:, 0:E], m.psum[:, 0, 0:E]).then_inc(route_ready, 1)
            for t in range(T):
                dve.tensor_tensor_reduce(out=m.nrm[:, t, :], in0=m.x[:, t, :], in1=m.x[:, t, :], scale=1.0, scalar=0.0,
                                         op0=ALU.mult, op1=ALU.add, accum_out=m.tmp[:, t, 0:1]).then_inc(squared, 1)
            dve.wait_ge(xsqrt, 1)
            dve.tensor_scalar(m.std[:], m.std[:], 1e-12, None, ALU.max).then_inc(xsqrt, 1)
            dve.wait_ge(xsqrt, 2)
            dve.reciprocal(m.rstd[:], m.std[:]).then_inc(xsqrt, 1)
            dve.wait_ge(score_mm, 1)
            dve.wait_ge(xsqrt, 3)
            scores = m.psum[:, 1, 0:2 * E * T].rearrange("p (t k e) -> p t k e", t=T, k=2)
            wide = lambda x: x.to_broadcast([P, T, E])
            dve.tensor_tensor(m.lg[:], scores[:, :, 0, :], wide(m.rstd[:].unsqueeze(2)), ALU.mult).then_inc(lg_step, 1)
            dve.wait_ge(lg_step, 1)
            dve.tensor_tensor(m.lg[:], scores[:, :, 1, :], m.lg[:], ALU.add).then_inc(lg_step, 1)
            dve.wait_ge(lg_step, 2)
            for t in range(T):
                dve.max(m.top[:, t, :], m.lg[:, t, :]).then_inc(lg_step, 1)
            dve.wait_ge(lg_step, T + 2)
            dve.tensor_tensor(m.gate[:], m.lg[:], wide(m.top[:, :, 1:2]), ALU.is_ge).then_inc(exp_ready, 1)
            dve.tensor_tensor(m.lg[:], m.lg[:], wide(m.top[:, :, 0:1]), ALU.subtract).then_inc(lg_step, 1)
            dve.wait_ge(exp_ready, 2)
            dve.tensor_tensor(m.gate[:], m.gate[:], m.pick[:], ALU.mult).then_inc(lg_step, 1)
            dve.wait_ge(lg_step, T + 4)
            dve.tensor_reduce(m.tmp[:, :, 1], m.gate[:], AX_X, ALU.add).then_inc(lg_step, 1)
            dve.wait_ge(lg_step, T + 5)
            dve.reciprocal(m.tmp[:, :, 2], m.tmp[:, :, 1]).then_inc(lg_step, 1)
            dve.wait_ge(lg_step, T + 6)
            dve.tensor_tensor(m.gate[:], m.gate[:], wide(m.tmp[:, :, 2:3]), ALU.mult).then_inc(lg_step, 1)

            def add_out(c):
                dve.wait_ge(down_mm, c + 1)
                dve.tensor_tensor(m.y[:, TB * c:TB * (c + 1), :], m.psum[:, 6 + c % 2, :].rearrange("p (t f) -> p t f", t=TB),
                                  m.x[:, TB * c:TB * (c + 1), :], ALU.add).then_inc(added, 1)

            for c in range(NCH):
                for k in range(FC):
                    n = c * FC + k
                    dve.wait_ge(gelu_done, n + 1)
                    dve.wait_ge(wide_mm, n + 1)
                    dve.tensor_tensor(m.h[:, c % 2, k, :], m.psum[:, 2 + n % 2, :], m.h[:, c % 2, k, :], ALU.mult)\
                        .then_inc(gated, 1)
                if c:
                    add_out(c - 1)
            add_out(NCH - 1)


def store_stage(nc, m, out):
    with ExitStack() as ctx:
        stored = stage_semaphores(nc, ctx, "out")("stored")
        block = ctx.enter_context(nc.Block())

        @block.sync
        def _(sp):
            sp.dma_start(out.rearrange("(t p) f -> p t f", p=P), m.x[:]).then_inc(stored, 16)
            sp.wait_ge(stored, 16)


def bias_rows_stage(nc, m, position, bias_rows):
    n = 3 * H
    with ExitStack() as ctx:
        sem = stage_semaphores(nc, ctx, "position")
        loaded, cut = sem("loaded"), sem("cut")
        block = ctx.enter_context(nc.Block())
        wide = m.nrm[:].rearrange("p t f -> p (t f)")[0:n, 0:S]
        narrow = m.part[0:n, 0, 0, 0:S]

        @block.sync
        def _(sp):
            sp.dma_start(wide, position).then_inc(loaded, 16)
            sp.wait_ge(cut, 1)
            for b in range(NB):
                sp.dma_start(bias_rows[:, b * H:(b + 1) * H, :], narrow).then_inc(loaded, 16)
            sp.wait_ge(loaded, 16 * (1 + NB))

        @block.vector
        def _(dve):
            dve.wait_ge(loaded, 16)
            dve.tensor_copy(narrow, wide).then_inc(cut, 1)


def copy_stage(nc, m, tag):
    with ExitStack() as ctx:
        copied = stage_semaphores(nc, ctx, tag)("copied")
        block = ctx.enter_context(nc.Block())

        @block.vector
        def _(dve):
            dve.tensor_copy(m.y[:], m.x[:]).then_inc(copied, 1)


def build_program(nc, ins, out, stop=None):
    RETIRED.clear()
    with ExitStack() as ctx:
        m = allocate(nc, ctx)
        nc.disable_value_cache = True
        m.experts_w = ins["experts_w"]
        q_stack = nc.dram_tensor("q_stack", [ROW_BIAS, NB * H, S], BF16).ap()
        k_stack = nc.dram_tensor("k_stack", [ROW_BIAS, NB * H, S], BF16).ap()
        bias_rows = nc.dram_tensor("bias_rows", [3, NB * H, S], BF16).ap()

        def attention(a, causal, rows=None):
            project_stage(nc, m, a, ins["attn_w"], q_stack, k_stack)
            attention_stage(nc, m, a, causal, rows, q_stack, k_stack)
            out_project_stage(nc, m, a)

        load_stage(nc, m, ins)
        bias_rows_stage(nc, m, ins["position"], bias_rows)
        norm_stage(nc, m, "n0", m.y, turned=True, ln=0)
        attention(0, False)
        if stop == "a0": return m
        norm_stage(nc, m, "n1", m.y, turned=True, ln=1)
        ffn_bias_stage(nc, m)
        experts_stage(nc, m, "ffn", 1, 0, "all")
        norm_stage(nc, m, "n2", m.x, add=m.y, plain_out=m.x)
        copy_stage(nc, m, "c1")
        if stop == "b1": return m
        for layer in range(2):
            norm_stage(nc, m, f"l{layer}a", m.y, turned=True, ln=2 + 2 * layer)
            attention(1 + layer, True)
            norm_stage(nc, m, f"l{layer}b", m.y, turned=True, ln=3 + 2 * layer)
            gates_stage(nc, m, layer, by_sequence=layer == 1)
            if layer == 0:
                experts_stage(nc, m, "moe0", E, 1, "all")
            else:
                experts_stage(nc, m, "moe1", 2 * NB, 1 + E, "chosen")
            if stop == f"l{layer}": return m
        norm_stage(nc, m, "n3", m.x, add=m.y, plain_out=m.x, turned=True, ln=None)
        copy_stage(nc, m, "c2")
        if stop == "b2": return m
        attention(3, True, bias_rows)
        norm_stage(nc, m, "n4", m.y, plain_out=m.x, turned=True, ln=None)
        if stop == "b3": return m
        tail_stage(nc, m, out)
        norm_stage(nc, m, "n5", m.y, plain_out=m.x)
        store_stage(nc, m, out)



def _layout(x):
    import numpy as np

    a = {k: np.asarray(v) for k, v in x.items()}
    f32 = np.float32

    def heads_last(w):
        return w.reshape(*w.shape[:-1], H, HD).swapaxes(-1, -2).reshape(w.shape)

    def attn(q, k, v, o):
        return np.stack([heads_last(q), heads_last(k), v, o], axis=1)

    w0 = a["L0_attn_in_proj_w"].T
    w3 = a["L1_attn_w_in"].T
    attn_w = [attn(w0[:, 0:D], w0[:, D:2 * D], w0[:, 2 * D:], a["L0_attn_out_w"].T)]
    attn_w += [attn(a["L0_ffn_wq"][l], a["L0_ffn_wk"][l], a["L0_ffn_wv"][l], a["L0_ffn_wo"][l]) for l in range(2)]
    attn_w += [attn(w3[:, 0:D], w3[:, D:2 * D], w3[:, 2 * D:], a["L1_attn_w_out"].T)]
    b0 = a["L0_attn_in_proj_b"]
    zero = np.zeros(D, f32)
    q_b = [b0[0:D], a["L0_ffn_bq"][0], a["L0_ffn_bq"][1], zero]
    k_b = [b0[D:2 * D], a["L0_ffn_bk"][0], a["L0_ffn_bk"][1], zero]
    v_b = [b0[2 * D:], a["L0_ffn_bv"][0], a["L0_ffn_bv"][1], zero]
    o_b = [a["L0_attn_out_b"], a["L0_ffn_bo"][0], a["L0_ffn_bo"][1], zero]
    abcol = np.stack([np.stack([heads_last(q_b[i]), heads_last(k_b[i])], axis=-1) for i in range(4)], axis=1)
    abrow = np.stack([np.stack([v_b[i], o_b[i]]) for i in range(4)])
    lncol = [(a["L0_attn_norm1_w"], a["L0_attn_norm1_b"]), (a["L0_attn_norm2_w"], a["L0_attn_norm2_b"])]
    for l in range(2):
        lncol += [(a["L0_ffn_ln1_w"][l], a["L0_ffn_ln1_b"][l]), (a["L0_ffn_ln2_w"][l], a["L0_ffn_ln2_b"][l])]
    lncol = np.stack([np.stack(p, axis=-1) for p in lncol], axis=1)

    def expert(w1, b1, w2):
        return np.concatenate([w1, b1.reshape(FC, P).T, w2.reshape(FC, P, D).transpose(1, 0, 2).reshape(P, FC * D)], axis=1)

    experts = [expert(a["L0_attn_lin1_w"].T, a["L0_attn_lin1_b"], a["L0_attn_lin2_w"].T)]
    experts += [expert(a["L0_ffn_e_w1"][l, e], a["L0_ffn_e_b1"][l, e], a["L0_ffn_e_w2"][l, e]) for l in range(2) for e in range(E)]
    tail_w = expert(a["L1_ffn_w1"].transpose(1, 0, 2).reshape(D, F), a["L1_ffn_b1"].reshape(F), a["L1_ffn_w2"].reshape(F, D))
    b2 = np.stack([a["L0_ffn_e_b2"][0], a["L0_ffn_e_b2"][1], a["L1_ffn_b2"]], axis=1)

    q, k = np.arange(P)[:, None], np.arange(P)[None, :]
    mask = np.stack([np.where(k > q, -BIG / 3, 0.0), np.where(k < q, -BIG / 3, 0.0)], axis=1).astype(f32)
    slope = (2.0 ** (-8.0 / H * (np.arange(H) + 1.0))).astype(f32).astype(np.float64)
    rest = slope[:, None] * (np.arange(S) - S // 2)[None, :]
    position = []
    for _ in range(3):
        bits = rest.astype(f32).view(np.uint32)
        cut = (((bits.astype(np.uint64) + 0x8000) & 0xFFFF0000).astype(np.uint32)).view(f32)
        position.append(cut)
        rest = rest - cut
    expand = (np.arange(F)[None, :] // (F // E) == np.arange(E)[:, None]).astype(f32)
    arrays = {
        "x": a["L0_attn_x"].reshape(TOK, D), "attn_w": np.stack(attn_w), "abcol": abcol, "abrow": abrow, "lncol": lncol,
        "experts_w": np.stack(experts), "tail_w": tail_w, "b2": b2, "b2ffn": a["L0_attn_lin2_b"],
        "gate_w": a["L0_ffn_gate_w"].transpose(1, 0, 2), "gate_b": a["L0_ffn_gate_b"],
        "centroids": a["L1_ffn_centroids"], "route_w": a["L1_ffn_w_route"].T,
        "ident": np.eye(P, dtype=f32), "mask": mask, "iota8": np.arange(E, dtype=f32),
        "position": np.stack(position).reshape(3 * H, S), "expand": expand,
    }
    return {n: np.ascontiguousarray(v) for n, v in arrays.items()}


def kernel(**inputs):
    import concourse.bacc as _bacc
    from concourse.bass_utils import run_bass_kernel_spmd as _run

    nc = _bacc.Bacc("TRN2", target_bir_lowering=False, num_devices=1)
    arrays = {f"in_{n}": v for n, v in _layout(inputs).items()}
    ins = {n[3:]: nc.dram_tensor(n, v.shape, mybir.dt.from_np(v.dtype), kind="ExternalInput").ap() for n, v in arrays.items()}
    out = nc.dram_tensor("out_0", (TOK, D), F32, kind="ExternalOutput").ap()
    build_program(nc, ins, out)
    r = _run(nc, [arrays], core_ids=[0])
    return r.results[0]["out_0"].reshape(NB, S, D)
```

```python
from contextlib import ExitStack

import concourse.bass as bass
from concourse import mybir

F32 = mybir.dt.float32
BF16 = mybir.dt.bfloat16
U32 = mybir.dt.uint32
ALU = mybir.AluOpType
ACT = mybir.ActivationFunctionType
AX_X = mybir.AxisListType.X

P = 128
NB, S, D = 2, 1024, 128
H, HD = 16, 8
TOK = NB * S
T = TOK // P
BANK = 512
TB = BANK // P
NCH = TOK // BANK
QT = S // P
G = 4
NG = NB * H // G
GW = G * HD
HG = H // G
E = 8
F = 512
FC = F // P
WCOLS = F + FC + FC * D
EPS = 1e-5
BIG = 3.0e38

Q_PART = [0, 0, 0, 1, 1, 1, 2, 2]
K_PART = [0, 1, 2, 0, 1, 2, 0, 1]
TERMS = len(Q_PART)
ROW_BIAS = TERMS * HD
ROW_MAX = P - 3
VW = HD + 1


class Memory:
    pass


def allocate(nc, ctx):
    m = Memory()

    def sb(name, shape, dt=F32):
        return ctx.enter_context(nc.sbuf_tensor(name, shape, dt))

    m.psum = ctx.enter_context(nc.psum_tensor("psum", [P, 8, BANK], F32))
    m.x = sb("x_outer", [P, T, D])
    m.y = sb("y_inner", [P, T, D])
    m.nrm = sb("normalized", [P, T, D])
    m.stats = sb("stats", [P, T, 6])
    m.meanvar = sb("meanvar", [P, T, 2])
    m.std = sb("std", [P, T])
    m.rstd = sb("rstd", [P, T])
    m.xT = sb("xT", [P, TOK])
    m.ident = sb("ident", [P, P])
    m.identb = sb("identb", [P, P], BF16)
    m.mask = sb("mask", [P, 2, P])
    m.maskb = sb("maskb", [P, 2, P], BF16)
    m.zero = sb("zero", [P, 1])
    m.iota8 = sb("iota8", [P, E])
    m.lncol = sb("lncol", [P, 6, 2])
    m.aw = sb("attn_w", [P, 4, D])
    m.abcol = sb("attn_bias_cols", [P, 4, 2])
    m.abrow = sb("attn_bias_rows", [P, 4, 2, D])
    m.qbias = sb("scaled_q_bias", [P, 4])
    m.part = sb("qk_parts", [P, 2, 3, TOK], BF16)
    m.full = sb("qk_full", [P, 2, 2, BANK])
    m.rest = sb("qk_rest", [P, 2, 2, BANK])
    m.v = sb("v_all", [P, NG, QT, G * VW])
    m.vst = sb("v_stage", [P, 3, QT, G * VW])
    m.qs = sb("q_slots", [P, 3, 2, G, BANK], BF16)
    m.ks = sb("k_slots", [P, 3, G, S], BF16)
    m.prob = sb("prob", [P, 4, 2, BANK])
    m.outT = sb("outT", [P, 2, BANK])
    m.rsum = sb("row_sum_inverse", [P, 2, TB, G])
    m.ctx = sb("ctx_all", [P, T, D])
    m.mx = sb("chunk_max", [P, G, QT, 2])
    m.negm = sb("neg_max", [P, 2, G * TB])
    m.negr = sb("neg_max_rest", [P, 2, G * TB])
    m.negp = sb("neg_max_parts", [P, 2, 3, G * TB], BF16)
    m.maxT = sb("neg_max_turned", [3 * G * TB, P], BF16)
    m.wring = sb("expert_w", [P, 2, WCOLS])
    m.h = m.prob[:].rearrange("p s c n -> p (s c) n").rearrange("p (u k) n -> p u k n", u=2)
    m.gate_w = sb("gate_w", [P, 2, E])
    m.gate_b = sb("gate_b", [P, 2, E])
    m.b2 = sb("b2", [E, 3, D])
    m.b2ffn = sb("b2_ffn", [P, D])
    m.lg = sb("logits", [P, T, E])
    m.top = sb("top8", [P, T, 8])
    m.idx = sb("top8_index", [P, T, 8], U32)
    m.idxf = sb("top8_index_f", [P, T, 8])
    m.pick = sb("pick", [P, T, E])
    m.gate = sb("gates", [P, T, E])
    m.sel = sb("selected_weights", [P, T, 2])
    m.tmp = sb("gate_tmp", [P, T, 4])
    m.gT = sb("gatesT", [E, T, P])
    m.msum = sb("token_mean", [P, NB])
    m.mrep = sb("token_mean_rep", [P, NB, P])
    m.tail_w = sb("tail_w", [P, WCOLS])
    m.cent = sb("centroids", [E, D])
    m.cscr = sb("centroid_scratch", [E, D])
    m.cn = sb("centroid_norm", [E, 4])
    m.route = sb("route_w", [P, 2 * E])
    m.expand = sb("expand", [E, F])
    return m


STAGE_SEMAPHORES = 16


def stage_semaphores(nc, ctx, tag):
    if nc.free_len() < STAGE_SEMAPHORES:
        nc.clear_and_free_semaphores(RETIRED)
        RETIRED.clear()
        nc.all_engine_barrier()
    made = []

    def sem(name):
        made.append(nc.alloc_semaphore(f"{tag}_{name}"))
        return made[-1]

    ctx.callback(lambda: RETIRED.extend(made))
    return sem


RETIRED = []


def broadcast_rows(row, n=P):
    return row.partition_broadcast(n)


def load_stage(nc, m, ins):
    with ExitStack() as ctx:
        sem = stage_semaphores(nc, ctx, "shared")
        loaded, made, built = sem("loaded"), sem("made"), sem("built")
        block = ctx.enter_context(nc.Block())

        @block.sync
        def _(sp):
            sp.dma_start(m.x[:], ins["x"].rearrange("(t p) f -> p t f", p=P)).then_inc(loaded, 16)
            sp.dma_start(m.ident[:], ins["ident"]).then_inc(loaded, 16)
            sp.dma_start(m.mask[:], ins["mask"]).then_inc(loaded, 16)
            sp.dma_start(m.lncol[:], ins["lncol"]).then_inc(loaded, 16)
            sp.dma_start(m.abcol[:], ins["abcol"]).then_inc(loaded, 16)
            sp.dma_start(m.abrow[:], broadcast_rows(ins["abrow"])).then_inc(loaded, 16)
            sp.dma_start(m.gate_w[:], ins["gate_w"]).then_inc(loaded, 16)
            sp.dma_start(m.gate_b[:], broadcast_rows(ins["gate_b"])).then_inc(loaded, 16)
            sp.dma_start(m.iota8[:], broadcast_rows(ins["iota8"])).then_inc(loaded, 16)
            sp.dma_start(m.b2[:], ins["b2"]).then_inc(loaded, 16)
            sp.dma_start(m.b2ffn[:], broadcast_rows(ins["b2ffn"])).then_inc(loaded, 16)
            sp.dma_start(m.tail_w[:], ins["tail_w"]).then_inc(loaded, 16)
            sp.dma_start(m.cent[:], ins["centroids"]).then_inc(loaded, 16)
            sp.dma_start(m.route[:, E:2 * E], ins["route_w"]).then_inc(loaded, 16)
            sp.dma_start(m.expand[:], ins["expand"]).then_inc(loaded, 16)
            sp.wait_ge(loaded, 15 * 16)

        @block.gpsimd
        def _(pool):
            for n, (buffer, value) in enumerate(((m.qs[64:96], 1.0), (m.qs[96:128], 0.0))):
                if n:
                    pool.wait_ge(made, n)
                pool.memset(buffer, value).then_inc(made, 1)

        @block.vector
        def _(dve):
            dve.memset(m.ks[64:96], 0.0).then_inc(built, 1)
            dve.memset(m.ks[96:128], 1.0).then_inc(built, 1)
            v = m.v[:].rearrange("p g t (j w) -> p (g t j) w", w=VW)
            dve.memset(v[:, :, HD:VW], 1.0).then_inc(built, 1)
            dve.memset(m.zero[:], 0.0).then_inc(built, 1)
            dve.wait_ge(loaded, 15 * 16)
            dve.tensor_copy(m.identb[:], m.ident[:]).then_inc(built, 1)
            dve.tensor_copy(m.maskb[:], m.mask[:]).then_inc(built, 1)
            dve.tensor_scalar(m.qbias[:], m.abcol[:, :, 0], float(HD) ** -0.5, None, ALU.mult).then_inc(built, 1)
            dve.tensor_copy(m.y[:], m.x[:]).then_inc(built, 1)
            dve.wait_ge(built, 8)
            dve.wait_ge(made, 2)


def norm_stage(nc, m, tag, src, turned=False, ln=0, add=None, plain_out=None):
    dst = plain_out if plain_out is not None else m.nrm
    work = m.y if add is not None else src
    with ExitStack() as ctx:
        sem = stage_semaphores(nc, ctx, f"{tag}")
        summed, measured, aggregated, var_ready = sem("summed"), sem("measured"), sem("aggregated"), sem("var_ready")
        std_ready, rstd_ready = sem("std_ready"), sem("rstd_ready")
        normalized, turned_sem, evacuated = sem("normalized"), sem("turned"), sem("evacuated")
        block = ctx.enter_context(nc.Block())

        @block.vector
        def _(dve):
            if add is not None:
                for c in range(NCH):
                    dve.tensor_tensor(work[:, TB * c:TB * (c + 1), :], src[:, TB * c:TB * (c + 1), :],
                                      add[:, TB * c:TB * (c + 1), :], ALU.add).then_inc(summed, 1)
            for t in range(T):
                if add is not None:
                    dve.wait_ge(summed, t // TB + 1)
                dve.bn_stats(m.stats[:, t, :], work[:, t, :]).then_inc(measured, 1)
            for t in range(T):
                dve.wait_ge(measured, t + 1)
                dve.bn_aggr(m.meanvar[:, t, :], m.stats[:, t, :]).then_inc(aggregated, 1)
            dve.wait_ge(aggregated, T)
            dve.tensor_scalar(m.std[:], m.meanvar[:, :, 1], EPS, None, ALU.add).then_inc(var_ready, 1)
            dve.wait_ge(std_ready, 1)
            dve.reciprocal(m.rstd[:], m.std[:]).then_inc(rstd_ready, 1)
            dve.wait_ge(rstd_ready, 1)
            for t in range(T):
                dve.tensor_scalar(dst[:, t, :], work[:, t, :], m.meanvar[:, t, 0:1], m.rstd[:, t:t + 1],
                                  ALU.subtract, ALU.mult).then_inc(normalized, 1)

        @block.scalar
        def _(act):
            act.wait_ge(var_ready, 1)
            act.activation(m.std[:], m.std[:], ACT.Sqrt).then_inc(std_ready, 1)
            if turned:
                for c in range(NCH):
                    act.wait_ge(turned_sem, c + 1)
                    out = m.xT[:, BANK * c:BANK * (c + 1)]
                    if ln is None:
                        act.activation(out, m.psum[:, c, :], ACT.Copy).then_inc(evacuated, 1)
                    else:
                        act.activation(out, m.psum[:, c, :], ACT.Identity, bias=m.lncol[:, ln, 1:2],
                                       scale=m.lncol[:, ln, 0:1]).then_inc(evacuated, 1)

        if turned:
            @block.tensor
            def _(pe):
                for t in range(T):
                    pe.wait_ge(normalized, t + 1)
                    ins = pe.transpose(m.psum[:, t // TB, P * (t % TB):P * (t % TB + 1)], dst[:, t, :], m.ident[:])
                    if t % TB == TB - 1:
                        ins.then_inc(turned_sem, 1)


def project_stage(nc, m, a, attn_w):
    with ExitStack() as ctx:
        sem = stage_semaphores(nc, ctx, f"proj{a}")
        w_loaded, qk_mm, v_mm = sem("w_loaded"), sem("qk_mm"), sem("v_mm")
        full_ready, hi_ready, rest_ready, mid_ready = sem("full_ready"), sem("hi_ready"), sem("rest_ready"), sem("mid_ready")
        lo_ready, v_ready = sem("lo_ready"), sem("v_ready")
        block = ctx.enter_context(nc.Block())
        parts = lambda s, part, c: m.part[:, s, part, BANK * c:BANK * (c + 1)]

        @block.sync
        def _(sp):
            sp.dma_start(m.aw[:], attn_w[a]).then_inc(w_loaded, 16)

        @block.tensor
        def _(pe):
            pe.wait_ge(w_loaded, 16)
            for c in range(NCH):
                for s in range(2):
                    if c >= 2:
                        pe.wait_ge(hi_ready, 2 * (c - 2) + s + 1)
                    pe.matmul(m.psum[:, 2 * (c % 2) + s, :], m.aw[:, s, :], m.xT[:, BANK * c:BANK * (c + 1)],
                              start=True, stop=True).then_inc(qk_mm, 1)
                if c >= 2:
                    pe.wait_ge(v_ready, c - 1)
                for t in range(TB):
                    tok = BANK * c + P * t
                    ins = pe.matmul(m.psum[:, 4 + c % 2, P * t:P * (t + 1)], m.xT[:, tok:tok + P], m.aw[:, 2, :],
                                    start=True, stop=True)
                ins.then_inc(v_mm, 1)

        @block.scalar
        def _(act):
            for n in range(2 * NCH):
                c, s = n // 2, n % 2
                act.wait_ge(qk_mm, n + 1)
                if n >= 4:
                    act.wait_ge(rest_ready, n - 3)
                bias = m.qbias[:, a:a + 1] if s == 0 else m.abcol[:, a, 1:2]
                scale = float(HD) ** -0.5 if s == 0 else 1.0
                act.activation(m.full[:, s, c % 2, :], m.psum[:, 2 * (c % 2) + s, :], ACT.Identity, bias=bias,
                               scale=scale).then_inc(full_ready, 1)
                act.activation(parts(s, 0, c), m.psum[:, 2 * (c % 2) + s, :], ACT.Identity, bias=bias,
                               scale=scale).then_inc(hi_ready, 1)

        @block.vector
        def _(dve):
            for n in range(2 * NCH):
                c, s = n // 2, n % 2
                dve.wait_ge(full_ready, n + 1)
                dve.wait_ge(hi_ready, n + 1)
                if n >= 4:
                    dve.wait_ge(lo_ready, n - 3)
                dve.tensor_tensor(m.rest[:, s, c % 2, :], m.full[:, s, c % 2, :], parts(s, 0, c),
                                  ALU.subtract).then_inc(rest_ready, 1)
                dve.wait_ge(rest_ready, n + 1)
                dve.tensor_copy(parts(s, 1, c), m.rest[:, s, c % 2, :]).then_inc(mid_ready, 1)
                if s == 1:
                    dve.wait_ge(v_mm, c + 1)
                    b, kt = c // (NCH // NB), TB * (c % (NCH // NB))
                    val = m.psum[:, 4 + c % 2, :].rearrange("p (t g j w) -> p t g j w", t=TB, g=HG, j=G)
                    for t in range(TB):
                        out = m.v[:, b * HG:(b + 1) * HG, kt + t, :].rearrange("p g (j w) -> p g j w", j=G)[:, :, :, 0:HD]
                        ins = dve.tensor_tensor(out, val[:, t],
                                                m.abrow[:, a, 0, :].rearrange("p (g j w) -> p g j w", g=HG, j=G), ALU.add)
                    ins.then_inc(v_ready, 1)

        @block.gpsimd
        def _(pool):
            for n in range(2 * NCH):
                c, s = n // 2, n % 2
                pool.wait_ge(mid_ready, n + 1)
                pool.tensor_tensor(parts(s, 2, c), m.rest[:, s, c % 2, :], parts(s, 1, c),
                                   ALU.subtract).then_inc(lo_ready, 1)


def attention_stage(nc, m, a, causal, bias_rows):
    RING = 3
    halves = [[kt for kt in range(QT) if not causal or kt < TB * (hf + 1)] for hf in range(2)]
    units = [(hf, kt) for hf in range(2) for kt in reversed(halves[hf])]
    U = len(units)
    first_q = lambda u: max(units[u][0] * BANK, units[u][1] * P) if causal else units[u][0] * BANK
    width = lambda u: BANK * (units[u][0] + 1) - first_q(u)
    last_of_half = [len(halves[0]) - 1, U - 1]
    rows = [[], []]
    for hf in range(2):
        for qt in range(TB * hf, TB * (hf + 1)):
            for k0 in (0, BANK):
                keys = min(S if not causal else P * (qt + 1), k0 + BANK) - k0
                together = max(BANK // keys, 1) if keys > 0 else 0
                if keys > 0:
                    rows[hf] += [(range(j, j + together), qt, k0, keys) for j in range(0, G, together)]

    def plan(next_group, this_group, last_group):
        others = []
        if this_group:
            for u in range(U):
                others += [(("col", u, p), 0.9 * width(u)) for p in range(2)]
                if u:
                    others.append((("pv", u - 1, 0), 1.8 * width(u - 1)))
                if u == 0:
                    if last_group:
                        others.append((("pv", U - 1, 1), 1.8 * BANK))
                    others.append((("turn_max", 1, 0), 100))
                if u == 1 and last_group:
                    others.append((("turn", 1, 1), 2 * BANK))
                if u == last_of_half[0] + 3:
                    others.append((("turn", 0, 0), 2 * BANK))
        elif last_group:
            others += [(("pv", U - 1, 1), 1), (("turn", 1, 1), 1)]
        spread = []
        if next_group:
            for hf in range(2):
                for n, r in enumerate(rows[hf]):
                    spread.append((("row", r), 65 + 1.04 * len(r[0]) * r[3]))
                    if hf == 1 and n == 3:
                        spread.append((("turn_max", 0, 1), 100))
                spread.append((("negate", hf), 200))
        if not others or not spread:
            return [s for s, _ in others + spread]
        steps, done, rows_done = [], 0.0, 0.0
        total, rows_total = sum(w for _, w in others), sum(w for _, w in spread)
        for s, w in others:
            steps.append(s)
            done += w
            while spread and rows_done / rows_total < done / total:
                steps.append(spread[0][0])
                rows_done += spread.pop(0)[1]
        return steps + [s for s, _ in spread]

    in_ring = lambda s: s[0] in ("row", "turn", "turn_max")
    ring_len = lambda steps: sum(in_ring(s) for s in steps)
    first, body0, body = plan(True, False, False), plan(True, True, False), plan(True, True, True)
    last, tail = plan(False, True, True), plan(False, False, True)
    SLOTS = 3
    assert (NG - 2) % SLOTS == 0 and SLOTS % RING == 0

    def program(eng, run):
        run(first, -1, 0, 0)
        run(body0, 0, 0, ring_len(first))
        base = ring_len(first) + ring_len(body0)
        with eng.Fori(0, (NG - 2) // SLOTS) as i:
            for k in range(SLOTS):
                run(body, 1 + k, i, base + k * ring_len(body))
        base += (NG - 2) * ring_len(body)
        run(last, NG - 1, 0, base)
        run(tail, NG, 0, base + ring_len(last))

    with ExitStack() as ctx:
        sem = stage_semaphores(nc, ctx, f"attn{a}")
        stacks_loaded, max_loaded = sem("stacks_loaded"), sem("max_loaded")
        ring_full, ring_free = sem("ring_full"), sem("ring_free")
        col_full, prob_full = sem("col_full"), sem("prob_full")
        pv_done, out_copied, inverted = sem("pv_done"), sem("out_copied"), sem("inverted")
        cleared, v_staged, neg_made, neg_step, neg_split = sem("cleared"), sem("v_staged"), sem("neg_made"), sem("neg_step"), sem("neg_split")
        block = ctx.enter_context(nc.Block())
        STACK_DMAS = 3 * TERMS + (1 if bias_rows is not None else 0)
        MAX_LOAD = 3 * 16
        OUT = 7
        HH = G * TB

        CRED_RING, CRED_COL, CRED_PV, CRED_OUT, CRED_TURN = RING, 2, 2, 1, 2
        col_bank = lambda u, p: RING + 2 * p

        def of_group(g, i):
            return lambda n, x: i * (SLOTS * n) + (g * n + x)

        def ring_at(steps, count, i):
            return lambda x: i * (SLOTS * ring_len(body)) + (count + x)

        max_at = lambda steps, hf: ring_len(steps[:[s[:2] for s in steps].index(("turn_max", hf))]) + 1

        @block.sync
        def _(sp):
            def load(g):
                slot = bass.ds((g % SLOTS) * G, G)
                qs, ks = m.qs[:].rearrange("p s h j t -> p (s h j) t"), m.ks[:].rearrange("p s j t -> p (s j) t")
                b, rows32 = g // HG, slice((g % HG) * GW, (g % HG + 1) * GW)
                for t in range(TERMS):
                    rows = slice(t * HD, (t + 1) * HD)
                    for hf in range(2):
                        sp.dma_start(qs[rows, bass.ds((g % SLOTS) * (2 * G) + hf * G, G), :],
                                     m.part[rows32, 0, Q_PART[t], bass.ds(b * S + hf * BANK, BANK)]).then_inc(stacks_loaded, 16)
                    sp.dma_start(ks[rows, slot, :], m.part[rows32, 1, K_PART[t], bass.ds(b * S, S)]).then_inc(stacks_loaded, 16)
                if bias_rows is not None:
                    sp.dma_start(ks[ROW_BIAS:ROW_BIAS + 3, slot, :], bias_rows[:, bass.ds((g % HG) * G, G), :])\
                        .then_inc(stacks_loaded, 16)

            def load_max(g, hf, turned):
                sp.wait_ge(ring_free, turned)
                if g or hf:
                    sp.wait_ge(max_loaded, g * (2 * MAX_LOAD) + hf * MAX_LOAD)
                qs = m.qs[:].rearrange("p s h j t -> p (s h) (j t)")
                for part in range(3):
                    sp.dma_start(qs[ROW_MAX + part:ROW_MAX + part + 1, bass.ds((g % SLOTS) * 2 + hf, 1), :],
                                 m.maxT[HH * part:HH * (part + 1), :]).then_inc(max_loaded, 16)

            n = ring_len(body)
            base = CRED_RING + ring_len(first)
            for g in range(SLOTS):
                load(g)
                sp.wait_ge(stacks_loaded, 16 * STACK_DMAS * (g + 1))
                if g == 0:
                    load_max(0, 0, CRED_RING + max_at(first, 0))
            load_max(0, 1, base + max_at(body0, 1))
            load_max(1, 0, base + max_at(body0, 0))
            base += ring_len(body0)
            load_max(1, 1, base + max_at(body, 1))
            for g in range(1, NG - 2):
                sp.wait_ge(pv_done, g * U + CRED_PV)
                load(g + 2)
                load_max(g + 1, 0, g * n + (base - n + max_at(body, 0)))
                sp.wait_ge(stacks_loaded, g * (16 * STACK_DMAS) + SLOTS * 16 * STACK_DMAS)
                load_max(g + 1, 1, g * n + (base + max_at(body, 1)))
            load_max(NG - 1, 0, base + n * (NG - 3) + max_at(body, 0))
            load_max(NG - 1, 1, base + n * (NG - 2) + max_at(last, 1))
            sp.wait_ge(max_loaded, 2 * MAX_LOAD * NG)

        @block.gpsimd
        def _(pool):
            def copy(out, x):
                return pool.tensor_tensor(out, x, m.zero[:].to_broadcast(x.shape), ALU.subtract)

            def group(g, slot_used):
                if slot_used is not None:
                    pool.wait_ge(pv_done, slot_used)
                v = m.v[:].rearrange("p g t c -> p (g t c)")[:, bass.ds(g * (QT * G * VW), QT * G * VW)]
                vst = m.vst[:].rearrange("p s t c -> p (s t c)")[:, bass.ds((g % SLOTS) * (QT * G * VW), QT * G * VW)]
                copy(vst, v).then_inc(v_staged, 1)
                for hf in range(2):
                    pool.wait_ge(neg_made, g * 2 + (hf + 1))
                    if slot_used is not None:
                        pool.wait_ge(max_loaded, g * (2 * MAX_LOAD) + (hf - 1) * MAX_LOAD)
                    elif g > 0:
                        pool.wait_ge(max_loaded, (2 * g + hf - 1) * MAX_LOAD)
                    parts, negm, negr = m.negp[:, hf], m.negm[:, hf], m.negr[:, hf]
                    copy(parts[:, 0], negm).then_inc(neg_step, 1)
                    pool.wait_ge(neg_step, g * 6 + (3 * hf + 1))
                    pool.tensor_tensor(negr, negm, parts[:, 0], ALU.subtract).then_inc(neg_step, 1)
                    pool.wait_ge(neg_step, g * 6 + (3 * hf + 2))
                    copy(parts[:, 1], negr).then_inc(neg_step, 1)
                    pool.wait_ge(neg_step, g * 6 + (3 * hf + 3))
                    pool.tensor_tensor(parts[:, 2], negr, parts[:, 1], ALU.subtract).then_inc(neg_split, 1)

            for g in range(SLOTS):
                group(g, None)
            with pool.Fori(SLOTS, NG) as g:
                group(g, g * U + (CRED_PV - (SLOTS - 1) * U))

        @block.tensor
        def _(pe):
            def run(steps, g, i, count):
                at, ring = of_group(g, i), ring_at(steps, count, i)
                this_slot, next_slot, next_at = g % SLOTS, (g + 1) % SLOTS, of_group(g + 1, i)
                n = 0
                for step in steps:
                    kind = step[0]
                    if in_ring(step):
                        pe.wait_ge(ring_free, ring(n + 1))
                        bank = (count + n) % RING
                        n += 1
                    if kind == "row":
                        heads, qt, k0, keys = step[1]
                        if qt == 0 and k0 == 0 and heads[0] == 0:
                            pe.wait_ge(stacks_loaded, next_at(16 * STACK_DMAS, 16 * STACK_DMAS))
                        diagonal = causal and k0 + keys == P * (qt + 1)
                        for h, j in enumerate(heads):
                            out = m.psum[:, bank, h * keys:(h + 1) * keys]
                            ins = pe.matmul(out, m.qs[0:ROW_MAX, next_slot, qt // TB, j, P * (qt % TB):P * (qt % TB + 1)],
                                            m.ks[0:ROW_MAX, next_slot, j, k0:k0 + keys], start=True, stop=not diagonal)
                            if diagonal:
                                ins = pe.matmul(out[:, keys - P:keys], m.identb[:], m.maskb[:, 0, :], start=False, stop=True)
                        ins.then_inc(ring_full, 1)
                    elif kind == "turn_max":
                        hf, ahead = step[1:]
                        pe.wait_ge(neg_split, (next_at if ahead else at)(2, hf + 1))
                        pe.matmul(m.psum[0:3 * HH, bank, 0:P], m.negp[:, hf].rearrange("p a b -> p (a b)"), m.identb[:],
                                  start=True, stop=True).then_inc(ring_full, 1)
                    elif kind == "turn":
                        hf, back = step[1:]
                        pe.wait_ge(out_copied, at(2, hf + 1 + CRED_OUT - 2 * back))
                        for k in range(TB):
                            ins = pe.transpose(m.psum[:, bank, P * k:P * (k + 1)], m.outT[:, hf, P * k:P * (k + 1)], m.ident[:])
                        ins.then_inc(ring_full, 1)
                    elif kind == "col":
                        u, p = step[1:]
                        hf, kt = units[u]
                        q0 = first_q(u)
                        if p == 0 and u in (0, last_of_half[0] + 1):
                            pe.wait_ge(max_loaded, at(2 * MAX_LOAD, MAX_LOAD * (hf + 1)))
                        pe.wait_ge(prob_full, at(2 * U, 2 * u + p + 1))
                        diagonal = causal and kt >= TB * hf
                        for jj in range(2):
                            out = m.psum[:, col_bank(u, p) + jj, q0 - BANK * hf:BANK]
                            ins = pe.matmul(out, m.ks[:, this_slot, 2 * p + jj, P * kt:P * (kt + 1)],
                                            m.qs[:, this_slot, hf, 2 * p + jj, q0 - BANK * hf:BANK], start=True, stop=not diagonal)
                            if diagonal:
                                ins = pe.matmul(out[:, 0:P], m.identb[:], m.maskb[:, 1, :], start=False, stop=True)
                        ins.then_inc(col_full, 1)
                    elif kind == "pv":
                        u, back = step[1:]
                        hf, kt = units[u]
                        off = first_q(u) - BANK * hf
                        begins = kt == halves[hf][-1]
                        if u == 0:
                            pe.wait_ge(v_staged, at(1, 1))
                        if begins:
                            pe.wait_ge(out_copied, at(2, hf + 1 - 2 * back))
                        pe.wait_ge(prob_full, at(2 * U, 2 * u + 2 + CRED_COL - 2 * U * back))
                        for j in range(G):
                            ins = pe.matmul(m.psum[32 * j:32 * j + VW, OUT, off:BANK],
                                            m.vst[:, (g - back) % SLOTS, kt, VW * j:VW * (j + 1)],
                                            m.prob[:, (2 * u + j // 2) % 4, j % 2, off:BANK],
                                            start=begins, stop=kt == 0, skip_group_check=True)
                        ins.then_inc(pv_done, 1)

            pe.wait_ge(cleared, 2)
            program(pe, run)

        @block.scalar
        def _(act):
            act.sem_inc(prob_full, CRED_COL)
            act.sem_inc(out_copied, CRED_OUT)

            def run(steps, g, i, count):
                at = of_group(g, i)
                for step in steps:
                    if step[0] == "col":
                        u, p = step[1:]
                        off = first_q(u) - BANK * units[u][0]
                        if p == 0:
                            act.wait_ge(pv_done, at(U, u + 1))
                        act.wait_ge(col_full, at(2 * U, 2 * u + p + 1))
                        b = col_bank(u, p)
                        act.activation(m.prob[:, (2 * u + p) % 4, :, off:BANK], m.psum[:, b:b + 2, off:BANK],
                                       ACT.Exp).then_inc(prob_full, 1)
                    elif step[0] == "pv" and step[1] in last_of_half:
                        u, back = step[1:]
                        hf = last_of_half.index(u)
                        act.wait_ge(pv_done, at(U, u + 1 + CRED_PV - U * back))
                        act.wait_ge(inverted, at(2, hf + 1 - 2 * back))
                        act.copy(m.outT[:, hf, :], m.psum[:, OUT, :]).then_inc(out_copied, 1)

            program(act, run)

        @block.vector
        def _(dve):
            dve.sem_inc(ring_free, CRED_RING)
            dve.sem_inc(pv_done, CRED_PV)
            dve.sem_inc(inverted, CRED_TURN)
            dve.memset(m.mx[:], -BIG).then_inc(cleared, 1)
            dve.memset(m.psum[:, OUT, :], 0.0).then_inc(cleared, 1)
            dve.wait_ge(cleared, 2)

            def run(steps, g, i, count):
                at, next_at, ring = of_group(g, i), of_group(g + 1, i), ring_at(steps, count, i)
                n = 0
                for step in steps:
                    kind = step[0]
                    if in_ring(step):
                        bank = (count + n) % RING
                        n += 1
                    if kind == "row":
                        heads, qt, k0, keys = step[1]
                        scores = m.psum[:, bank, 0:len(heads) * keys].rearrange("p (j k) -> p j k", k=keys)
                        dve.wait_ge(ring_full, ring(n))
                        dve.reduce_max(m.mx[:, heads[0]:heads[0] + len(heads), qt, k0 // BANK], scores, AX_X)\
                            .then_inc(ring_free, 1)
                    elif kind == "negate":
                        hf = step[1]
                        dve.wait_ge(ring_free, ring(n + CRED_RING))
                        if not (g == -1 and isinstance(i, int)):
                            dve.wait_ge(neg_split, next_at(2, hf - 1))
                        dve.tensor_reduce(m.negm[:, hf].rearrange("p (j t) -> p j t", j=G),
                                          m.mx[:, :, TB * hf:TB * (hf + 1), :], AX_X, ALU.max, negate=True)\
                            .then_inc(neg_made, 1)
                    elif kind == "turn_max":
                        hf, ahead = step[1:]
                        before = (next_at if ahead else at)(2 * MAX_LOAD, hf * MAX_LOAD)
                        dve.wait_ge(ring_full, ring(n))
                        if not (isinstance(before, int) and before == 0):
                            dve.wait_ge(max_loaded, before)
                        dve.tensor_copy(m.maxT[:], m.psum[0:3 * HH, bank, 0:P]).then_inc(ring_free, 1)
                    elif kind == "turn":
                        hf, back = step[1:]
                        sums = m.psum[:, bank, :].rearrange("p (t j w) -> p t j w", t=TB, j=G)
                        dve.wait_ge(ring_full, ring(n))
                        inv = m.rsum[:, hf]
                        dve.reciprocal(inv, sums[:, :, :, HD]).then_inc(inverted, 1)
                        dve.wait_ge(inverted, at(2, hf + 1 + CRED_TURN - 2 * back))
                        group = i * SLOTS + (g - back)
                        out = m.ctx[:].rearrange("p t (g j w) -> p t g j w", g=HG, j=G)
                        out = out[:, bass.ds(group // HG * QT + hf * TB, TB), bass.ds(group % HG, 1), :, :]
                        out = out.rearrange("p t g j w -> p t (g j) w")
                        dve.tensor_tensor(out, sums[:, :, :, 0:HD], inv.unsqueeze(3).to_broadcast([P, TB, G, HD]),
                                          ALU.mult).then_inc(ring_free, 1)

            program(dve, run)


def out_project_stage(nc, m, a):
    with ExitStack() as ctx:
        sem = stage_semaphores(nc, ctx, f"out{a}")
        turned, copied, projected, biased, added = sem("turned"), sem("copied"), sem("projected"), sem("biased"), sem("added")
        block = ctx.enter_context(nc.Block())
        ctxT = m.nrm[:].rearrange("p t f -> p (t f)")

        @block.tensor
        def _(pe):
            def project(c):
                pe.wait_ge(copied, c + 1)
                for k in range(TB):
                    col = BANK * c + P * k
                    ins = pe.matmul(m.psum[:, 4 + c, P * k:P * (k + 1)], ctxT[:, col:col + P], m.aw[:, 3, :],
                                    start=True, stop=True)
                ins.then_inc(projected, 1)

            for c in range(NCH):
                for k in range(TB):
                    ins = pe.transpose(m.psum[:, c, P * k:P * (k + 1)], m.ctx[:, TB * c + k, :], m.ident[:])
                ins.then_inc(turned, 1)
                if c:
                    project(c - 1)
            project(NCH - 1)

        @block.scalar
        def _(act):
            for c in range(NCH):
                act.wait_ge(turned, c + 1)
                act.copy(ctxT[:, BANK * c:BANK * (c + 1)], m.psum[:, c, :]).then_inc(copied, 1)

        @block.vector
        def _(dve):
            bias = m.abrow[:, a, 1, :].unsqueeze(1).to_broadcast([P, TB, D])
            for c in range(NCH):
                y = m.y[:, TB * c:TB * (c + 1), :]
                dve.tensor_tensor(y, y, bias, ALU.add).then_inc(biased, 1)
            for c in range(NCH):
                y = m.y[:, TB * c:TB * (c + 1), :]
                dve.wait_ge(projected, c + 1)
                dve.wait_ge(biased, c + 1)
                dve.tensor_tensor(y, m.psum[:, 4 + c, :].rearrange("p (t f) -> p t f", t=TB), y, ALU.add).then_inc(added, 1)


def ffn_bias_stage(nc, m):
    with ExitStack() as ctx:
        biased = stage_semaphores(nc, ctx, "ffn")("biased")
        block = ctx.enter_context(nc.Block())

        @block.vector
        def _(dve):
            dve.memset(m.gate[:], 1.0).then_inc(biased, 1)
            for c in range(NCH):
                y = m.y[:, TB * c:TB * (c + 1), :]
                dve.tensor_tensor(y, y, m.b2ffn[:].unsqueeze(1).to_broadcast([P, TB, D]), ALU.add).then_inc(biased, 1)


def top_two(dve, act, m, n, step, e2_ready):
    if act is not None:
        act.wait_ge(step, 2 * n + 1)
        act.activation(m.tmp[:, 0:n, 1], m.tmp[:, 0:n, 0], ACT.Exp).then_inc(e2_ready, 1)
        return
    for t in range(n):
        dve.max(m.top[:, t, :], m.lg[:, t, :]).then_inc(step, 1)
    for t in range(n):
        dve.wait_ge(step, t + 1)
        dve.max_index(m.idx[:, t, :], m.top[:, t, :], m.lg[:, t, :]).then_inc(step, 1)
    dve.wait_ge(step, 2 * n)
    dve.tensor_tensor(m.tmp[:, 0:n, 0], m.top[:, 0:n, 1], m.top[:, 0:n, 0], ALU.subtract).then_inc(step, 1)
    dve.tensor_copy(m.idxf[:, 0:n, :], m.idx[:, 0:n, :]).then_inc(step, 1)
    dve.wait_ge(e2_ready, 1)
    dve.tensor_scalar(m.tmp[:, 0:n, 2], m.tmp[:, 0:n, 1], 1.0, None, ALU.add).then_inc(step, 1)
    dve.wait_ge(step, 2 * n + 3)
    dve.reciprocal(m.sel[:, 0:n, 0], m.tmp[:, 0:n, 2]).then_inc(step, 1)
    dve.wait_ge(step, 2 * n + 4)
    dve.tensor_tensor(m.sel[:, 0:n, 1], m.sel[:, 0:n, 0], m.tmp[:, 0:n, 1], ALU.mult).then_inc(step, 1)
    dve.wait_ge(step, 2 * n + 5)
    iota = m.iota8[:].unsqueeze(1).to_broadcast([P, n, E])
    for k, out in ((0, m.gate), (1, m.pick)):
        out = out[:, 0:n, :]
        dve.tensor_tensor(out, iota, m.idxf[:, 0:n, k:k + 1].to_broadcast([P, n, E]), ALU.is_equal).then_inc(step, 1)
        dve.wait_ge(step, 2 * n + 6 + 2 * k)
        dve.tensor_tensor(out, out, m.sel[:, 0:n, k:k + 1].to_broadcast([P, n, E]), ALU.mult).then_inc(step, 1)
        dve.wait_ge(step, 2 * n + 7 + 2 * k)
    dve.tensor_tensor(m.gate[:, 0:n, :], m.gate[:, 0:n, :], m.pick[:, 0:n, :], ALU.add).then_inc(step, 1)
    dve.wait_ge(step, 2 * n + 10)


def gates_stage(nc, m, layer, by_sequence):
    with ExitStack() as ctx:
        sem = stage_semaphores(nc, ctx, f"gates{layer}")
        meaned, logits_mm, lg_ready, step, e2_ready = sem("meaned"), sem("logits_mm"), sem("lg_ready"), sem("step"), sem("e2_ready")
        gates_ready, turned, copied, biased_mm, biased = sem("gates_ready"), sem("turned"), sem("copied"), sem("biased_mm"), sem("biased")
        block = ctx.enter_context(nc.Block())
        n = NB if by_sequence else T
        lg_psum = m.psum[:, 0, 0:n * E].rearrange("p (t e) -> p t e", e=E)

        @block.tensor
        def _(pe):
            if by_sequence:
                pe.wait_ge(meaned, 2)
            for t in range(n):
                lhs = m.mrep[:, t, :] if by_sequence else m.xT[:, P * t:P * (t + 1)]
                ins = pe.matmul(m.psum[:, 0, E * t:E * (t + 1)], lhs, m.gate_w[:, layer, :], start=True, stop=True)
            ins.then_inc(logits_mm, 1)
            pe.wait_ge(gates_ready, NB)
            for t in range(T):
                ins = pe.transpose(m.psum[0:E, 1 + t // TB, P * (t % TB):P * (t % TB + 1)], m.gate[:, t, :], m.ident[:])
                if t % TB == TB - 1:
                    ins.then_inc(turned, 1)
            for c in range(NCH):
                pe.wait_ge(copied, c + 1)
                for k in range(TB):
                    bank = 5 + c % 3
                    if c == 3 and k == 0:
                        pe.wait_ge(biased, 1)
                    ins = pe.matmul(m.psum[:, bank, P * k:P * (k + 1)], m.gT[:, TB * c + k, :], m.b2[:, layer, :],
                                    start=True, stop=True)
                ins.then_inc(biased_mm, 1)

        @block.scalar
        def _(act):
            top_two(None, act, m, n, step, e2_ready)
            for c in range(NCH):
                act.wait_ge(turned, c + 1)
                act.copy(m.gT[:, TB * c:TB * (c + 1), :], m.psum[0:E, 1 + c, :].rearrange("e (t p) -> e t p", t=TB))\
                    .then_inc(copied, 1)

        @block.vector
        def _(dve):
            if by_sequence:
                dve.reduce_sum(m.msum[:], m.xT[:].rearrange("p (b s) -> p b s", b=NB), AX_X).then_inc(meaned, 1)
                dve.wait_ge(meaned, 1)
                dve.tensor_scalar(m.mrep[:], m.msum[:].unsqueeze(2).to_broadcast([P, NB, P]), 1.0 / S, None, ALU.mult)\
                    .then_inc(meaned, 1)
            dve.wait_ge(logits_mm, 1)
            dve.tensor_tensor(m.lg[:, 0:n, :], lg_psum, m.gate_b[:, layer, :].unsqueeze(1).to_broadcast([P, n, E]),
                              ALU.add).then_inc(lg_ready, 1)
            dve.wait_ge(lg_ready, 1)
            top_two(dve, None, m, n, step, e2_ready)
            if by_sequence:
                dve.tensor_copy(m.pick[:, 0:NB, :], m.gate[:, 0:NB, :]).then_inc(lg_ready, 1)
                dve.wait_ge(lg_ready, 2)
                for b in range(NB):
                    dve.tensor_copy(m.gate[:, b * QT:(b + 1) * QT, :], m.pick[:, b:b + 1, :].to_broadcast([P, QT, E]))\
                        .then_inc(gates_ready, 1)
            else:
                dve.sem_inc(gates_ready, NB)
            for c in range(NCH):
                dve.wait_ge(biased_mm, c + 1)
                y = m.y[:, TB * c:TB * (c + 1), :]
                dve.tensor_tensor(y, m.psum[:, 5 + c % 3, :].rearrange("p (t f) -> p t f", t=TB), y, ALU.add)\
                    .then_inc(biased, 1)


def experts_stage(nc, m, tag, experts, first, mode):
    with ExitStack() as ctx:
        sem = stage_semaphores(nc, ctx, f"{tag}")
        w_loaded = [sem("w_loaded0"), sem("w_loaded1")]
        up_mm, gelu_done, down_mm, added = sem("up_mm"), sem("gelu_done"), sem("down_mm"), sem("added")
        block = ctx.enter_context(nc.Block())
        chosen = mode == "chosen"
        passes = 2 if experts > 1 else 1
        loops = experts // passes
        C = NCH // NB if chosen else NCH
        UB = passes * C
        tok_step = S if chosen else 0
        CRED_UP, CRED_H, CRED_ACC = FC, 2, 2
        w1 = lambda p, k: m.wring[:, p, P * k:P * (k + 1)]
        b1 = lambda p, k: m.wring[:, p, F + k:F + k + 1]
        w2 = lambda p, k: m.wring[:, p, F + FC + D * k:F + FC + D * (k + 1)]

        def looped(eng, body):
            if loops == 1:
                body(0)
            else:
                with eng.Fori(0, loops) as i:
                    body(i)

        @block.sync
        def _(sp):
            experts_w = m.experts_w
            if loops == 1:
                sp.dma_start(m.wring[:, 0, :], experts_w[first]).then_inc(w_loaded[0], 16)
            else:
                for p in range(passes):
                    which = (sp.value_load(m.idx[0:1, 0:1, p:p + 1], min_val=0, max_val=E - 1) + first) if chosen else p + first
                    sp.dma_start(m.wring[:, p:p + 1, :], experts_w[bass.ds(which, 1)].rearrange("e p w -> p e w"))\
                        .then_inc(w_loaded[p], 16)
                with sp.Fori(1, loops) as i:
                    for p in range(passes):
                        if chosen:
                            which = sp.value_load(m.idx[0:1, bass.ds(i, 1), p:p + 1], min_val=0, max_val=E - 1) + first
                        else:
                            which = i * passes + (p + first)
                        sp.wait_ge(down_mm, i * UB + (CRED_H - (passes - 1 - p) * C))
                        sp.dma_start(m.wring[:, p:p + 1, :], experts_w[bass.ds(which, 1)].rearrange("e p w -> p e w"))\
                            .then_inc(w_loaded[p], 16)

        @block.tensor
        def _(pe):
            def body(i):
                for p in range(passes):
                    pe.wait_ge(w_loaded[p], i * 16 + 16)
                    for c in range(C):
                        u = p * C + c
                        for k in range(FC):
                            pe.wait_ge(gelu_done, i * (UB * FC) + (u * FC + k + 1))
                            pe.matmul(m.psum[:, k, :], w1(p, k), m.xT[:, bass.ds(i * tok_step + BANK * c, BANK)],
                                      start=True, stop=True).then_inc(up_mm, 1)
                        pe.wait_ge(added, i * UB + (u + 1))
                        for k in range(FC):
                            pe.wait_ge(gelu_done, i * (UB * FC) + (u * FC + k + 1 + CRED_UP))
                            for t in range(TB):
                                ins = pe.matmul(m.psum[:, 4 + u % 2, P * t:P * (t + 1)], m.h[:, u % 2, k, P * t:P * (t + 1)],
                                                w2(p, k), start=(k == 0 and t == 0), stop=k == FC - 1,
                                                skip_group_check=True)
                        ins.then_inc(down_mm, 1)
            looped(pe, body)

        @block.scalar
        def _(act):
            act.sem_inc(gelu_done, CRED_UP)

            def body(i):
                for p in range(passes):
                    act.wait_ge(w_loaded[p], i * 16 + 16)
                    for c in range(C):
                        u = p * C + c
                        act.wait_ge(down_mm, i * UB + (u + 1))
                        for k in range(FC):
                            act.wait_ge(up_mm, i * (UB * FC) + (u * FC + k + 1))
                            act.activation(m.h[:, u % 2, k, :], m.psum[:, k, :], ACT.Gelu, bias=b1(p, k))\
                                .then_inc(gelu_done, 1)
            looped(act, body)

        @block.vector
        def _(dve):
            dve.sem_inc(down_mm, CRED_H)
            dve.sem_inc(added, CRED_ACC)

            def body(i):
                for p in range(passes):
                    for c in range(C):
                        u = p * C + c
                        dve.wait_ge(down_mm, i * UB + (u + 1 + CRED_H))
                        dve.wait_ge(added, i * UB + (u + CRED_ACC))
                        for t in range(TB):
                            tile = TB * c + t
                            y = m.y[:].rearrange("p t f -> p (t f)")[:, bass.ds(i * (tok_step // P * D) + tile * D, D)]
                            if chosen:
                                gate = m.sel[:].rearrange("p t k -> p (t k)")[:, bass.ds(i * 2 + p, 1)]
                            else:
                                gate = m.gate[:].rearrange("p t e -> p (t e)")[:, bass.ds(i * passes + (tile * E + p), 1)]
                            ins = dve.scalar_tensor_tensor(out=y, in0=m.psum[:, 4 + u % 2, P * t:P * (t + 1)], scalar=gate,
                                                           in1=y, op0=ALU.mult, op1=ALU.add)
                        ins.then_inc(added, 1)
            looped(dve, body)


def tail_stage(nc, m, out):
    with ExitStack() as ctx:
        sem = stage_semaphores(nc, ctx, f"tail")
        cstep, csqrt, ct_mm, route_ready, score_mm = sem("cstep"), sem("csqrt"), sem("ct_mm"), sem("route_ready"), sem("score_mm")
        squared, xsqrt, lg_step, exp_ready = sem("squared"), sem("xsqrt"), sem("lg_step"), sem("exp_ready")
        turned, gt_ready, up_mm, gelu_done = sem("turned"), sem("gt_ready"), sem("up_mm"), sem("gelu_done")
        wide_mm, gated, down_mm, added = sem("wide_mm"), sem("gated"), sem("down_mm"), sem("added")
        block = ctx.enter_context(nc.Block())
        w1 = lambda k: m.tail_w[:, P * k:P * (k + 1)]
        b1 = lambda k: m.tail_w[:, F + k:F + k + 1]
        w2 = lambda k: m.tail_w[:, F + FC + D * k:F + FC + D * (k + 1)]
        N_SQ = 16

        @block.tensor
        def _(pe):
            pe.wait_ge(cstep, 5)
            pe.transpose(m.psum[:, 0, 0:E], m.cscr[:], m.ident[0:E, 0:E]).then_inc(ct_mm, 1)
            pe.wait_ge(route_ready, 1)
            for t in range(T):
                ins = pe.matmul(m.psum[:, 1, 2 * E * t:2 * E * (t + 1)], m.xT[:, P * t:P * (t + 1)], m.route[:],
                                start=True, stop=True)
            ins.then_inc(score_mm, 1)
            pe.wait_ge(lg_step, T + 7)
            for t in range(T):
                ins = pe.transpose(m.psum[0:E, 2 + t // TB, P * (t % TB):P * (t % TB + 1)], m.gate[:, t, :], m.ident[:])
                if t % TB == TB - 1:
                    ins.then_inc(turned, 1)
            for c in range(NCH):
                pe.wait_ge(gt_ready, NCH)
                for k in range(FC):
                    n = c * FC + k
                    if n >= 2:
                        pe.wait_ge(gelu_done, n - 1)
                    pe.matmul(m.psum[:, n % 2, :], w1(k), m.xT[:, BANK * c:BANK * (c + 1)], start=True, stop=True)\
                        .then_inc(up_mm, 1)
                    if n >= 2:
                        pe.wait_ge(gated, n - 1)
                    pe.matmul(m.psum[:, 2 + n % 2, :], m.expand[:, P * k:P * (k + 1)],
                              m.gT[:, TB * c:TB * (c + 1), :].rearrange("e t p -> e (t p)"), start=True, stop=True)\
                        .then_inc(wide_mm, 1)
                if c >= 2:
                    pe.wait_ge(added, c - 1)
                for k in range(FC):
                    pe.wait_ge(gated, c * FC + k + 1)
                    for t in range(TB):
                        pe.matmul(m.psum[:, 6 + c % 2, P * t:P * (t + 1)], m.h[:, c % 2, k, P * t:P * (t + 1)], w2(k),
                                  start=(k == 0 and t == 0), stop=False, skip_group_check=True)
                for t in range(TB):
                    ins = pe.matmul(m.psum[:, 6 + c % 2, P * t:P * (t + 1)], m.gT[:, TB * c + t, :], m.b2[:, 2, :],
                                    start=False, stop=True, skip_group_check=True)
                ins.then_inc(down_mm, 1)

        @block.scalar
        def _(act):
            act.wait_ge(cstep, 1)
            act.activation(m.cn[:, 1:2], m.cn[:, 0:1], ACT.Sqrt).then_inc(csqrt, 1)
            act.wait_ge(squared, 1 + T)
            act.activation(m.std[:], m.tmp[:, :, 0], ACT.Sqrt).then_inc(xsqrt, 1)
            act.wait_ge(lg_step, T + 3)
            act.activation(m.pick[:], m.lg[:], ACT.Exp).then_inc(exp_ready, 1)
            for c in range(NCH):
                act.wait_ge(turned, c + 1)
                act.copy(m.gT[:, TB * c:TB * (c + 1), :], m.psum[0:E, 2 + c, :].rearrange("e (t p) -> e t p", t=TB))\
                    .then_inc(gt_ready, 1)
            for c in range(NCH):
                if c >= 2:
                    act.wait_ge(down_mm, c - 1)
                for k in range(FC):
                    n = c * FC + k
                    act.wait_ge(up_mm, n + 1)
                    act.activation(m.h[:, c % 2, k, :], m.psum[:, n % 2, :], ACT.Gelu, bias=b1(k)).then_inc(gelu_done, 1)

        @block.vector
        def _(dve):
            dve.memset(m.cn[:], 0.0).then_inc(squared, 1)
            dve.wait_ge(squared, 1)
            dve.tensor_tensor_reduce(out=m.cscr[:], in0=m.cent[:], in1=m.cent[:], scale=1.0, scalar=0.0, op0=ALU.mult,
                                     op1=ALU.add, accum_out=m.cn[:, 0:1]).then_inc(cstep, 1)
            dve.wait_ge(csqrt, 1)
            dve.tensor_scalar(m.cn[:, 2:3], m.cn[:, 1:2], 1e-12, None, ALU.max).then_inc(cstep, 1)
            dve.wait_ge(cstep, 2)
            dve.reciprocal(m.cn[:, 3:4], m.cn[:, 2:3]).then_inc(cstep, 1)
            dve.wait_ge(cstep, 3)
            dve.tensor_scalar(m.cscr[:], m.cent[:], m.cn[:, 3:4], None, ALU.mult).then_inc(cstep, 2)
            dve.wait_ge(ct_mm, 1)
            dve.tensor_copy(m.route[:, 0:E], m.psum[:, 0, 0:E]).then_inc(route_ready, 1)
            for t in range(T):
                dve.tensor_tensor_reduce(out=m.nrm[:, t, :], in0=m.x[:, t, :], in1=m.x[:, t, :], scale=1.0, scalar=0.0,
                                         op0=ALU.mult, op1=ALU.add, accum_out=m.tmp[:, t, 0:1]).then_inc(squared, 1)
            dve.wait_ge(xsqrt, 1)
            dve.tensor_scalar(m.std[:], m.std[:], 1e-12, None, ALU.max).then_inc(xsqrt, 1)
            dve.wait_ge(xsqrt, 2)
            dve.reciprocal(m.rstd[:], m.std[:]).then_inc(xsqrt, 1)
            dve.wait_ge(score_mm, 1)
            dve.wait_ge(xsqrt, 3)
            scores = m.psum[:, 1, 0:2 * E * T].rearrange("p (t k e) -> p t k e", t=T, k=2)
            wide = lambda x: x.to_broadcast([P, T, E])
            dve.tensor_tensor(m.lg[:], scores[:, :, 0, :], wide(m.rstd[:].unsqueeze(2)), ALU.mult).then_inc(lg_step, 1)
            dve.wait_ge(lg_step, 1)
            dve.tensor_tensor(m.lg[:], scores[:, :, 1, :], m.lg[:], ALU.add).then_inc(lg_step, 1)
            dve.wait_ge(lg_step, 2)
            for t in range(T):
                dve.max(m.top[:, t, :], m.lg[:, t, :]).then_inc(lg_step, 1)
            dve.wait_ge(lg_step, T + 2)
            dve.tensor_tensor(m.gate[:], m.lg[:], wide(m.top[:, :, 1:2]), ALU.is_ge).then_inc(exp_ready, 1)
            dve.tensor_tensor(m.lg[:], m.lg[:], wide(m.top[:, :, 0:1]), ALU.subtract).then_inc(lg_step, 1)
            dve.wait_ge(exp_ready, 2)
            dve.tensor_tensor(m.gate[:], m.gate[:], m.pick[:], ALU.mult).then_inc(lg_step, 1)
            dve.wait_ge(lg_step, T + 4)
            dve.tensor_reduce(m.tmp[:, :, 1], m.gate[:], AX_X, ALU.add).then_inc(lg_step, 1)
            dve.wait_ge(lg_step, T + 5)
            dve.reciprocal(m.tmp[:, :, 2], m.tmp[:, :, 1]).then_inc(lg_step, 1)
            dve.wait_ge(lg_step, T + 6)
            dve.tensor_tensor(m.gate[:], m.gate[:], wide(m.tmp[:, :, 2:3]), ALU.mult).then_inc(lg_step, 1)

            def add_out(c):
                dve.wait_ge(down_mm, c + 1)
                dve.tensor_tensor(m.y[:, TB * c:TB * (c + 1), :], m.psum[:, 6 + c % 2, :].rearrange("p (t f) -> p t f", t=TB),
                                  m.x[:, TB * c:TB * (c + 1), :], ALU.add).then_inc(added, 1)

            for c in range(NCH):
                for k in range(FC):
                    n = c * FC + k
                    dve.wait_ge(gelu_done, n + 1)
                    dve.wait_ge(wide_mm, n + 1)
                    dve.tensor_tensor(m.h[:, c % 2, k, :], m.psum[:, 2 + n % 2, :], m.h[:, c % 2, k, :], ALU.mult)\
                        .then_inc(gated, 1)
                if c:
                    add_out(c - 1)
            add_out(NCH - 1)


def store_stage(nc, m, out):
    with ExitStack() as ctx:
        stored = stage_semaphores(nc, ctx, "out")("stored")
        block = ctx.enter_context(nc.Block())

        @block.sync
        def _(sp):
            sp.dma_start(out.rearrange("(t p) f -> p t f", p=P), m.x[:]).then_inc(stored, 16)
            sp.wait_ge(stored, 16)


def bias_rows_stage(nc, m, position, bias_rows):
    n = 3 * H
    with ExitStack() as ctx:
        sem = stage_semaphores(nc, ctx, "position")
        loaded, cut = sem("loaded"), sem("cut")
        block = ctx.enter_context(nc.Block())
        wide = m.nrm[:].rearrange("p t f -> p (t f)")[0:n, 0:S]
        narrow = m.part[0:n, 0, 0, 0:S]

        @block.sync
        def _(sp):
            sp.dma_start(wide, position).then_inc(loaded, 16)
            sp.wait_ge(cut, 1)
            sp.dma_start(bias_rows, narrow).then_inc(loaded, 16)
            sp.wait_ge(loaded, 16 * 2)

        @block.vector
        def _(dve):
            dve.wait_ge(loaded, 16)
            dve.tensor_copy(narrow, wide).then_inc(cut, 1)


def copy_stage(nc, m, tag):
    with ExitStack() as ctx:
        copied = stage_semaphores(nc, ctx, tag)("copied")
        block = ctx.enter_context(nc.Block())

        @block.vector
        def _(dve):
            dve.tensor_copy(m.y[:], m.x[:]).then_inc(copied, 1)


def build_program(nc, ins, out, stop=None):
    RETIRED.clear()
    with ExitStack() as ctx:
        m = allocate(nc, ctx)
        nc.disable_value_cache = True
        m.experts_w = ins["experts_w"]
        bias_rows = nc.dram_tensor("bias_rows", [3, H, S], BF16).ap()

        def attention(a, causal, rows=None):
            project_stage(nc, m, a, ins["attn_w"])
            attention_stage(nc, m, a, causal, rows)
            out_project_stage(nc, m, a)

        load_stage(nc, m, ins)
        bias_rows_stage(nc, m, ins["position"], bias_rows)
        norm_stage(nc, m, "n0", m.y, turned=True, ln=0)
        attention(0, False)
        if stop == "a0": return m
        norm_stage(nc, m, "n1", m.y, turned=True, ln=1)
        ffn_bias_stage(nc, m)
        experts_stage(nc, m, "ffn", 1, 0, "all")
        norm_stage(nc, m, "n2", m.x, add=m.y, plain_out=m.x)
        copy_stage(nc, m, "c1")
        if stop == "b1": return m
        for layer in range(2):
            norm_stage(nc, m, f"l{layer}a", m.y, turned=True, ln=2 + 2 * layer)
            attention(1 + layer, True)
            norm_stage(nc, m, f"l{layer}b", m.y, turned=True, ln=3 + 2 * layer)
            gates_stage(nc, m, layer, by_sequence=layer == 1)
            if layer == 0:
                experts_stage(nc, m, "moe0", E, 1, "all")
            else:
                experts_stage(nc, m, "moe1", 2 * NB, 1 + E, "chosen")
            if stop == f"l{layer}": return m
        norm_stage(nc, m, "n3", m.x, add=m.y, plain_out=m.x, turned=True, ln=None)
        copy_stage(nc, m, "c2")
        if stop == "b2": return m
        attention(3, True, bias_rows)
        norm_stage(nc, m, "n4", m.y, plain_out=m.x, turned=True, ln=None)
        if stop == "b3": return m
        tail_stage(nc, m, out)
        norm_stage(nc, m, "n5", m.y, plain_out=m.x)
        store_stage(nc, m, out)



def _layout(x):
    import numpy as np

    a = {k: np.asarray(v) for k, v in x.items()}
    f32 = np.float32

    def heads_last(w):
        return w.reshape(*w.shape[:-1], HG, G, HD).swapaxes(-1, -2).reshape(w.shape)

    def attn(q, k, v, o):
        return np.stack([heads_last(q), heads_last(k), v, o], axis=1)

    w0 = a["L0_attn_in_proj_w"].T
    w3 = a["L1_attn_w_in"].T
    attn_w = [attn(w0[:, 0:D], w0[:, D:2 * D], w0[:, 2 * D:], a["L0_attn_out_w"].T)]
    attn_w += [attn(a["L0_ffn_wq"][l], a["L0_ffn_wk"][l], a["L0_ffn_wv"][l], a["L0_ffn_wo"][l]) for l in range(2)]
    attn_w += [attn(w3[:, 0:D], w3[:, D:2 * D], w3[:, 2 * D:], a["L1_attn_w_out"].T)]
    b0 = a["L0_attn_in_proj_b"]
    zero = np.zeros(D, f32)
    q_b = [b0[0:D], a["L0_ffn_bq"][0], a["L0_ffn_bq"][1], zero]
    k_b = [b0[D:2 * D], a["L0_ffn_bk"][0], a["L0_ffn_bk"][1], zero]
    v_b = [b0[2 * D:], a["L0_ffn_bv"][0], a["L0_ffn_bv"][1], zero]
    o_b = [a["L0_attn_out_b"], a["L0_ffn_bo"][0], a["L0_ffn_bo"][1], zero]
    abcol = np.stack([np.stack([heads_last(q_b[i]), heads_last(k_b[i])], axis=-1) for i in range(4)], axis=1)
    abrow = np.stack([np.stack([v_b[i], o_b[i]]) for i in range(4)])
    lncol = [(a["L0_attn_norm1_w"], a["L0_attn_norm1_b"]), (a["L0_attn_norm2_w"], a["L0_attn_norm2_b"])]
    for l in range(2):
        lncol += [(a["L0_ffn_ln1_w"][l], a["L0_ffn_ln1_b"][l]), (a["L0_ffn_ln2_w"][l], a["L0_ffn_ln2_b"][l])]
    lncol = np.stack([np.stack(p, axis=-1) for p in lncol], axis=1)

    def expert(w1, b1, w2):
        return np.concatenate([w1, b1.reshape(FC, P).T, w2.reshape(FC, P, D).transpose(1, 0, 2).reshape(P, FC * D)], axis=1)

    experts = [expert(a["L0_attn_lin1_w"].T, a["L0_attn_lin1_b"], a["L0_attn_lin2_w"].T)]
    experts += [expert(a["L0_ffn_e_w1"][l, e], a["L0_ffn_e_b1"][l, e], a["L0_ffn_e_w2"][l, e]) for l in range(2) for e in range(E)]
    tail_w = expert(a["L1_ffn_w1"].transpose(1, 0, 2).reshape(D, F), a["L1_ffn_b1"].reshape(F), a["L1_ffn_w2"].reshape(F, D))
    b2 = np.stack([a["L0_ffn_e_b2"][0], a["L0_ffn_e_b2"][1], a["L1_ffn_b2"]], axis=1)

    q, k = np.arange(P)[:, None], np.arange(P)[None, :]
    mask = np.stack([np.where(k > q, -BIG / 3, 0.0), np.where(k < q, -BIG / 3, 0.0)], axis=1).astype(f32)
    slope = (2.0 ** (-8.0 / H * (np.arange(H) + 1.0))).astype(f32).astype(np.float64)
    rest = slope[:, None] * (np.arange(S) - S // 2)[None, :]
    position = []
    for _ in range(3):
        bits = rest.astype(f32).view(np.uint32)
        cut = (((bits.astype(np.uint64) + 0x8000) & 0xFFFF0000).astype(np.uint32)).view(f32)
        position.append(cut)
        rest = rest - cut
    expand = (np.arange(F)[None, :] // (F // E) == np.arange(E)[:, None]).astype(f32)
    arrays = {
        "x": a["L0_attn_x"].reshape(TOK, D), "attn_w": np.stack(attn_w), "abcol": abcol, "abrow": abrow, "lncol": lncol,
        "experts_w": np.stack(experts), "tail_w": tail_w, "b2": b2, "b2ffn": a["L0_attn_lin2_b"],
        "gate_w": a["L0_ffn_gate_w"].transpose(1, 0, 2), "gate_b": a["L0_ffn_gate_b"],
        "centroids": a["L1_ffn_centroids"], "route_w": a["L1_ffn_w_route"].T,
        "ident": np.eye(P, dtype=f32), "mask": mask, "iota8": np.arange(E, dtype=f32),
        "position": np.stack(position).reshape(3 * H, S), "expand": expand,
    }
    return {n: np.ascontiguousarray(v) for n, v in arrays.items()}


def kernel(**inputs):
    import concourse.bacc as _bacc
    from concourse.bass_utils import run_bass_kernel_spmd as _run

    nc = _bacc.Bacc("TRN2", target_bir_lowering=False, num_devices=1)
    arrays = {f"in_{n}": v for n, v in _layout(inputs).items()}
    ins = {n[3:]: nc.dram_tensor(n, v.shape, mybir.dt.from_np(v.dtype), kind="ExternalInput").ap() for n, v in arrays.items()}
    out = nc.dram_tensor("out_0", (TOK, D), F32, kind="ExternalOutput").ap()
    build_program(nc, ins, out)
    r = _run(nc, [arrays], core_ids=[0])
    return r.results[0]["out_0"].reshape(NB, S, D)
```

```python
from contextlib import ExitStack, contextmanager

import concourse.bass as bass
from concourse import mybir

F32 = mybir.dt.float32
F32R = mybir.dt.float32r
BF16 = mybir.dt.bfloat16
U32 = mybir.dt.uint32
ALU = mybir.AluOpType
ACT = mybir.ActivationFunctionType
AX_X = mybir.AxisListType.X

P = 128
NB, S, D = 2, 1024, 128
H, HD = 16, 8
TOK = NB * S
T = TOK // P
BANK = 512
TB = BANK // P
NCH = TOK // BANK
QT = S // P
G = 4
NG = NB * H // G
GW = G * HD
HG = H // G
E = 8
F = 512
FC = F // P
WCOLS = F + FC + FC * D
EPS = 1e-5
BIG = 3.0e38

Q_PART = [0, 0, 0, 1, 1, 1, 2, 2]
K_PART = [0, 1, 2, 0, 1, 2, 0, 1]
TERMS = len(Q_PART)
ROW_BIAS = TERMS * HD
ROW_MAX = P - 3
VW = HD + 1


class Memory:
    pass


def allocate(nc, ctx):
    m = Memory()

    def sb(name, shape, dt=F32):
        return ctx.enter_context(nc.sbuf_tensor(name, shape, dt))

    m.psum = ctx.enter_context(nc.psum_tensor("psum", [P, 8, BANK], F32))
    m.x = sb("x_outer", [P, T, D])
    m.y = sb("y_inner", [P, T, D])
    m.nrm = sb("normalized", [P, T, D])
    m.stats = sb("stats", [P, T, 6])
    m.meanvar = sb("meanvar", [P, T, 2])
    m.std = sb("std", [P, T])
    m.rstd = sb("rstd", [P, T])
    m.shift = sb("shift", [P, T])
    m.unused = sb("unused", [P, 4])
    m.xT = sb("xT", [P, TOK])
    m.ident = sb("ident", [P, P])
    m.identb = sb("identb", [P, P], BF16)
    m.maskb = sb("maskb", [P, 2, P], BF16)
    m.zero = sb("zero", [P, 1])
    m.iota8 = sb("iota8", [P, E])
    m.lncol = sb("lncol", [P, 6, 2])
    m.attn_w = sb("attn_w", [P, 4, 4, D])
    m.abcol = sb("attn_bias_cols", [P, 4, 2])
    m.abrow = sb("attn_bias_rows", [P, 4, 2, D])
    m.qbias = sb("scaled_q_bias", [P, 4])
    m.part = sb("qk_parts", [P, 2, 3, TOK], BF16)
    m.v = sb("v_all", [P, T, H * VW])
    m.vst = sb("v_stage", [P, 3, QT, G * VW])
    m.qs = sb("q_slots", [P, 3, G, S], BF16)
    m.ks = sb("k_slots", [P, 3, G, S], BF16)
    m.prob = sb("prob", [P, 4, 2, BANK])
    m.full, m.rest = m.prob[:, 0:2], m.prob[:, 2:4]
    m.outT = sb("outT", [P, 2, BANK])
    m.rsum = sb("row_sum_inverse", [P, 2, TB, G])
    m.ctx = m.nrm
    m.mx = sb("chunk_max", [P, G, QT, 2])
    m.negm = sb("neg_max", [P, 2, TB, G])
    m.negr = sb("neg_max_rest", [P, 2, TB, G])
    m.negp = sb("neg_max_parts", [P, 2, TB, 3, G], BF16)
    m.maxT = sb("neg_max_turned", [3 * G, BANK], BF16)
    m.x_part = [sb(f"x_part{part}", [P, TOK], F32R) for part in range(2)]
    m.w_part = sb("w_part", [P, 2, 2, F], F32R)
    m.wring = sb("expert_w", [P, 2, WCOLS])
    m.h = m.prob[:].rearrange("p s c n -> p (s c) n").rearrange("p (u k) n -> p u k n", u=2)
    m.gate_w = sb("gate_w", [P, 2, E])
    m.gate_b = sb("gate_b", [P, 2, E])
    m.b2 = sb("b2", [E, 3, D])
    m.b2ffn = sb("b2_ffn", [P, D])
    m.lg = sb("logits", [P, T, E])
    m.top = sb("top8", [P, T, 8])
    m.idx = sb("top8_index", [P, T, 8], U32)
    m.idxf = sb("top8_index_f", [P, T, 8])
    m.pick = sb("pick", [P, T, E])
    m.gate = sb("gates", [P, T, E])
    m.sel = sb("selected_weights", [P, T, 2])
    m.tmp = sb("gate_tmp", [P, T, 4])
    m.gT = sb("gatesT", [E, T, P])
    m.msum = sb("token_mean", [P, NB])
    m.mrep = sb("token_mean_rep", [P, NB, P])
    m.tail_w = sb("tail_w", [P, WCOLS])
    m.cent = sb("centroids", [E, D])
    m.cscr = sb("centroid_scratch", [E, D])
    m.cn = sb("centroid_norm", [E, 4])
    m.route = sb("route_w", [P, 2 * E])
    m.expand = sb("expand", [E, F])
    return m


REGION_SEMAPHORES = 70
RETIRED = []


@contextmanager
def region(nc, m):
    if nc.free_len() < REGION_SEMAPHORES:
        nc.clear_and_free_semaphores(RETIRED)
        RETIRED.clear()
        nc.all_engine_barrier()
    m.made = []
    with nc.Block() as m.block:
        yield
    RETIRED.extend(m.made)


def stage_semaphores(nc, m, tag):
    def sem(name):
        m.made.append(nc.alloc_semaphore(f"{tag}_{name}"))
        return m.made[-1]

    return sem


def wait_all(eng, values):
    for sem, value in values:
        eng.wait_ge(sem, value)


def broadcast_rows(row, n=P):
    return row.partition_broadcast(n)


ONE_PAIR = 0x3F803F80


def pairs(slots):
    return slots[:].rearrange("p s j t -> p (s j t)").bitcast(U32)


def load_stage(nc, m, ins):
    sem = stage_semaphores(nc, m, "shared")
    x_loaded = [sem(f"x_loaded{c}") for c in range(NCH)]
    first_loaded, loaded, made, built = sem("first_loaded"), sem("loaded"), sem("made"), sem("built")
    scaled = sem("scaled")
    block = m.block
    first = ((m.ident, ins["ident"]), (m.lncol, ins["lncol"]), (m.attn_w, ins["attn_w"]), (m.abcol, ins["abcol"]),
             (m.abrow, broadcast_rows(ins["abrow"])))
    rest = ((m.identb, ins["identb"].bitcast(BF16)), (m.maskb, ins["maskb"].bitcast(BF16)),
            (m.gate_w, ins["gate_w"]), (m.gate_b, broadcast_rows(ins["gate_b"])), (m.iota8, broadcast_rows(ins["iota8"])),
            (m.b2, ins["b2"]), (m.b2ffn, broadcast_rows(ins["b2ffn"])), (m.tail_w, ins["tail_w"]),
            (m.cent, ins["centroids"]), (m.expand, ins["expand"]))

    @block.sync
    def _(sp):
        rows = ins["x"].rearrange("(t p) f -> p t f", p=P)
        for c in range(NCH):
            sp.dma_start(m.x[:, TB * c:TB * (c + 1), :], rows[:, TB * c:TB * (c + 1), :]).then_inc(x_loaded[c], 16)
        for buffer, source in first:
            sp.dma_start(buffer[:], source).then_inc(first_loaded, 16)
        for buffer, source in rest:
            sp.dma_start(buffer[:], source).then_inc(loaded, 16)
        sp.dma_start(m.route[:, E:2 * E], ins["route_w"]).then_inc(loaded, 16)
        for n in range(2):
            sp.dma_start(m.ks[64 + 32 * n:96 + 32 * n].rearrange("p s j t -> p (s j t)"),
                         broadcast_rows(ins["zeros_ones"][n].bitcast(BF16), 32)).then_inc(loaded, 16)
        sp.wait_ge(loaded, (len(rest) + 3) * 16)
        sp.wait_ge(made, 2)
        sp.wait_ge(built, 2)

    @block.gpsimd
    def _(pool):
        for n, (rows, value) in enumerate(((slice(64, 96), ONE_PAIR), (slice(96, P), 0))):
            pool.memset(pairs(m.qs)[rows], value).then_inc(made, 1)
            pool.wait_ge(made, n + 1)

    @block.vector
    def _(dve):
        dve.memset(m.zero[:], 0.0).then_inc(built, 1)
        v = m.v[:].rearrange("p t (h w) -> p (t h) w", w=VW)
        dve.memset(v[:, :, HD:VW], 1.0).then_inc(built, 1)
        dve.wait_ge(built, 2)

    @block.tensor
    def _(pe):
        pe.wait_ge(first_loaded, len(first) * 16)

    @block.scalar
    def _(act):
        act.wait_ge(built, 1)
        act.wait_ge(first_loaded, len(first) * 16)
        act.activation(m.qbias[:], m.abcol[:, :, 0], ACT.Copy, scale=float(HD) ** -0.5).then_inc(scaled, 1)
        act.wait_ge(scaled, 1)

    return lambda c: [(x_loaded[c], 16)]


def load_table(act, m, function, stage):
    act.activation(m.unused[:, stage:stage + 1], m.zero[:], function)


def norm_stage(nc, m, tag, src, turned=False, ln=0, add=None, plain_out=None, ready=None):
    dst = plain_out if plain_out is not None else m.nrm
    work = m.y if add is not None else src
    sem = stage_semaphores(nc, m, f"{tag}")
    summed, measured, aggregated, var_ready = sem("summed"), sem("measured"), sem("aggregated"), sem("var_ready")
    std_ready, rstd_ready = sem("std_ready"), sem("rstd_ready")
    turned_sem, evacuated, shift_ready = sem("turned"), sem("evacuated"), sem("shift_ready")
    act_tiles = [t for t in range(T) if t % 8 in (3, 6, 7)]
    by_dve, by_act = sem("by_dve"), sem("by_act")
    acts_done = lambda c: sum(t < TB * (c + 1) for t in act_tiles)
    normalized_chunk = lambda c: [(by_dve, TB * (c + 1) - acts_done(c)), (by_act, acts_done(c))]
    block = m.block

    @block.vector
    def _(dve):
        if add is not None:
            for c in range(NCH):
                if ready is not None:
                    wait_all(dve, ready(c))
                dve.tensor_tensor(work[:, TB * c:TB * (c + 1), :], src[:, TB * c:TB * (c + 1), :],
                                  add[:, TB * c:TB * (c + 1), :], ALU.add).then_inc(summed, 1)
        for t in range(T):
            if add is not None:
                dve.wait_ge(summed, t // TB + 1)
            elif ready is not None and t % TB == 0:
                wait_all(dve, ready(t // TB))
            dve.bn_stats(m.stats[:, t, :], work[:, t, :]).then_inc(measured, 1)
        for t in range(T):
            dve.wait_ge(measured, t + 1)
            dve.bn_aggr(m.meanvar[:, t, :], m.stats[:, t, :]).then_inc(aggregated, 1)
        dve.wait_ge(aggregated, T)
        dve.tensor_scalar(m.std[:], m.meanvar[:, :, 1], EPS, None, ALU.add).then_inc(var_ready, 1)
        dve.wait_ge(std_ready, 1)
        dve.reciprocal(m.rstd[:], m.std[:]).then_inc(rstd_ready, 1)
        dve.wait_ge(rstd_ready, 1)
        dve.scalar_tensor_tensor(out=m.shift[:], in0=m.meanvar[:, :, 0], scalar=-1.0, in1=m.rstd[:], op0=ALU.mult,
                                 op1=ALU.mult).then_inc(shift_ready, 1)
        for t in range(T):
            if t not in act_tiles:
                dve.tensor_scalar(dst[:, t, :], work[:, t, :], m.meanvar[:, t, 0:1], m.rstd[:, t:t + 1],
                                  ALU.subtract, ALU.mult).then_inc(by_dve, 1)

    @block.scalar
    def _(act):
        load_table(act, m, ACT.Sqrt, 0)
        act.wait_ge(var_ready, 1)
        act.activation(m.std[:], m.std[:], ACT.Sqrt).then_inc(std_ready, 1)
        act.wait_ge(shift_ready, 1)
        for t in act_tiles:
            act.activation(dst[:, t, :], work[:, t, :], ACT.Identity, bias=m.shift[:, t:t + 1],
                           scale=m.rstd[:, t:t + 1]).then_inc(by_act, 1)
        if turned:
            for c in range(NCH):
                act.wait_ge(turned_sem, c + 1)
                out = m.xT[:, BANK * c:BANK * (c + 1)]
                if ln is None:
                    act.activation(out, m.psum[:, c, :], ACT.Copy).then_inc(evacuated, 1)
                else:
                    act.activation(out, m.psum[:, c, :], ACT.Identity, bias=m.lncol[:, ln, 1:2],
                                   scale=m.lncol[:, ln, 0:1]).then_inc(evacuated, 1)

    if turned:
        @block.tensor
        def _(pe):
            for t in range(T):
                if t % TB == 0:
                    wait_all(pe, normalized_chunk(t // TB))
                ins = pe.transpose(m.psum[:, t // TB, P * (t % TB):P * (t % TB + 1)], dst[:, t, :], m.ident[:])
                if t % TB == TB - 1:
                    ins.then_inc(turned_sem, 1)

    return (lambda c: [(evacuated, c + 1)]) if turned else normalized_chunk


def project_stage(nc, m, a, ready):
    sem = stage_semaphores(nc, m, f"proj{a}")
    qk_mm, v_mm = sem("qk_mm"), sem("v_mm")
    full_ready, hi_ready, rest_ready, mid_ready = sem("full_ready"), sem("hi_ready"), sem("rest_ready"), sem("mid_ready")
    lo_ready, v_ready = sem("lo_ready"), sem("v_ready")
    block = m.block
    parts = lambda s, part, c: m.part[:, s, part, BANK * c:BANK * (c + 1)]

    @block.tensor
    def _(pe):
        for c in range(NCH):
            if ready is not None:
                wait_all(pe, ready(min(2 * c + 1, NCH - 1)))
            for s in range(2):
                if c >= 2:
                    pe.wait_ge(hi_ready, 2 * (c - 2) + s + 1)
                pe.matmul(m.psum[:, 2 * (c % 2) + s, :], m.attn_w[:, a, s, :], m.xT[:, BANK * c:BANK * (c + 1)],
                          start=True, stop=True).then_inc(qk_mm, 1)
            if c >= 2:
                pe.wait_ge(v_ready, c - 1)
            for t in range(TB):
                tok = BANK * c + P * t
                ins = pe.matmul(m.psum[:, 4 + c % 2, P * t:P * (t + 1)], m.xT[:, tok:tok + P], m.attn_w[:, a, 2, :],
                                start=True, stop=True)
            ins.then_inc(v_mm, 1)

    @block.scalar
    def _(act):
        for n in range(2 * NCH):
            c, s = n // 2, n % 2
            act.wait_ge(qk_mm, n + 1)
            if n >= 4:
                act.wait_ge(rest_ready, n - 3)
            bias = m.qbias[:, a:a + 1] if s == 0 else m.abcol[:, a, 1:2]
            scale = float(HD) ** -0.5 if s == 0 else 1.0
            act.activation(m.full[:, s, c % 2, :], m.psum[:, 2 * (c % 2) + s, :], ACT.Identity, bias=bias,
                           scale=scale).then_inc(full_ready, 1)
            act.activation(parts(s, 0, c), m.psum[:, 2 * (c % 2) + s, :], ACT.Identity, bias=bias,
                           scale=scale).then_inc(hi_ready, 1)

    @block.vector
    def _(dve):
        for n in range(2 * NCH):
            c, s = n // 2, n % 2
            dve.wait_ge(full_ready, n + 1)
            dve.wait_ge(hi_ready, n + 1)
            if n >= 4:
                dve.wait_ge(lo_ready, n - 3)
            dve.tensor_tensor(m.rest[:, s, c % 2, :], m.full[:, s, c % 2, :], parts(s, 0, c),
                              ALU.subtract).then_inc(rest_ready, 1)
            dve.wait_ge(rest_ready, n + 1)
            dve.tensor_copy(parts(s, 1, c), m.rest[:, s, c % 2, :]).then_inc(mid_ready, 1)
            if s == 1:
                dve.wait_ge(v_mm, c + 1)
                out = m.v[:, TB * c:TB * (c + 1), :].rearrange("p t (h w) -> p t h w", w=VW)[:, :, :, 0:HD]
                ins = dve.tensor_tensor(out, m.psum[:, 4 + c % 2, :].rearrange("p (t h w) -> p t h w", t=TB, w=HD),
                                        m.abrow[:, a, 0, :].rearrange("p (h w) -> p h w", w=HD).unsqueeze(1)
                                        .to_broadcast([P, TB, H, HD]), ALU.add)
                ins.then_inc(v_ready, 1)

    @block.gpsimd
    def _(pool):
        for n in range(2 * NCH):
            c, s = n // 2, n % 2
            pool.wait_ge(mid_ready, n + 1)
            pool.tensor_tensor(parts(s, 2, c), m.rest[:, s, c % 2, :], parts(s, 1, c),
                               ALU.subtract).then_inc(lo_ready, 1)

    return hi_ready, mid_ready, lo_ready, v_ready


def attention_stage(nc, m, a, causal, bias_rows, projected):
    RING = 3
    halves = [[kt for kt in range(QT) if not causal or kt < TB * (hf + 1)] for hf in range(2)]
    units = [(hf, kt) for hf in range(2) for kt in reversed(halves[hf])]
    U = len(units)
    first_q = lambda u: max(units[u][0] * BANK, units[u][1] * P) if causal else units[u][0] * BANK
    width = lambda u: BANK * (units[u][0] + 1) - first_q(u)
    last_of_half = [len(halves[0]) - 1, U - 1]
    rows = [[], []]
    for hf in range(2):
        for qt in range(TB * hf, TB * (hf + 1)):
            for k0 in (0, BANK):
                keys = min(S if not causal else P * (qt + 1), k0 + BANK) - k0
                together = max(BANK // keys, 1) if keys > 0 else 0
                if keys > 0:
                    rows[hf] += [(range(j, j + together), qt, k0, keys) for j in range(0, G, together)]

    def plan(next_group, this_group, last_group):
        others = []
        if this_group:
            for u in range(U):
                others += [(("col", u, p), 0.9 * width(u)) for p in range(2)]
                if u:
                    others.append((("pv", u - 1, 0), 1.8 * width(u - 1)))
                if u == 0:
                    if last_group:
                        others.append((("pv", U - 1, 1), 1.8 * BANK))
                    others.append((("turn_max", 1, 0), 100))
                if u == 1 and last_group:
                    others.append((("turn", 1, 1), 2 * BANK))
                if u == last_of_half[0] + 3:
                    others.append((("turn", 0, 0), 2 * BANK))
        elif last_group:
            others += [(("pv", U - 1, 1), 1), (("turn", 1, 1), 1)]
        spread = []
        if next_group:
            for hf in range(2):
                for n, r in enumerate(rows[hf]):
                    spread.append((("row", r), 65 + 1.04 * len(r[0]) * r[3]))
                    if hf == 1 and n == 3:
                        spread.append((("turn_max", 0, 1), 100))
                spread.append((("negate", hf), 200))
        if not others or not spread:
            return [s for s, _ in others + spread]
        steps, done, rows_done = [], 0.0, 0.0
        total, rows_total = sum(w for _, w in others), sum(w for _, w in spread)
        for s, w in others:
            steps.append(s)
            done += w
            while spread and rows_done / rows_total < done / total:
                steps.append(spread[0][0])
                rows_done += spread.pop(0)[1]
        return steps + [s for s, _ in spread]

    in_ring = lambda s: s[0] in ("row", "turn", "turn_max")
    ring_len = lambda steps: sum(in_ring(s) for s in steps)
    first, body0, body = plan(True, False, False), plan(True, True, False), plan(True, True, True)
    last, tail = plan(False, True, True), plan(False, False, True)
    SLOTS = 3
    assert (NG - 2) % SLOTS == 0 and SLOTS % RING == 0

    def program(eng, run):
        run(first, -1, 0, 0)
        run(body0, 0, 0, ring_len(first))
        base = ring_len(first) + ring_len(body0)
        with eng.Fori(0, (NG - 2) // SLOTS) as i:
            for k in range(SLOTS):
                run(body, 1 + k, i, base + k * ring_len(body))
        base += (NG - 2) * ring_len(body)
        run(last, NG - 1, 0, base)
        run(tail, NG, 0, base + ring_len(last))

    sem = stage_semaphores(nc, m, f"attn{a}")
    stacks_loaded, max_loaded = sem("stacks_loaded"), sem("max_loaded")
    ring_full, ring_free = sem("ring_full"), sem("ring_free")
    col_full, prob_full = sem("col_full"), sem("prob_full")
    pv_done, out_copied, inverted = sem("pv_done"), sem("out_copied"), sem("inverted")
    cleared, v_staged, neg_made, neg_step, neg_split = sem("cleared"), sem("v_staged"), sem("neg_made"), sem("neg_step"), sem("neg_split")
    block = m.block
    STACK_DMAS = 2 * TERMS + (1 if bias_rows is not None else 0)
    MAX_LOAD = 16
    hi_ready, mid_ready, lo_ready, v_ready = projected
    OUT = 7

    CRED_RING, CRED_COL, CRED_PV, CRED_OUT, CRED_TURN = RING, 2, 2, 1, 2
    col_bank = lambda u, p: RING + 2 * p

    def of_group(g, i):
        return lambda n, x: i * (SLOTS * n) + (g * n + x)

    def ring_at(steps, count, i):
        return lambda x: i * (SLOTS * ring_len(body)) + (count + x)

    max_at = lambda steps, hf: ring_len(steps[:[s[:2] for s in steps].index(("turn_max", hf))]) + 1

    @block.sync
    def _(sp):
        def load(g):
            slot = bass.ds((g % SLOTS) * G, G)
            qs, ks = (x[:].rearrange("p s j t -> p (s j) t") for x in (m.qs, m.ks))
            b, rows32 = g // HG, slice((g % HG) * GW, (g % HG + 1) * GW)
            for part, ready in enumerate((hi_ready, mid_ready, lo_ready)):
                sp.wait_ge(ready, 2 * NCH // NB * (b + 1))
                for s, (stack, of_term) in enumerate(((qs, Q_PART), (ks, K_PART))):
                    for t in range(TERMS):
                        if of_term[t] == part:
                            sp.dma_start(stack[t * HD:(t + 1) * HD, slot, :],
                                         m.part[rows32, s, part, b * S:(b + 1) * S]).then_inc(stacks_loaded, 16)
            if bias_rows is not None:
                sp.dma_start(ks[ROW_BIAS:ROW_BIAS + 3, slot, :], bias_rows[:, bass.ds((g % HG) * G, G), :])\
                    .then_inc(stacks_loaded, 16)

        def load_max(g, hf, turned):
            sp.wait_ge(ring_free, turned)
            if g or hf:
                sp.wait_ge(max_loaded, g * (2 * MAX_LOAD) + hf * MAX_LOAD)
            qs = m.qs[:].rearrange("p s j t -> p (s j) t")
            sp.dma_start(qs[ROW_MAX:P, bass.ds((g % SLOTS) * G, G), BANK * hf:BANK * (hf + 1)], m.maxT[:])\
                .then_inc(max_loaded, 16)

        n = ring_len(body)
        base = CRED_RING + ring_len(first)
        load(0)
        sp.wait_ge(stacks_loaded, 16 * STACK_DMAS)
        load_max(0, 0, CRED_RING + max_at(first, 0))
        load(1)
        sp.wait_ge(stacks_loaded, 2 * 16 * STACK_DMAS)
        load_max(0, 1, base + max_at(body0, 1))
        load(2)
        sp.wait_ge(stacks_loaded, 3 * 16 * STACK_DMAS)
        load_max(1, 0, base + max_at(body0, 0))
        base += ring_len(body0)
        load_max(1, 1, base + max_at(body, 1))
        for g in range(1, NG - 2):
            sp.wait_ge(pv_done, g * U + CRED_PV)
            load(g + 2)
            load_max(g + 1, 0, g * n + (base - n + max_at(body, 0)))
            sp.wait_ge(stacks_loaded, g * (16 * STACK_DMAS) + SLOTS * 16 * STACK_DMAS)
            load_max(g + 1, 1, g * n + (base + max_at(body, 1)))
        load_max(NG - 1, 0, base + n * (NG - 3) + max_at(body, 0))
        load_max(NG - 1, 1, base + n * (NG - 2) + max_at(last, 1))
        sp.wait_ge(max_loaded, 2 * MAX_LOAD * NG)

    @block.gpsimd
    def _(pool):
        def copy(out, x):
            return pool.tensor_tensor(out, x, (m.zero[:] if len(x.shape) == 2 else m.zero[:].unsqueeze(2)).to_broadcast(x.shape), ALU.subtract)

        def group(g, slot_used):
            if slot_used is not None:
                pool.wait_ge(pv_done, slot_used)
            v = m.v[:].rearrange("p (b t) (g c) -> p b t g c", b=NB, g=HG)[:, bass.ds(g // HG, 1), :, bass.ds(g % HG, 1), :]
            v = v.rearrange("p b t g c -> p (b t) (g c)")
            vst = m.vst[:].rearrange("p s t c -> p (s t) c")[:, bass.ds((g % SLOTS) * QT, QT), :]
            copy(vst, v).then_inc(v_staged, 1)
            for hf in range(2):
                pool.wait_ge(neg_made, g * 2 + (hf + 1))
                if slot_used is not None:
                    pool.wait_ge(max_loaded, g * (2 * MAX_LOAD) + (hf - 1) * MAX_LOAD)
                elif g > 0:
                    pool.wait_ge(max_loaded, (2 * g + hf - 1) * MAX_LOAD)
                parts = m.negp[:, hf].rearrange("p t a j -> p a t j")
                negm, negr = m.negm[:, hf], m.negr[:, hf]
                copy(parts[:, 0], negm).then_inc(neg_step, 1)
                pool.wait_ge(neg_step, g * 6 + (3 * hf + 1))
                pool.tensor_tensor(negr, negm, parts[:, 0], ALU.subtract).then_inc(neg_step, 1)
                pool.wait_ge(neg_step, g * 6 + (3 * hf + 2))
                copy(parts[:, 1], negr).then_inc(neg_step, 1)
                pool.wait_ge(neg_step, g * 6 + (3 * hf + 3))
                pool.tensor_tensor(parts[:, 2], negr, parts[:, 1], ALU.subtract).then_inc(neg_split, 1)

        pool.wait_ge(v_ready, NCH)
        for g in range(SLOTS):
            group(g, None)
        with pool.Fori(SLOTS, NG) as g:
            group(g, g * U + (CRED_PV - (SLOTS - 1) * U))

    @block.tensor
    def _(pe):
        def run(steps, g, i, count):
            at, ring = of_group(g, i), ring_at(steps, count, i)
            this_slot, next_slot, next_at = g % SLOTS, (g + 1) % SLOTS, of_group(g + 1, i)
            n = 0
            for step in steps:
                kind = step[0]
                if in_ring(step):
                    pe.wait_ge(ring_free, ring(n + 1))
                    bank = (count + n) % RING
                    n += 1
                if kind == "row":
                    heads, qt, k0, keys = step[1]
                    if qt == 0 and k0 == 0 and heads[0] == 0:
                        pe.wait_ge(stacks_loaded, next_at(16 * STACK_DMAS, 16 * STACK_DMAS))
                    diagonal = causal and k0 + keys == P * (qt + 1)
                    for h, j in enumerate(heads):
                        out = m.psum[:, bank, h * keys:(h + 1) * keys]
                        ins = pe.matmul(out, m.qs[0:ROW_MAX, next_slot, j, P * qt:P * (qt + 1)],
                                        m.ks[0:ROW_MAX, next_slot, j, k0:k0 + keys], start=True, stop=not diagonal)
                        if diagonal:
                            ins = pe.matmul(out[:, keys - P:keys], m.identb[:], m.maskb[:, 0, :], start=False, stop=True)
                    ins.then_inc(ring_full, 1)
                elif kind == "turn_max":
                    hf, ahead = step[1:]
                    pe.wait_ge(neg_split, (next_at if ahead else at)(2, hf + 1))
                    for t in range(TB):
                        ins = pe.matmul(m.psum[0:3 * G, bank, P * t:P * (t + 1)], m.negp[:, hf, t].rearrange("p a j -> p (a j)"),
                                        m.identb[:], start=True, stop=True)
                    ins.then_inc(ring_full, 1)
                elif kind == "turn":
                    hf, back = step[1:]
                    pe.wait_ge(out_copied, at(2, hf + 1 + CRED_OUT - 2 * back))
                    for k in range(TB):
                        ins = pe.transpose(m.psum[:, bank, P * k:P * (k + 1)], m.outT[:, hf, P * k:P * (k + 1)], m.ident[:])
                    ins.then_inc(ring_full, 1)
                elif kind == "col":
                    u, p = step[1:]
                    hf, kt = units[u]
                    q0 = first_q(u)
                    if p == 0 and u in (0, last_of_half[0] + 1):
                        pe.wait_ge(max_loaded, at(2 * MAX_LOAD, MAX_LOAD * (hf + 1)))
                    pe.wait_ge(prob_full, at(2 * U, 2 * u + p + 1))
                    diagonal = causal and kt >= TB * hf
                    for jj in range(2):
                        out = m.psum[:, col_bank(u, p) + jj, q0 - BANK * hf:BANK]
                        ins = pe.matmul(out, m.ks[:, this_slot, 2 * p + jj, P * kt:P * (kt + 1)],
                                        m.qs[:, this_slot, 2 * p + jj, q0:BANK * (hf + 1)], start=True, stop=not diagonal)
                        if diagonal:
                            ins = pe.matmul(out[:, 0:P], m.identb[:], m.maskb[:, 1, :], start=False, stop=True)
                    ins.then_inc(col_full, 1)
                elif kind == "pv":
                    u, back = step[1:]
                    hf, kt = units[u]
                    off = first_q(u) - BANK * hf
                    begins = kt == halves[hf][-1]
                    if u == 0:
                        pe.wait_ge(v_staged, at(1, 1))
                    if begins:
                        pe.wait_ge(out_copied, at(2, hf + 1 - 2 * back))
                    pe.wait_ge(prob_full, at(2 * U, 2 * u + 2 + CRED_COL - 2 * U * back))
                    for j in range(G):
                        ins = pe.matmul(m.psum[32 * j:32 * j + VW, OUT, off:BANK],
                                        m.vst[:, (g - back) % SLOTS, kt, VW * j:VW * (j + 1)],
                                        m.prob[:, (2 * u + j // 2) % 4, j % 2, off:BANK],
                                        start=begins, stop=kt == 0, skip_group_check=True)
                    ins.then_inc(pv_done, 1)

        pe.wait_ge(hi_ready, 2 * NCH)
        pe.wait_ge(v_ready, NCH)
        pe.wait_ge(cleared, 2)
        program(pe, run)

    @block.scalar
    def _(act):
        load_table(act, m, ACT.Exp, 1)
        act.sem_inc(prob_full, CRED_COL)
        act.sem_inc(out_copied, CRED_OUT)

        def run(steps, g, i, count):
            at = of_group(g, i)
            for step in steps:
                if step[0] == "col":
                    u, p = step[1:]
                    off = first_q(u) - BANK * units[u][0]
                    if p == 0:
                        act.wait_ge(pv_done, at(U, u + 1))
                    act.wait_ge(col_full, at(2 * U, 2 * u + p + 1))
                    b = col_bank(u, p)
                    act.activation(m.prob[:, (2 * u + p) % 4, :, off:BANK], m.psum[:, b:b + 2, off:BANK],
                                   ACT.Exp).then_inc(prob_full, 1)
                elif step[0] == "pv" and step[1] in last_of_half:
                    u, back = step[1:]
                    hf = last_of_half.index(u)
                    act.wait_ge(pv_done, at(U, u + 1 + CRED_PV - U * back))
                    act.wait_ge(inverted, at(2, hf + 1 - 2 * back))
                    act.copy(m.outT[:, hf, :], m.psum[:, OUT, :]).then_inc(out_copied, 1)

        program(act, run)

    @block.vector
    def _(dve):
        dve.sem_inc(ring_free, CRED_RING)
        dve.sem_inc(pv_done, CRED_PV)
        dve.sem_inc(inverted, CRED_TURN)
        dve.memset(m.mx[:], -BIG).then_inc(cleared, 1)
        dve.memset(m.psum[:, OUT, :], 0.0).then_inc(cleared, 1)
        dve.wait_ge(cleared, 2)

        def run(steps, g, i, count):
            at, next_at, ring = of_group(g, i), of_group(g + 1, i), ring_at(steps, count, i)
            n = 0
            for step in steps:
                kind = step[0]
                if in_ring(step):
                    bank = (count + n) % RING
                    n += 1
                if kind == "row":
                    heads, qt, k0, keys = step[1]
                    scores = m.psum[:, bank, 0:len(heads) * keys].rearrange("p (j k) -> p j k", k=keys)
                    dve.wait_ge(ring_full, ring(n))
                    dve.reduce_max(m.mx[:, heads[0]:heads[0] + len(heads), qt, k0 // BANK], scores, AX_X)\
                        .then_inc(ring_free, 1)
                elif kind == "negate":
                    hf = step[1]
                    dve.wait_ge(ring_free, ring(n + CRED_RING))
                    if not (g == -1 and isinstance(i, int)):
                        dve.wait_ge(neg_split, next_at(2, hf - 1))
                    dve.tensor_reduce(m.negm[:, hf], m.mx[:, :, TB * hf:TB * (hf + 1), :].rearrange("p j t c -> p t j c"),
                                      AX_X, ALU.max, negate=True)\
                        .then_inc(neg_made, 1)
                elif kind == "turn_max":
                    hf, ahead = step[1:]
                    before = (next_at if ahead else at)(2 * MAX_LOAD, hf * MAX_LOAD)
                    dve.wait_ge(ring_full, ring(n))
                    if not (isinstance(before, int) and before == 0):
                        dve.wait_ge(max_loaded, before)
                    dve.tensor_copy(m.maxT[:], m.psum[0:3 * G, bank, :]).then_inc(ring_free, 1)
                elif kind == "turn":
                    hf, back = step[1:]
                    sums = m.psum[:, bank, :].rearrange("p (t j w) -> p t j w", t=TB, j=G)
                    dve.wait_ge(ring_full, ring(n))
                    inv = m.rsum[:, hf]
                    dve.reciprocal(inv, sums[:, :, :, HD]).then_inc(inverted, 1)
                    dve.wait_ge(inverted, at(2, hf + 1 + CRED_TURN - 2 * back))
                    group = i * SLOTS + (g - back)
                    out = m.ctx[:].rearrange("p t (g j w) -> p t g j w", g=HG, j=G)
                    out = out[:, bass.ds(group // HG * QT + hf * TB, TB), bass.ds(group % HG, 1), :, :]
                    out = out.rearrange("p t g j w -> p t (g j) w")
                    dve.tensor_tensor(out, sums[:, :, :, 0:HD], inv.unsqueeze(3).to_broadcast([P, TB, G, HD]),
                                      ALU.mult).then_inc(ring_free, 1)

        program(dve, run)

    all_steps = ring_len(first) + ring_len(body0) + (NG - 2) * ring_len(body) + ring_len(last) + ring_len(tail)
    return ring_free, all_steps + CRED_RING


def residual_stage(nc, m, a, base):
    based = stage_semaphores(nc, m, f"base{a}")("based")
    block = m.block

    @block.vector
    def _(dve):
        bias = m.abrow[:, a, 1, :].unsqueeze(1).to_broadcast([P, TB, D])
        for c in range(NCH):
            tiles = slice(TB * c, TB * (c + 1))
            dve.tensor_tensor(m.y[:, tiles, :], base[:, tiles, :], bias, ALU.add).then_inc(based, 1)

    return [(based, NCH)]


def out_project_stage(nc, m, a, attended, based):
    sem = stage_semaphores(nc, m, f"out{a}")
    turned, copied, projected, added = sem("turned"), sem("copied"), sem("projected"), sem("added")
    block = m.block
    ctxT = m.xT

    @block.tensor
    def _(pe):
        def project(c):
            pe.wait_ge(copied, c + 1)
            for k in range(TB):
                col = BANK * c + P * k
                ins = pe.matmul(m.psum[:, 4 + c, P * k:P * (k + 1)], ctxT[:, col:col + P], m.attn_w[:, a, 3, :],
                                start=True, stop=True)
            ins.then_inc(projected, 1)

        pe.wait_ge(*attended)
        for c in range(NCH):
            for k in range(TB):
                ins = pe.transpose(m.psum[:, c, P * k:P * (k + 1)], m.ctx[:, TB * c + k, :], m.ident[:])
            ins.then_inc(turned, 1)
            if c:
                project(c - 1)
        project(NCH - 1)

    @block.scalar
    def _(act):
        for c in range(NCH):
            act.wait_ge(turned, c + 1)
            act.copy(ctxT[:, BANK * c:BANK * (c + 1)], m.psum[:, c, :]).then_inc(copied, 1)

    @block.vector
    def _(dve):
        wait_all(dve, based)
        for c in range(NCH):
            y = m.y[:, TB * c:TB * (c + 1), :]
            dve.wait_ge(projected, c + 1)
            dve.tensor_tensor(y, m.psum[:, 4 + c, :].rearrange("p (t f) -> p t f", t=TB), y, ALU.add).then_inc(added, 1)

    return lambda c: [(added, c + 1)]


def ffn_bias_stage(nc, m, normed):
    biased = stage_semaphores(nc, m, "ffn")("biased")
    block = m.block

    @block.vector
    def _(dve):
        dve.memset(m.gate[:], 1.0).then_inc(biased, 1)
        wait_all(dve, normed(NCH - 1))
        for c in range(NCH):
            y = m.y[:, TB * c:TB * (c + 1), :]
            dve.tensor_tensor(y, y, m.b2ffn[:].unsqueeze(1).to_broadcast([P, TB, D]), ALU.add).then_inc(biased, 1)

    return biased, 1 + NCH


def top_two(dve, act, m, n, step, e2_ready):
    if act is not None:
        act.wait_ge(step, n + 1)
        act.activation(m.tmp[:, 0:n, 1], m.tmp[:, 0:n, 0], ACT.Exp).then_inc(e2_ready, 1)
        return
    for t in range(n):
        dve.max(m.top[:, t, :], m.lg[:, t, :]).then_inc(step, 1)
    dve.wait_ge(step, n)
    dve.tensor_tensor(m.tmp[:, 0:n, 0], m.top[:, 0:n, 1], m.top[:, 0:n, 0], ALU.subtract).then_inc(step, 1)
    for t in range(n):
        dve.max_index(m.idx[:, t, :], m.top[:, t, :], m.lg[:, t, :]).then_inc(step, 1)
    dve.wait_ge(step, 2 * n + 1)
    dve.tensor_copy(m.idxf[:, 0:n, :], m.idx[:, 0:n, :]).then_inc(step, 1)
    dve.wait_ge(e2_ready, 1)
    dve.tensor_scalar(m.tmp[:, 0:n, 2], m.tmp[:, 0:n, 1], 1.0, None, ALU.add).then_inc(step, 1)
    dve.wait_ge(step, 2 * n + 3)
    dve.reciprocal(m.sel[:, 0:n, 0], m.tmp[:, 0:n, 2]).then_inc(step, 1)
    dve.wait_ge(step, 2 * n + 4)
    dve.tensor_tensor(m.sel[:, 0:n, 1], m.sel[:, 0:n, 0], m.tmp[:, 0:n, 1], ALU.mult).then_inc(step, 1)
    dve.wait_ge(step, 2 * n + 5)
    iota = m.iota8[:].unsqueeze(1).to_broadcast([P, n, E])
    for k, out in ((0, m.gate), (1, m.pick)):
        out = out[:, 0:n, :]
        dve.tensor_tensor(out, iota, m.idxf[:, 0:n, k:k + 1].to_broadcast([P, n, E]), ALU.is_equal).then_inc(step, 1)
        dve.wait_ge(step, 2 * n + 6 + 2 * k)
        dve.tensor_tensor(out, out, m.sel[:, 0:n, k:k + 1].to_broadcast([P, n, E]), ALU.mult).then_inc(step, 1)
        dve.wait_ge(step, 2 * n + 7 + 2 * k)
    dve.tensor_tensor(m.gate[:, 0:n, :], m.gate[:, 0:n, :], m.pick[:, 0:n, :], ALU.add).then_inc(step, 1)
    dve.wait_ge(step, 2 * n + 10)


def gates_stage(nc, m, layer, by_sequence, ready):
    sem = stage_semaphores(nc, m, f"gates{layer}")
    meaned, logits_mm, lg_ready, step, e2_ready = sem("meaned"), sem("logits_mm"), sem("lg_ready"), sem("step"), sem("e2_ready")
    gates_ready = sem("gates_ready")
    block = m.block
    n = NB if by_sequence else T
    LG = 6
    lg_psum = m.psum[:, LG, 0:n * E].rearrange("p (t e) -> p t e", e=E)

    @block.tensor
    def _(pe):
        if by_sequence:
            pe.wait_ge(meaned, 2)
        for t in range(n):
            if not by_sequence and t % TB == 0:
                wait_all(pe, ready(t // TB))
            lhs = m.mrep[:, t, :] if by_sequence else m.xT[:, P * t:P * (t + 1)]
            ins = pe.matmul(m.psum[:, LG, E * t:E * (t + 1)], lhs, m.gate_w[:, layer, :], start=True, stop=True)
        ins.then_inc(logits_mm, 1)

    @block.scalar
    def _(act):
        load_table(act, m, ACT.Exp, 2)
        top_two(None, act, m, n, step, e2_ready)

    @block.vector
    def _(dve):
        if by_sequence:
            wait_all(dve, ready(NCH - 1))
            dve.reduce_sum(m.msum[:], m.xT[:].rearrange("p (b s) -> p b s", b=NB), AX_X).then_inc(meaned, 1)
            dve.wait_ge(meaned, 1)
            dve.tensor_scalar(m.mrep[:], m.msum[:].unsqueeze(2).to_broadcast([P, NB, P]), 1.0 / S, None, ALU.mult)\
                .then_inc(meaned, 1)
        dve.wait_ge(logits_mm, 1)
        dve.tensor_tensor(m.lg[:, 0:n, :], lg_psum, m.gate_b[:, layer, :].unsqueeze(1).to_broadcast([P, n, E]),
                          ALU.add).then_inc(lg_ready, 1)
        dve.wait_ge(lg_ready, 1)
        top_two(dve, None, m, n, step, e2_ready)
        if by_sequence:
            dve.tensor_copy(m.pick[:, 0:NB, :], m.gate[:, 0:NB, :]).then_inc(lg_ready, 1)
            dve.wait_ge(lg_ready, 2)
            for b in range(NB):
                dve.tensor_copy(m.gate[:, b * QT:(b + 1) * QT, :], m.pick[:, b:b + 1, :].to_broadcast([P, QT, E]))\
                    .then_inc(gates_ready, 1)
        else:
            dve.sem_inc(gates_ready, NB)

    return gates_ready, NB


def gated_bias_stage(nc, m, layer, gated, ready):
    sem = stage_semaphores(nc, m, f"bias{layer}")
    turned, copied, biased_mm, biased = sem("turned"), sem("copied"), sem("biased_mm"), sem("biased")
    block = m.block
    bank = lambda c: 4 + c

    @block.tensor
    def _(pe):
        pe.wait_ge(*gated)
        pe.wait_ge(*ready)
        for t in range(T):
            ins = pe.transpose(m.psum[0:E, t // TB, P * (t % TB):P * (t % TB + 1)], m.gate[:, t, :], m.ident[:])
            if t % TB == TB - 1:
                ins.then_inc(turned, 1)
        for c in range(NCH):
            pe.wait_ge(copied, c + 1)
            for k in range(TB):
                ins = pe.matmul(m.psum[:, bank(c), P * k:P * (k + 1)], m.gT[:, TB * c + k, :], m.b2[:, layer, :],
                                start=True, stop=True)
            ins.then_inc(biased_mm, 1)

    @block.scalar
    def _(act):
        for c in range(NCH):
            act.wait_ge(turned, c + 1)
            act.copy(m.gT[:, TB * c:TB * (c + 1), :], m.psum[0:E, c, :].rearrange("e (t p) -> e t p", t=TB))\
                .then_inc(copied, 1)

    @block.vector
    def _(dve):
        dve.wait_ge(*ready)
        for c in range(NCH):
            dve.wait_ge(biased_mm, c + 1)
            y = m.y[:, TB * c:TB * (c + 1), :]
            dve.tensor_tensor(y, m.psum[:, bank(c), :].rearrange("p (t f) -> p t f", t=TB), y, ALU.add).then_inc(biased, 1)

    return lambda c: [(biased, c + 1)]


def cut_x_stage(nc, m, tag, ready):
    sem = stage_semaphores(nc, m, tag)
    first_cut, x_cut = sem("first_cut"), sem("x_cut")
    block = m.block
    chunk = lambda b, c: b[:, BANK * c:BANK * (c + 1)]

    @block.vector
    def _(dve):
        for c in range(NCH):
            wait_all(dve, ready(c))
            dve.tensor_copy(chunk(m.x_part[0], c), chunk(m.xT, c)).then_inc(first_cut, 1)
            dve.wait_ge(first_cut, c + 1)
            dve.tensor_tensor(chunk(m.x_part[1], c), chunk(m.xT, c), chunk(m.x_part[0], c), ALU.subtract).then_inc(x_cut, 1)

    return lambda c: [(x_cut, c + 1)]


def cut_weights(pool, m, slot, w1, w_cut, before):
    first, rest = m.w_part[:, slot, 0, :], m.w_part[:, slot, 1, :]
    pool.tensor_tensor(first, w1, m.zero[:].to_broadcast([P, F]), ALU.subtract).then_inc(w_cut, 1)
    pool.wait_ge(w_cut, before + 1)
    pool.tensor_tensor(rest, w1, first, ALU.subtract).then_inc(w_cut, 1)


def up_product(pe, m, out, slot, k, tokens):
    for n, (w, x) in enumerate(((0, 0), (0, 1), (1, 0))):
        ins = pe.matmul(out, m.w_part[:, slot, w, P * k:P * (k + 1)], m.x_part[x][:, tokens], start=n == 0, stop=n == 2)
    return ins


def experts_stage(nc, m, tag, experts, first, mode, ready, gated, turned):
    sem = stage_semaphores(nc, m, f"{tag}")
    w_loaded = [sem("w_loaded0"), sem("w_loaded1")]
    up_mm, gelu_done, down_mm, added = sem("up_mm"), sem("gelu_done"), sem("down_mm"), sem("added")
    w_cut = sem("w_cut")
    block = m.block
    chosen = mode == "chosen"
    passes = 2 if experts > 1 else 1
    loops = experts // passes
    C = NCH // NB if chosen else NCH
    UB = passes * C
    tok_step = S if chosen else 0
    CRED_UP, CRED_H, CRED_ACC = FC, 2, 2
    b1 = lambda p, k: m.wring[:, p, F + k:F + k + 1]
    w2 = lambda p, k: m.wring[:, p, F + FC + D * k:F + FC + D * (k + 1)]

    def looped(eng, body):
        if loops == 1:
            body(0)
        else:
            with eng.Fori(0, loops) as i:
                body(i)

    @block.sync
    def _(sp):
        experts_w = m.experts_w
        if loops == 1:
            sp.dma_start(m.wring[:, 0, :], experts_w[first]).then_inc(w_loaded[0], 16)
        else:
            if chosen:
                sp.wait_ge(*gated)
            for p in range(passes):
                which = (sp.value_load(m.idx[0:1, 0:1, p:p + 1], min_val=0, max_val=E - 1) + first) if chosen else p + first
                sp.dma_start(m.wring[:, p:p + 1, :], experts_w[bass.ds(which, 1)].rearrange("e p w -> p e w"))\
                    .then_inc(w_loaded[p], 16)
            with sp.Fori(1, loops) as i:
                for p in range(passes):
                    if chosen:
                        which = sp.value_load(m.idx[0:1, bass.ds(i, 1), p:p + 1], min_val=0, max_val=E - 1) + first
                    else:
                        which = i * passes + (p + first)
                    sp.wait_ge(down_mm, i * UB + (CRED_H - (passes - 1 - p) * C))
                    sp.dma_start(m.wring[:, p:p + 1, :], experts_w[bass.ds(which, 1)].rearrange("e p w -> p e w"))\
                        .then_inc(w_loaded[p], 16)

    @block.gpsimd
    def _(pool):
        def body(i):
            for p in range(passes):
                pool.wait_ge(w_loaded[p], i * 16 + 16)
                cut_weights(pool, m, p, m.wring[:, p, 0:F], w_cut, i * (2 * passes) + 2 * p)
        looped(pool, body)

    @block.tensor
    def _(pe):
        wait_all(pe, turned(NCH - 1))

        def body(i):
            for p in range(passes):
                pe.wait_ge(w_loaded[p], i * 16 + 16)
                pe.wait_ge(w_cut, i * (2 * passes) + (2 * p + 2))
                for c in range(C):
                    u = p * C + c
                    wait_all(pe, ready(NCH - 1 if chosen else c))
                    for k in range(FC):
                        pe.wait_ge(gelu_done, i * (UB * FC) + (u * FC + k + 1))
                        up_product(pe, m, m.psum[:, k, :], p, k, bass.ds(i * tok_step + BANK * c, BANK)).then_inc(up_mm, 1)
                    pe.wait_ge(added, i * UB + (u + 1))
                    for k in range(FC):
                        pe.wait_ge(gelu_done, i * (UB * FC) + (u * FC + k + 1 + CRED_UP))
                        for t in range(TB):
                            ins = pe.matmul(m.psum[:, 4 + u % 2, P * t:P * (t + 1)], m.h[:, u % 2, k, P * t:P * (t + 1)],
                                            w2(p, k), start=(k == 0 and t == 0), stop=k == FC - 1,
                                            skip_group_check=True)
                    ins.then_inc(down_mm, 1)
        looped(pe, body)

    @block.scalar
    def _(act):
        act.sem_inc(gelu_done, CRED_UP)
        load_table(act, m, ACT.Gelu, 3)

        def body(i):
            for p in range(passes):
                act.wait_ge(w_loaded[p], i * 16 + 16)
                for c in range(C):
                    u = p * C + c
                    act.wait_ge(down_mm, i * UB + (u + 1))
                    for k in range(FC):
                        act.wait_ge(up_mm, i * (UB * FC) + (u * FC + k + 1))
                        act.activation(m.h[:, u % 2, k, :], m.psum[:, k, :], ACT.Gelu, bias=b1(p, k))\
                            .then_inc(gelu_done, 1)
        looped(act, body)

    @block.vector
    def _(dve):
        dve.sem_inc(down_mm, CRED_H)
        dve.sem_inc(added, CRED_ACC)
        dve.wait_ge(*gated)

        def body(i):
            for p in range(passes):
                for c in range(C):
                    u = p * C + c
                    dve.wait_ge(down_mm, i * UB + (u + 1 + CRED_H))
                    dve.wait_ge(added, i * UB + (u + CRED_ACC))
                    for t in range(TB):
                        tile = TB * c + t
                        y = m.y[:].rearrange("p t f -> p (t f)")[:, bass.ds(i * (tok_step // P * D) + tile * D, D)]
                        if chosen:
                            gate = m.sel[:].rearrange("p t k -> p (t k)")[:, bass.ds(i * 2 + p, 1)]
                        else:
                            gate = m.gate[:].rearrange("p t e -> p (t e)")[:, bass.ds(i * passes + (tile * E + p), 1)]
                        ins = dve.scalar_tensor_tensor(out=y, in0=m.psum[:, 4 + u % 2, P * t:P * (t + 1)], scalar=gate,
                                                       in1=y, op0=ALU.mult, op1=ALU.add)
                    ins.then_inc(added, 1)
        looped(dve, body)

    return added, loops * UB + CRED_ACC


def tail_stage(nc, m, ready, cut):
    sem = stage_semaphores(nc, m, f"tail")
    cstep, csqrt, ct_mm, route_ready, score_mm = sem("cstep"), sem("csqrt"), sem("ct_mm"), sem("route_ready"), sem("score_mm")
    squared, xsqrt, lg_step, exp_ready = sem("squared"), sem("xsqrt"), sem("lg_step"), sem("exp_ready")
    turned, gt_ready, up_mm, gelu_done = sem("turned"), sem("gt_ready"), sem("up_mm"), sem("gelu_done")
    wide_mm, gated, down_mm, added = sem("wide_mm"), sem("gated"), sem("down_mm"), sem("added")
    block = m.block
    w_cut = sem("w_cut")
    b1 = lambda k: m.tail_w[:, F + k:F + k + 1]
    w2 = lambda k: m.tail_w[:, F + FC + D * k:F + FC + D * (k + 1)]
    N_SQ = 16

    @block.gpsimd
    def _(pool):
        cut_weights(pool, m, 0, m.tail_w[:, 0:F], w_cut, 0)

    @block.tensor
    def _(pe):
        wait_all(pe, ready(NCH - 1))
        pe.wait_ge(cstep, 5)
        pe.transpose(m.psum[:, 0, 0:E], m.cscr[:], m.ident[0:E, 0:E]).then_inc(ct_mm, 1)
        pe.wait_ge(route_ready, 1)
        for t in range(T):
            ins = pe.matmul(m.psum[:, 1, 2 * E * t:2 * E * (t + 1)], m.xT[:, P * t:P * (t + 1)], m.route[:],
                            start=True, stop=True)
        ins.then_inc(score_mm, 1)
        pe.wait_ge(lg_step, T + 7)
        for t in range(T):
            ins = pe.transpose(m.psum[0:E, 2 + t // TB, P * (t % TB):P * (t % TB + 1)], m.gate[:, t, :], m.ident[:])
            if t % TB == TB - 1:
                ins.then_inc(turned, 1)
        pe.wait_ge(w_cut, 2)
        for c in range(NCH):
            wait_all(pe, cut(c))
            pe.wait_ge(gt_ready, NCH)
            for k in range(FC):
                n = c * FC + k
                if n >= 2:
                    pe.wait_ge(gelu_done, n - 1)
                up_product(pe, m, m.psum[:, n % 2, :], 0, k, slice(BANK * c, BANK * (c + 1))).then_inc(up_mm, 1)
                if n >= 2:
                    pe.wait_ge(gated, n - 1)
                pe.matmul(m.psum[:, 2 + n % 2, :], m.expand[:, P * k:P * (k + 1)],
                          m.gT[:, TB * c:TB * (c + 1), :].rearrange("e t p -> e (t p)"), start=True, stop=True)\
                    .then_inc(wide_mm, 1)
            if c >= 2:
                pe.wait_ge(added, c - 1)
            for k in range(FC):
                pe.wait_ge(gated, c * FC + k + 1)
                for t in range(TB):
                    pe.matmul(m.psum[:, 6 + c % 2, P * t:P * (t + 1)], m.h[:, c % 2, k, P * t:P * (t + 1)], w2(k),
                              start=(k == 0 and t == 0), stop=False, skip_group_check=True)
            for t in range(TB):
                ins = pe.matmul(m.psum[:, 6 + c % 2, P * t:P * (t + 1)], m.gT[:, TB * c + t, :], m.b2[:, 2, :],
                                start=False, stop=True, skip_group_check=True)
            ins.then_inc(down_mm, 1)

    @block.scalar
    def _(act):
        act.wait_ge(cstep, 1)
        act.activation(m.cn[:, 1:2], m.cn[:, 0:1], ACT.Sqrt).then_inc(csqrt, 1)
        act.wait_ge(squared, 1 + T)
        act.activation(m.std[:], m.tmp[:, :, 0], ACT.Sqrt).then_inc(xsqrt, 1)
        act.wait_ge(lg_step, T + 3)
        act.activation(m.pick[:], m.lg[:], ACT.Exp).then_inc(exp_ready, 1)
        for c in range(NCH):
            act.wait_ge(turned, c + 1)
            act.copy(m.gT[:, TB * c:TB * (c + 1), :], m.psum[0:E, 2 + c, :].rearrange("e (t p) -> e t p", t=TB))\
                .then_inc(gt_ready, 1)
        for c in range(NCH):
            if c >= 2:
                act.wait_ge(down_mm, c - 1)
            for k in range(FC):
                n = c * FC + k
                act.wait_ge(up_mm, n + 1)
                act.activation(m.h[:, c % 2, k, :], m.psum[:, n % 2, :], ACT.Gelu, bias=b1(k)).then_inc(gelu_done, 1)

    @block.vector
    def _(dve):
        dve.memset(m.cn[:], 0.0).then_inc(squared, 1)
        dve.wait_ge(squared, 1)
        dve.tensor_tensor_reduce(out=m.cscr[:], in0=m.cent[:], in1=m.cent[:], scale=1.0, scalar=0.0, op0=ALU.mult,
                                 op1=ALU.add, accum_out=m.cn[:, 0:1]).then_inc(cstep, 1)
        dve.wait_ge(csqrt, 1)
        dve.tensor_scalar(m.cn[:, 2:3], m.cn[:, 1:2], 1e-12, None, ALU.max).then_inc(cstep, 1)
        dve.wait_ge(cstep, 2)
        dve.reciprocal(m.cn[:, 3:4], m.cn[:, 2:3]).then_inc(cstep, 1)
        dve.wait_ge(cstep, 3)
        dve.tensor_scalar(m.cscr[:], m.cent[:], m.cn[:, 3:4], None, ALU.mult).then_inc(cstep, 2)
        dve.wait_ge(ct_mm, 1)
        dve.tensor_copy(m.route[:, 0:E], m.psum[:, 0, 0:E]).then_inc(route_ready, 1)
        for t in range(T):
            dve.tensor_tensor_reduce(out=m.nrm[:, t, :], in0=m.x[:, t, :], in1=m.x[:, t, :], scale=1.0, scalar=0.0,
                                     op0=ALU.mult, op1=ALU.add, accum_out=m.tmp[:, t, 0:1]).then_inc(squared, 1)
        dve.wait_ge(xsqrt, 1)
        dve.tensor_scalar(m.std[:], m.std[:], 1e-12, None, ALU.max).then_inc(xsqrt, 1)
        dve.wait_ge(xsqrt, 2)
        dve.reciprocal(m.rstd[:], m.std[:]).then_inc(xsqrt, 1)
        dve.wait_ge(score_mm, 1)
        dve.wait_ge(xsqrt, 3)
        scores = m.psum[:, 1, 0:2 * E * T].rearrange("p (t k e) -> p t k e", t=T, k=2)
        wide = lambda x: x.to_broadcast([P, T, E])
        dve.tensor_tensor(m.lg[:], scores[:, :, 0, :], wide(m.rstd[:].unsqueeze(2)), ALU.mult).then_inc(lg_step, 1)
        dve.wait_ge(lg_step, 1)
        dve.tensor_tensor(m.lg[:], scores[:, :, 1, :], m.lg[:], ALU.add).then_inc(lg_step, 1)
        dve.wait_ge(lg_step, 2)
        for t in range(T):
            dve.max(m.top[:, t, :], m.lg[:, t, :]).then_inc(lg_step, 1)
        dve.wait_ge(lg_step, T + 2)
        dve.tensor_tensor(m.gate[:], m.lg[:], wide(m.top[:, :, 1:2]), ALU.is_ge).then_inc(exp_ready, 1)
        dve.tensor_tensor(m.lg[:], m.lg[:], wide(m.top[:, :, 0:1]), ALU.subtract).then_inc(lg_step, 1)
        dve.wait_ge(exp_ready, 2)
        dve.tensor_tensor(m.gate[:], m.gate[:], m.pick[:], ALU.mult).then_inc(lg_step, 1)
        dve.wait_ge(lg_step, T + 4)
        dve.tensor_reduce(m.tmp[:, :, 1], m.gate[:], AX_X, ALU.add).then_inc(lg_step, 1)
        dve.wait_ge(lg_step, T + 5)
        dve.reciprocal(m.tmp[:, :, 2], m.tmp[:, :, 1]).then_inc(lg_step, 1)
        dve.wait_ge(lg_step, T + 6)
        dve.tensor_tensor(m.gate[:], m.gate[:], wide(m.tmp[:, :, 2:3]), ALU.mult).then_inc(lg_step, 1)

        def add_out(c):
            dve.wait_ge(down_mm, c + 1)
            dve.tensor_tensor(m.y[:, TB * c:TB * (c + 1), :], m.psum[:, 6 + c % 2, :].rearrange("p (t f) -> p t f", t=TB),
                              m.x[:, TB * c:TB * (c + 1), :], ALU.add).then_inc(added, 1)

        for c in range(NCH):
            for k in range(FC):
                n = c * FC + k
                dve.wait_ge(gelu_done, n + 1)
                dve.wait_ge(wide_mm, n + 1)
                dve.tensor_tensor(m.h[:, c % 2, k, :], m.psum[:, 2 + n % 2, :], m.h[:, c % 2, k, :], ALU.mult)\
                    .then_inc(gated, 1)
            if c:
                add_out(c - 1)
        add_out(NCH - 1)

    return lambda c: [(added, c + 1)]


def store_stage(nc, m, out, ready):
    stored = stage_semaphores(nc, m, "out")("stored")
    block = m.block

    @block.sync
    def _(sp):
        rows = out.rearrange("(t p) f -> p t f", p=P)
        for c in range(NCH):
            wait_all(sp, ready(c))
            sp.dma_start(rows[:, TB * c:TB * (c + 1), :], m.x[:, TB * c:TB * (c + 1), :]).then_inc(stored, 16)
        sp.wait_ge(stored, 16 * NCH)


def build_program(nc, ins, out):
    RETIRED.clear()
    with ExitStack() as ctx:
        m = allocate(nc, ctx)
        nc.disable_value_cache = True
        m.experts_w = ins["experts_w"]

        def attention(a, causal, base, normed, rows=None):
            projected = project_stage(nc, m, a, normed)
            based = residual_stage(nc, m, a, base)
            attended = attention_stage(nc, m, a, causal, rows, projected)
            return out_project_stage(nc, m, a, attended, based)

        with region(nc, m):
            loaded = load_stage(nc, m, ins)
            normed = norm_stage(nc, m, "n0", m.x, turned=True, ln=0, ready=loaded)
            added = attention(0, False, m.x, normed)
            normed = norm_stage(nc, m, "n1", m.y, turned=True, ln=1, ready=added)
            cut = cut_x_stage(nc, m, "cut_ffn", normed)
            biased = ffn_bias_stage(nc, m, normed)
            added = experts_stage(nc, m, "ffn", 1, 0, "all", cut, biased, normed)
            normed = norm_stage(nc, m, "n2", m.x, add=m.y, plain_out=m.x, ready=lambda c: [added])
        for layer in range(2):
            with region(nc, m):
                base = m.x if layer == 0 else m.y
                normed = norm_stage(nc, m, f"l{layer}a", base, turned=True, ln=2 + 2 * layer)
                added = attention(1 + layer, True, base, normed)
                normed = norm_stage(nc, m, f"l{layer}b", m.y, turned=True, ln=3 + 2 * layer, ready=added)
                cut = cut_x_stage(nc, m, f"cut{layer}", normed)
                gated = gates_stage(nc, m, layer, layer == 1, normed)
                if layer == 0:
                    added = experts_stage(nc, m, "moe0", E, 1, "all", cut, gated, normed)
                else:
                    added = experts_stage(nc, m, "moe1", 2 * NB, 1 + E, "chosen", cut, gated, normed)
                biased = gated_bias_stage(nc, m, layer, gated, added)
                if layer == 1:
                    normed = norm_stage(nc, m, "n3", m.x, add=m.y, plain_out=m.x, turned=True, ln=None, ready=biased)
        with region(nc, m):
            added = attention(3, True, m.x, None, ins["position"].bitcast(BF16))
            normed = norm_stage(nc, m, "n4", m.y, plain_out=m.x, turned=True, ln=None, ready=added)
            cut = cut_x_stage(nc, m, "cut_tail", normed)
            added = tail_stage(nc, m, normed, cut)
            normed = norm_stage(nc, m, "n5", m.y, plain_out=m.x, ready=added)
            store_stage(nc, m, out, normed)



def _layout(x):
    import numpy as np

    a = {k: np.asarray(v) for k, v in x.items()}
    f32 = np.float32

    def heads_last(w):
        return w.reshape(*w.shape[:-1], HG, G, HD).swapaxes(-1, -2).reshape(w.shape)

    def attn(q, k, v, o):
        return np.stack([heads_last(q), heads_last(k), v, o], axis=1)

    w0 = a["L0_attn_in_proj_w"].T
    w3 = a["L1_attn_w_in"].T
    attn_w = [attn(w0[:, 0:D], w0[:, D:2 * D], w0[:, 2 * D:], a["L0_attn_out_w"].T)]
    attn_w += [attn(a["L0_ffn_wq"][l], a["L0_ffn_wk"][l], a["L0_ffn_wv"][l], a["L0_ffn_wo"][l]) for l in range(2)]
    attn_w += [attn(w3[:, 0:D], w3[:, D:2 * D], w3[:, 2 * D:], a["L1_attn_w_out"].T)]
    b0 = a["L0_attn_in_proj_b"]
    zero = np.zeros(D, f32)
    q_b = [b0[0:D], a["L0_ffn_bq"][0], a["L0_ffn_bq"][1], zero]
    k_b = [b0[D:2 * D], a["L0_ffn_bk"][0], a["L0_ffn_bk"][1], zero]
    v_b = [b0[2 * D:], a["L0_ffn_bv"][0], a["L0_ffn_bv"][1], zero]
    o_b = [a["L0_attn_out_b"], a["L0_ffn_bo"][0], a["L0_ffn_bo"][1], zero]
    abcol = np.stack([np.stack([heads_last(q_b[i]), heads_last(k_b[i])], axis=-1) for i in range(4)], axis=1)
    abrow = np.stack([np.stack([v_b[i], o_b[i]]) for i in range(4)])
    lncol = [(a["L0_attn_norm1_w"], a["L0_attn_norm1_b"]), (a["L0_attn_norm2_w"], a["L0_attn_norm2_b"])]
    for l in range(2):
        lncol += [(a["L0_ffn_ln1_w"][l], a["L0_ffn_ln1_b"][l]), (a["L0_ffn_ln2_w"][l], a["L0_ffn_ln2_b"][l])]
    lncol = np.stack([np.stack(p, axis=-1) for p in lncol], axis=1)

    def expert(w1, b1, w2):
        return np.concatenate([w1, b1.reshape(FC, P).T, w2.reshape(FC, P, D).transpose(1, 0, 2).reshape(P, FC * D)], axis=1)

    experts = [expert(a["L0_attn_lin1_w"].T, a["L0_attn_lin1_b"], a["L0_attn_lin2_w"].T)]
    experts += [expert(a["L0_ffn_e_w1"][l, e], a["L0_ffn_e_b1"][l, e], a["L0_ffn_e_w2"][l, e]) for l in range(2) for e in range(E)]
    tail_w = expert(a["L1_ffn_w1"].transpose(1, 0, 2).reshape(D, F), a["L1_ffn_b1"].reshape(F), a["L1_ffn_w2"].reshape(F, D))
    b2 = np.stack([a["L0_ffn_e_b2"][0], a["L0_ffn_e_b2"][1], a["L1_ffn_b2"]], axis=1)

    def bits16(v):
        return ((np.asarray(v, f32).view(np.uint32).astype(np.uint64) + 0x8000) >> 16).astype(np.uint16)

    q, k = np.arange(P)[:, None], np.arange(P)[None, :]
    mask = np.stack([np.where(k > q, -BIG / 3, 0.0), np.where(k < q, -BIG / 3, 0.0)], axis=1).astype(f32)
    slope = (2.0 ** (-8.0 / H * (np.arange(H) + 1.0))).astype(f32).astype(np.float64)
    rest = slope[:, None] * (np.arange(S) - S // 2)[None, :]
    position = []
    for _ in range(3):
        position.append(bits16(rest))
        rest = rest - (position[-1].astype(np.uint32) << 16).view(f32)
    expand = (np.arange(F)[None, :] // (F // E) == np.arange(E)[:, None]).astype(f32)
    arrays = {
        "x": a["L0_attn_x"].reshape(TOK, D), "attn_w": np.stack(attn_w, axis=1), "abcol": abcol, "abrow": abrow, "lncol": lncol,
        "experts_w": np.stack(experts), "tail_w": tail_w, "b2": b2, "b2ffn": a["L0_attn_lin2_b"],
        "gate_w": a["L0_ffn_gate_w"].transpose(1, 0, 2), "gate_b": a["L0_ffn_gate_b"],
        "centroids": a["L1_ffn_centroids"], "route_w": a["L1_ffn_w_route"].T,
        "ident": np.eye(P, dtype=f32), "identb": bits16(np.eye(P)), "maskb": bits16(mask), "iota8": np.arange(E, dtype=f32),
        "zeros_ones": bits16(np.repeat([[0.0], [1.0]], 3 * G * S, axis=1)),
        "position": np.stack(position), "expand": expand,
    }
    return {n: np.ascontiguousarray(v) for n, v in arrays.items()}


def kernel(**inputs):
    import concourse.bacc as _bacc
    from concourse.bass_utils import run_bass_kernel_spmd as _run

    nc = _bacc.Bacc("TRN2", target_bir_lowering=False, num_devices=1)
    arrays = {f"in_{n}": v for n, v in _layout(inputs).items()}
    ins = {n[3:]: nc.dram_tensor(n, v.shape, mybir.dt.from_np(v.dtype), kind="ExternalInput").ap() for n, v in arrays.items()}
    out = nc.dram_tensor("out_0", (TOK, D), F32, kind="ExternalOutput").ap()
    build_program(nc, ins, out)
    r = _run(nc, [arrays], core_ids=[0])
    return r.results[0]["out_0"].reshape(NB, S, D)
```
